# Optimizing a Trainium2 kernel written in Bass

```python
import numpy as np
import jax
import jax.numpy as jnp

def _softmax(x, axis=-1):
    return jax.nn.softmax(x, axis=axis)

def _gelu(x):
    return jax.nn.gelu(x, approximate=True)

def _silu(x):
    return jax.nn.silu(x)

def _sigmoid(x):
    return jax.nn.sigmoid(x)

def _layernorm(x, axis=-1, eps=1e-05):
    m = jnp.mean(x, axis=axis, keepdims=True)
    v = jnp.var(x, axis=axis, keepdims=True)
    return (x - m) / jnp.sqrt(v + eps)

def _scatter_add(tgt, idx, src, axis=0):
    return tgt.at[idx].add(src)

def _segment_sum(src, seg, n):
    return jax.ops.segment_sum(src, seg, n)
kernel_name = 'mk_adj_preln_d2_adj_r2_d7460c'

def setup_inputs(seed: int=0):
    np.random.seed(seed)
    _w = jnp.asarray

    def _rec_inputs():
        import jax
        import jax.numpy as jnp
        _gk = jax.random.key(seed)
        x = -0.0001538 + 1 * jax.random.normal(jax.random.fold_in(_gk, 1), (64, 128, 384), jnp.float32)
        _a = jax.random.bernoulli(jax.random.fold_in(_gk, 2), 0.125, (64, 128, 128))
        _af = _a.astype(jnp.float32)
        adj = _af
        return (x, adj)
    x, adj = _rec_inputs()

    def _L0_gnn_setup():
        import jax, jax.numpy as jnp
        import numpy as np
        LN_EPS = 1e-12

        def _digcn_forward(hidden_state, adjacency_matrix, Wl, bl, Ws, bs, Wr, br, ln_w, ln_b):
            B, S, D = hidden_state.shape
            temper = jnp.asarray(D, jnp.float32) ** 0.5
            i = jnp.arange(S)
            upper = (i[None, :] > i[:, None]).astype(hidden_state.dtype)
            lower = (i[None, :] < i[:, None]).astype(hidden_state.dtype)

            def layer(h, params):
                wl, b_l, ws, b_s, wr, b_r, g, beta = params
                u = jnp.einsum('bid,bjd->bij', h, h) / temper
                a = jax.nn.softmax(u, axis=-1)
                delta = a * adjacency_matrix
                attn = delta / (jnp.sum(delta, axis=-1, keepdims=True) + 1e-10)
                hl = h @ wl.T + b_l
                hs = h @ ws.T + b_s
                hr = h @ wr.T + b_r
                diag_a = jnp.diagonal(attn, axis1=1, axis2=2)
                ctx = jnp.einsum('bij,bjd->bid', attn * upper, hl) + diag_a[..., None] * hs + jnp.einsum('bij,bjd->bid', attn * lower, hr)
                mean = ctx.mean(-1, keepdims=True)
                var = ctx.var(-1, keepdims=True)
                o = (ctx - mean) / jnp.sqrt(var + LN_EPS) * g + beta
                return (jax.nn.relu(o), None)
            out, _ = jax.lax.scan(layer, hidden_state, (Wl, bl, Ws, bs, Wr, br, ln_w, ln_b))
            return out
        key = jax.random.key(seed)
        ks = jax.random.split(key, 6)
        B, S, D, L = (8, 512, 384, 2)
        scale = (1.0 / D) ** 0.5
        hidden_state = jax.random.normal(ks[0], (B, S, D), jnp.float32)
        adjacency_matrix = (jax.random.uniform(ks[1], (B, S, S)) < 0.05).astype(jnp.float32)
        Wl = jax.random.normal(ks[2], (L, D, D), jnp.float32) * scale
        Ws = jax.random.normal(ks[3], (L, D, D), jnp.float32) * scale
        Wr = jax.random.normal(ks[4], (L, D, D), jnp.float32) * scale
        bl = jnp.zeros((L, D), jnp.float32)
        bs = jnp.zeros((L, D), jnp.float32)
        br = jnp.zeros((L, D), jnp.float32)
        ln_w = jnp.ones((L, D), jnp.float32)
        ln_b = jnp.zeros((L, D), jnp.float32)
        return dict(hidden_state=hidden_state, adjacency_matrix=adjacency_matrix, Wl=Wl, bl=bl, Ws=Ws, bs=bs, Wr=Wr, br=br, ln_w=ln_w, ln_b=ln_b)
    _L0_gnn_all = _L0_gnn_setup()
    _L0_gnn_in = {k: v for k, v in _L0_gnn_all.items() if k in ('Wl', 'bl', 'Ws', 'bs', 'Wr', 'br', 'ln_w', 'ln_b')}
    del _L0_gnn_all

    def _L1_gnn_setup():
        import jax, jax.numpy as jnp
        import numpy as np
        B, S, H, L = (32, 256, 384, 2)

        def _layer_norm(z, a, b, eps=0.001):
            mu = jnp.mean(z, axis=-1, keepdims=True)
            sigma = jnp.std(z, axis=-1, keepdims=True, ddof=1)
            return (z - mu) / (sigma + eps) * a + b
        key = jax.random.key(seed)
        ks = jax.random.split(key, 6)
        hidden_state = jax.random.normal(ks[0], (B, S, H), dtype=jnp.float32)
        adjacency_matrix = (jax.random.uniform(ks[1], (B, S, S)) < 0.2).astype(jnp.float32)
        W_left = 0.05 * jax.random.normal(ks[2], (L, H, H), dtype=jnp.float32)
        W_right = 0.05 * jax.random.normal(ks[3], (L, H, H), dtype=jnp.float32)
        W_lin = 0.05 * jax.random.normal(ks[4], (L, H, H), dtype=jnp.float32)
        b_lin = jnp.zeros((L, H), dtype=jnp.float32)
        ln_a = jnp.ones((L, H), dtype=jnp.float32)
        ln_b = jnp.zeros((L, H), dtype=jnp.float32)
        return {'hidden_state': hidden_state, 'adjacency_matrix': adjacency_matrix, 'W_left': W_left, 'W_right': W_right, 'W_lin': W_lin, 'b_lin': b_lin, 'ln_a': ln_a, 'ln_b': ln_b}
    _L1_gnn_all = _L1_gnn_setup()
    _L1_gnn_in = {k: v for k, v in _L1_gnn_all.items() if k in ('W_left', 'W_right', 'W_lin', 'b_lin', 'ln_a', 'ln_b')}
    del _L1_gnn_all
    return {'x': x, 'adj': adj, 'L0_gnn_Wl': _L0_gnn_in['Wl'], 'L0_gnn_bl': _L0_gnn_in['bl'], 'L0_gnn_Ws': _L0_gnn_in['Ws'], 'L0_gnn_bs': _L0_gnn_in['bs'], 'L0_gnn_Wr': _L0_gnn_in['Wr'], 'L0_gnn_br': _L0_gnn_in['br'], 'L0_gnn_ln_w': _L0_gnn_in['ln_w'], 'L0_gnn_ln_b': _L0_gnn_in['ln_b'], 'L1_gnn_W_left': _L1_gnn_in['W_left'], 'L1_gnn_W_right': _L1_gnn_in['W_right'], 'L1_gnn_W_lin': _L1_gnn_in['W_lin'], 'L1_gnn_b_lin': _L1_gnn_in['b_lin'], 'L1_gnn_ln_a': _L1_gnn_in['ln_a'], 'L1_gnn_ln_b': _L1_gnn_in['ln_b']}

def reference(x, adj, L0_gnn_Wl, L0_gnn_bl, L0_gnn_Ws, L0_gnn_bs, L0_gnn_Wr, L0_gnn_br, L0_gnn_ln_w, L0_gnn_ln_b, L1_gnn_W_left, L1_gnn_W_right, L1_gnn_W_lin, L1_gnn_b_lin, L1_gnn_ln_a, L1_gnn_ln_b):
    import jax
    import jax.numpy as jnp

    def _L0_gnn_ref(hidden_state, adjacency_matrix, Wl, bl, Ws, bs, Wr, br, ln_w, ln_b):
        import jax, jax.numpy as jnp
        import numpy as np
        LN_EPS = 1e-12

        def _digcn_forward(hidden_state, adjacency_matrix, Wl, bl, Ws, bs, Wr, br, ln_w, ln_b):
            B, S, D = hidden_state.shape
            temper = jnp.asarray(D, jnp.float32) ** 0.5
            i = jnp.arange(S)
            upper = (i[None, :] > i[:, None]).astype(hidden_state.dtype)
            lower = (i[None, :] < i[:, None]).astype(hidden_state.dtype)

            def layer(h, params):
                wl, b_l, ws, b_s, wr, b_r, g, beta = params
                u = jnp.einsum('bid,bjd->bij', h, h) / temper
                a = jax.nn.softmax(u, axis=-1)
                delta = a * adjacency_matrix
                attn = delta / (jnp.sum(delta, axis=-1, keepdims=True) + 1e-10)
                hl = h @ wl.T + b_l
                hs = h @ ws.T + b_s
                hr = h @ wr.T + b_r
                diag_a = jnp.diagonal(attn, axis1=1, axis2=2)
                ctx = jnp.einsum('bij,bjd->bid', attn * upper, hl) + diag_a[..., None] * hs + jnp.einsum('bij,bjd->bid', attn * lower, hr)
                mean = ctx.mean(-1, keepdims=True)
                var = ctx.var(-1, keepdims=True)
                o = (ctx - mean) / jnp.sqrt(var + LN_EPS) * g + beta
                return (jax.nn.relu(o), None)
            out, _ = jax.lax.scan(layer, hidden_state, (Wl, bl, Ws, bs, Wr, br, ln_w, ln_b))
            return out
        return _digcn_forward(hidden_state, adjacency_matrix, Wl, bl, Ws, bs, Wr, br, ln_w, ln_b)

    def _L1_gnn_ref(hidden_state, adjacency_matrix, W_left, W_right, W_lin, b_lin, ln_a, ln_b):
        import jax, jax.numpy as jnp
        import numpy as np
        B, S, H, L = (32, 256, 384, 2)

        def _layer_norm(z, a, b, eps=0.001):
            mu = jnp.mean(z, axis=-1, keepdims=True)
            sigma = jnp.std(z, axis=-1, keepdims=True, ddof=1)
            return (z - mu) / (sigma + eps) * a + b
        temper = float(np.sqrt(H))
        adj = adjacency_matrix
        adj_tri = jnp.triu(adj, k=1)
        diag_mask = jnp.triu(adj, k=0) - adj_tri
        h = hidden_state
        for l in range(L):
            m_left = jnp.einsum('bsh,oh->bso', h, W_left[l])
            m_right = jnp.einsum('bsh,oh->bso', h, W_right[l])
            u_left = jnp.einsum('bih,bjh->bij', h, m_left) / temper
            u_right = jnp.einsum('bih,bjh->bij', h, m_right) / temper
            u = u_left * adj_tri + u_left * diag_mask + u_right * jnp.swapaxes(adj_tri, 1, 2)
            delta_exp_u = jnp.exp(u) * adj
            attention = delta_exp_u / (jnp.sum(delta_exp_u, axis=2, keepdims=True) + 1e-10)
            h_lin = jnp.einsum('bsh,oh->bso', h, W_lin[l]) + b_lin[l]
            ctx = jnp.matmul(attention, h_lin)
            h = jax.nn.relu(_layer_norm(ctx, ln_a[l], ln_b[l]))
        return h
    h = jnp.maximum(_layernorm(x, axis=-1), 0.0)
    x = x + _L0_gnn_ref(h, adj, L0_gnn_Wl, L0_gnn_bl, L0_gnn_Ws, L0_gnn_bs, L0_gnn_Wr, L0_gnn_br, L0_gnn_ln_w, L0_gnn_ln_b)
    h = jnp.maximum(_layernorm(x, axis=-1), 0.0)
    x = x + _L1_gnn_ref(h, adj, L1_gnn_W_left, L1_gnn_W_right, L1_gnn_W_lin, L1_gnn_b_lin, L1_gnn_ln_a, L1_gnn_ln_b)
    return x

_drawn_inputs = setup_inputs


def setup_inputs(seed=0):
    import zlib

    import numpy as np

    out = dict(_drawn_inputs(seed))
    spreads = {'L0_gnn_bl': (0.0, 0.1),
     'L0_gnn_bs': (0.0, 0.1),
     'L0_gnn_br': (0.0, 0.1),
     'L0_gnn_ln_w': (1.0, 0.2),
     'L0_gnn_ln_b': (0.0, 0.1),
     'L1_gnn_b_lin': (0.0, 0.1),
     'L1_gnn_ln_a': (1.0, 0.2),
     'L1_gnn_ln_b': (0.0, 0.1)}
    factors = {'L1_gnn_W_left': 4.089, 'L1_gnn_W_right': 8.0}
    for name, (base, spread) in spreads.items():
        noise = np.random.default_rng([zlib.crc32(name.encode()), seed]).standard_normal(out[name].shape)
        drawn = base * np.exp(spread * noise) if base else spread * noise
        out[name] = jnp.asarray(drawn.astype(out[name].dtype))
    for name, factor in factors.items():
        out[name] = (out[name] * factor).astype(out[name].dtype)
    return out
```

```python
from contextlib import ExitStack

import concourse.bass as bass
from concourse import mybir

P = 128
S = 128
D = 384
KT = D // P
G = 2
STREAMS = 2
LAYERS = 2
STEPS = STREAMS * LAYERS
GS = G * S
GD = G * D
SCALE = float(D) ** -0.5
PRE_EPS = 1e-5
CTX_EPS = 1e-12
SIGMA_EPS = 1e-3
SUM_EPS = 1e-10

ALU = mybir.AluOpType
ACT = mybir.ActivationFunctionType
F32 = mybir.dt.float32
F32R = mybir.dt.float32r
AX_X = mybir.AxisListType.X

ROW_BIAS = 0
ROW_LN = 6
ROW_LIN = 8
ROW_LN2 = 10
ROWS = 12
C_IDENT, C_UPPER, C_LOWER, C_LEFT, C_RIGHT = range(5)


def after(it, k, per_step, n):
    return it * (STEPS * per_step) + (k * per_step + n)


def after_norm(it, s, per_norm, n):
    return it * (STREAMS * per_norm) + (s * per_norm + n)


def three_passes(pe, out, pairs):
    last = None
    for i, (a_hi, a_lo, b_hi, b_lo) in enumerate(pairs):
        pe.matmul(out, a_hi, b_hi, start=(i == 0), stop=False)
        pe.matmul(out, a_hi, b_lo, start=False, stop=False)
        last = pe.matmul(out, a_lo, b_hi, start=False, stop=(i == len(pairs) - 1))
    return last


def network_one(nc, x, adj, weights, rows, columns, consts, x1):
    graphs = x.shape[0]
    iters = graphs // (G * STREAMS)
    x_g = x.rearrange("(i b) p d -> i p b d", b=G)
    x1_g = x1.rearrange("(i b) p d -> i p b d", b=G)
    adj_g = adj.rearrange("(i b) p d -> i p b d", b=G)

    with ExitStack() as ctx:
        def sb(name, shape, dt=F32):
            return ctx.enter_context(nc.sbuf_tensor("n1_" + name, shape, dt))

        def ps(name, shape):
            return ctx.enter_context(nc.psum_tensor("n1_ps_" + name, shape, F32))

        def sem(name):
            return ctx.enter_context(nc.semaphore("n1_" + name))

        w_raw = sb("w_raw", [P, 3, KT * D])
        w_hi = sb("w_hi", [P, LAYERS * 3, KT, D], F32R)
        w_lo = sb("w_lo", [P, LAYERS * 3, KT, D], F32R)
        row = sb("row", [P, ROW_LIN, D])
        col = sb("col", [P, 4 * KT])
        const = sb("const", [P, 5, S])
        ident = const[:, C_IDENT, :]
        minus_half = sb("minus_half", [P, G])

        x_in = [sb(f"x_in{s}", [P, G, D]) for s in range(STREAMS)]
        x_res = [sb(f"x_res{s}", [P, G, D]) for s in range(STREAMS)]
        x_out = [sb(f"x_out{s}", [P, G, D]) for s in range(STREAMS)]
        adj_in = [sb(f"adj_in{s}", [P, G, S]) for s in range(STREAMS)]
        ctx_o = [sb(f"ctx_o{s}", [P, G, D]) for s in range(STREAMS)]
        hT_hi = [sb(f"hT_hi{s}", [P, KT, GS], F32R) for s in range(STREAMS)]
        hT_lo = [sb(f"hT_lo{s}", [P, KT, GS], F32R) for s in range(STREAMS)]

        hT = sb("hT", [P, KT, GS])
        proj = sb("proj", [P, G, 2, D])
        proj_hi = sb("proj_hi", [P, G, 2, D], F32R)
        proj_lo = sb("proj_lo", [P, G, 2, D], F32R)
        own = sb("own", [P, G, D])
        prob = sb("prob", [P, G, S])
        delta = sb("delta", [P, G, S])
        attn = sb("attn", [P, G, S])
        attn_diag = sb("attn_diag", [P, G, S])
        aT = sb("aT", [P, G, 2, S])
        aT_hi = sb("aT_hi", [P, G, 2, S], F32R)
        aT_lo = sb("aT_lo", [P, G, 2, S], F32R)
        neg_max = sb("neg_max", [P, G])
        exp_bias = sb("exp_bias", [P, G])
        z_sum = sb("z_sum", [P, G])
        d_sum = sb("d_sum", [P, G])
        den = sb("den", [P, G])
        inv_den = sb("inv_den", [P, G])
        diag = sb("diag", [P, G])
        c_stats = sb("c_stats", [P, G, 6])
        c_mv = sb("c_mv", [P, G, 2])
        c_var = sb("c_var", [P, G])
        c_rstd = sb("c_rstd", [P, G])
        x_stats = sb("x_stats", [P, G, 6])
        x_mv = sb("x_mv", [P, G, 2])
        x_var = sb("x_var", [P, G])
        x_rstd = sb("x_rstd", [P, G])

        ps_oT = ps("oT", [P, 1024])
        ps_ua = ps("ua", [P, 2, GS])
        ps_w = ps("w", [P, 3, 512])
        ps_ctx = ps("ctx", [P, G, 512])

        const_loaded, w_loaded = sem("const_loaded"), [sem(f"w_loaded{i}") for i in range(6)]
        x_loaded = [sem(f"x_loaded{s}") for s in range(STREAMS)]
        adj_loaded = [sem(f"adj_loaded{s}") for s in range(STREAMS)]
        x1_stored = [sem(f"x1_stored{s}") for s in range(STREAMS)]
        w_hi_ready, w_lo_ready = sem("w_hi_ready"), sem("w_lo_ready")
        half_ready = sem("half_ready")
        o_ready, oT_psum, hT_ready = sem("o_ready"), sem("oT_psum"), sem("hT_ready")
        hT_hi_ready, hT_lo_ready = sem("hT_hi_ready"), sem("hT_lo_ready")
        u_psum, max_done, exp_bias_ready = sem("u_psum"), sem("max_done"), sem("exp_bias_ready")
        exp_done, delta_done, den_done = sem("exp_done"), sem("delta_done"), sem("den_done")
        inv_den_done, attn_ready, diag_done = sem("inv_den_done"), sem("attn_ready"), sem("diag_done")
        aT_psum, aT_ready = sem("aT_psum"), sem("aT_ready")
        aT_hi_ready, aT_lo_ready = sem("aT_hi_ready"), sem("aT_lo_ready")
        proj_psum, proj_out = sem("proj_psum"), sem("proj_out")
        proj_hi_ready, proj_lo_ready = sem("proj_hi_ready"), sem("proj_lo_ready")
        ctx_psum, ctx_done, c_stats_done = sem("ctx_psum"), sem("ctx_done"), sem("c_stats_done")
        c_mv_done, c_var_ready, c_rstd_ready = sem("c_mv_done"), sem("c_var_ready"), sem("c_rstd_ready")
        x_stats_done, x_mv_done = sem("x_stats_done"), sem("x_mv_done")
        x_var_ready, x_rstd_ready = sem("x_var_ready"), sem("x_rstd_ready")
        x_res_ready, scaled_done, shifted_done = sem("x_res_ready"), sem("scaled_done"), sem("shifted_done")
        x1_ready = sem("x1_ready")

        stats_seen = sem("stats_seen")

        block = ctx.enter_context(nc.Block())

        @block.sync
        def _(sp):
            def group(it, s):
                return (it % iters) * STREAMS + s

            def load_x(it, s):
                i = group(it, s)
                sp.dma_start(x_in[s][:], x_g[bass.ds(i, 1)].rearrange("a p b d -> (a p) b d")
                             ).then_inc(x_loaded[s], 16)

            def load_adj(it, s):
                i = group(it, s)
                sp.dma_start(adj_in[s][:], adj_g[bass.ds(i, 1)].rearrange("a p b d -> (a p) b d")
                             ).then_inc(adj_loaded[s], 16)

            load_x(0, 0)
            sp.dma_start(const[:], consts).then_inc(const_loaded, 16)
            sp.dma_start(col[:], columns).then_inc(const_loaded, 16)
            for i in range(3):
                sp.dma_start(w_raw[:, i, :], weights[i]).then_inc(w_loaded[i], 16)
            load_adj(0, 0)
            load_x(0, 1)
            load_adj(0, 1)
            for r in range(ROW_LIN):
                sp.dma_start(row[:, r, :], rows[r:r + 1, :].partition_broadcast(P)).then_inc(const_loaded, 16)
            for i in range(3, 6):
                sp.wait_ge(w_hi_ready, i - 2)
                sp.wait_ge(w_lo_ready, i - 2)
                sp.dma_start(w_raw[:, i - 3, :], weights[i]).then_inc(w_loaded[i], 16)
            sp.wait_ge(o_ready, 1)
            sp.wait_ge(x_res_ready, 1)
            load_x(1, 0)
            for s in range(STREAMS):
                sp.sem_inc(x1_stored[s], 16)

            with sp.Fori(0, iters) as it:
                due = [sp.to_reg(v) for v in (
                    after(it, 1, 1, 1),
                    after_norm(it, 1, 1, 1),
                    after(it, 2, G, G),
                    after_norm(it, 0, G, G),
                    after(it, 4, 1, 1),
                    after_norm(it, 2, 1, 1),
                    after(it, 3, G, G),
                    after_norm(it, 1, G, G),
                )]
                sp.wait_ge(o_ready, due[0])
                sp.wait_ge(x_res_ready, due[1])
                load_x(it + 1, 1)
                sp.wait_ge(delta_done, due[2])
                load_adj(it + 1, 0)
                sp.wait_ge(x1_ready, due[3])
                sp.dma_start(x1_g[bass.ds(group(it, 0), 1)].rearrange("a p b d -> (a p) b d"),
                             x_out[0][:]).then_inc(x1_stored[0], 16)
                sp.wait_ge(o_ready, due[4])
                sp.wait_ge(x_res_ready, due[5])
                load_x(it + 2, 0)
                sp.wait_ge(delta_done, due[6])
                load_adj(it + 1, 1)
                sp.wait_ge(x1_ready, due[7])
                sp.dma_start(x1_g[bass.ds(group(it, 1), 1)].rearrange("a p b d -> (a p) b d"),
                             x_out[1][:]).then_inc(x1_stored[1], 16)
            sp.wait_ge(x_loaded[0], 16 * (iters + 2))
            sp.wait_ge(x_loaded[1], 16 * (iters + 1))
            for s in range(STREAMS):
                sp.wait_ge(adj_loaded[s], 16 * (iters + 1))
                sp.wait_ge(x1_stored[s], 16 * (iters + 1))

        @block.tensor
        def _(pe):
            def transpose_o(it, k):
                s = k % STREAMS
                pe.wait_ge(o_ready, after(it, k, 1, 1))
                if k or not isinstance(it, int):
                    pe.wait_ge(hT_ready, after(it, k, 1, 0))
                for kt in range(KT):
                    for b in range(G):
                        last = pe.transpose(ps_oT[:, kt * GS + b * S:kt * GS + (b + 1) * S],
                                            ctx_o[s][:, b, kt * P:(kt + 1) * P], ident)
                last.then_inc(oT_psum, 1)

            def scores(it, k):
                s = k % STREAMS
                pe.wait_ge(hT_hi_ready, after(it, k, 1, 1))
                pe.wait_ge(hT_lo_ready, after(it, k, 1, 1))
                for b in range(G):
                    h = [(hT_hi[s][:, kt, b * S:(b + 1) * S], hT_lo[s][:, kt, b * S:(b + 1) * S])
                         for kt in range(KT)]
                    last = three_passes(pe, ps_ua[:, 0, b * S:(b + 1) * S], [(*t, *t) for t in h])
                last.then_inc(u_psum, 1)

            def project(it, k, b, m):
                s, n = k % STREAMS, b * 3 + m
                pe.wait_ge(proj_out, after(it, k, 6, n + 1))
                w = (k // STREAMS) * 3 + m
                three_passes(pe, ps_w[:, m, 0:D], [
                    (hT_hi[s][:, kt, b * S:(b + 1) * S], hT_lo[s][:, kt, b * S:(b + 1) * S],
                     w_hi[:, w, kt, :], w_lo[:, w, kt, :]) for kt in range(KT)]).then_inc(proj_psum, 1)

            def transpose_attn(it, k):
                pe.wait_ge(attn_ready, after(it, k, G, G))
                for b in range(G):
                    last = pe.transpose(ps_ua[:, 1, b * S:(b + 1) * S], attn[:, b, :], ident)
                last.then_inc(aT_psum, 1)

            def context(it, k, b):
                if b == 0:
                    pe.wait_ge(aT_hi_ready, after(it, k, 1, 1))
                    pe.wait_ge(aT_lo_ready, after(it, k, 1, 1))
                pe.wait_ge(proj_hi_ready, after(it, k, G, b + 1))
                pe.wait_ge(proj_lo_ready, after(it, k, G, b + 1))
                three_passes(pe, ps_ctx[:, b, 0:D], [
                    (aT_hi[:, b, m, :], aT_lo[:, b, m, :], proj_hi[:, b, m, :], proj_lo[:, b, m, :])
                    for m in range(2)]).then_inc(ctx_psum, 1)

            pe.wait_ge(const_loaded, 16 * (2 + ROW_LIN))
            transpose_o(0, 0)
            pe.wait_ge(w_hi_ready, LAYERS * 3)
            pe.wait_ge(w_lo_ready, LAYERS * 3)
            with pe.Fori(0, iters) as it:
                for k in range(STEPS):
                    scores(it, k)
                    for m in range(3):
                        project(it, k, 0, m)
                    project(it, k, 1, 0)
                    transpose_attn(it, k)
                    transpose_o(it, k + 1)
                    project(it, k, 1, 1)
                    project(it, k, 1, 2)
                    for b in range(G):
                        context(it, k, b)

        @block.scalar
        def _(act):
            def relu_hT(it, k):
                layer = (k % STEPS) // STREAMS
                act.wait_ge(oT_psum, after(it, k, 1, 1))
                if k or not isinstance(it, int):
                    act.wait_ge(hT_lo_ready, after(it, k, 1, 0))
                if layer == 0:
                    last = act.activation(hT[:].rearrange("p t n -> p (t n)"), ps_oT[:, 0:KT * GS], ACT.Relu)
                else:
                    for kt in range(KT):
                        last = act.activation(hT[:, kt, :], ps_oT[:, kt * GS:(kt + 1) * GS], ACT.Relu,
                                              bias=col[:, KT + kt:KT + kt + 1], scale=col[:, kt:kt + 1])
                last.then_inc(hT_ready, 1)
                act.wait_ge(hT_ready, after(it, k, 1, 1))
                act.activation(hT_hi[k % STREAMS][:], hT[:], ACT.Copy).then_inc(hT_hi_ready, 1)

            def keep_x(it, s, first=False):
                if first:
                    act.wait_ge(x_loaded[s], 16)
                else:
                    act.wait_ge(x_loaded[s], 16 * it + 16 * (2 - s))
                act.activation(x_res[s][:], x_in[s][:], ACT.Copy).then_inc(x_res_ready, 1)

            def proj_high(it, k, b):
                act.wait_ge(proj_out, after(it, k, 6, 3 + b * 3 + 2))
                act.activation(proj_hi[:, b], proj[:, b], ACT.Copy).then_inc(proj_hi_ready, 1)

            for i in range(LAYERS * 3):
                act.wait_ge(w_loaded[i], 16)
                act.activation(w_hi[:, i].rearrange("p t n -> p (t n)"), w_raw[:, i % 3, :], ACT.Copy
                               ).then_inc(w_hi_ready, 1)
                if i == 2:
                    keep_x(0, 0, first=True)
                    act.wait_ge(const_loaded, 16 * (2 + ROW_LIN))
                    relu_hT(0, 0)
            with act.Fori(0, iters) as it:
                for k in range(STEPS):
                    act.wait_ge(exp_bias_ready, after(it, k, 1, 1))
                    for b in range(G):
                        act.activation(prob[:, b, :], ps_ua[:, 0, b * S:(b + 1) * S], ACT.Exp,
                                       bias=exp_bias[:, b:b + 1], scale=SCALE,
                                       accum_out=z_sum[:, b:b + 1]).then_inc(exp_done, 1)
                    if k == 0:
                        keep_x(it, 1)
                    if k == 3:
                        act.wait_ge(x1_ready, after_norm(it, 0, G, G))
                        keep_x(it, 0)
                    proj_high(it, k, 0)
                    act.wait_ge(aT_ready, after(it, k, 1, 1))
                    act.activation(aT_hi[:], aT[:], ACT.Copy).then_inc(aT_hi_ready, 1)
                    relu_hT(it, k + 1)
                    proj_high(it, k, 1)

        @block.gpsimd
        def _(pool):
            def power(out, base, exponent):
                return pool.tensor_tensor(out, base, exponent, ALU.pow)

            def hT_low(it, k):
                pool.wait_ge(hT_ready, after(it, k, 1, 1))
                pool.wait_ge(hT_hi_ready, after(it, k, 1, 1))
                pool.tensor_tensor(hT_lo[k % STREAMS][:], hT[:], hT_hi[k % STREAMS][:].bitcast(F32),
                                   ALU.subtract).then_inc(hT_lo_ready, 1)

            def proj_low(it, k, b):
                pool.wait_ge(proj_hi_ready, after(it, k, G, b + 1))
                pool.tensor_tensor(proj_lo[:, b], proj[:, b], proj_hi[:, b].bitcast(F32),
                                   ALU.subtract).then_inc(proj_lo_ready, 1)

            def x_power(it, s):
                pool.wait_ge(x_var_ready, after_norm(it, s, 1, 1))
                power(x_rstd[:], x_var[:], minus_half[:]).then_inc(x_rstd_ready, 1)

            pool.memset(minus_half[:], -0.5).then_inc(half_ready, 1)
            pool.wait_ge(half_ready, 1)
            x_power(0, 0)
            hT_low(0, 0)
            with pool.Fori(0, iters) as it:
                for k in range(STEPS):
                    if k == 0:
                        x_power(it, 1)
                    if k == 3:
                        x_power(it, 2)
                    proj_low(it, k, 0)
                    proj_low(it, k, 1)
                    hT_low(it, k + 1)
                    pool.wait_ge(c_var_ready, after(it, k, 1, 1))
                    power(c_rstd[:], c_var[:], minus_half[:]).then_inc(c_rstd_ready, 1)

        @block.vector
        def _(dve):
            def stats_wait(sem_of_stats, value):
                dve.wait_ge(sem_of_stats, value)
                dve.sem_inc(stats_seen, 1)

            def pre_norm(it, s):
                if isinstance(it, int):
                    dve.wait_ge(x_loaded[s], 16)
                else:
                    dve.wait_ge(x_loaded[s % 2], 16 * it + 16 * (2 if s == 2 else 1))
                t = s % STREAMS
                for b in range(G):
                    dve.bn_stats(x_stats[:, b, :], x_in[t][:, b, :]).then_inc(x_stats_done, 1)
                stats_wait(x_stats_done, after_norm(it, s, G, G))
                for b in range(G):
                    dve.bn_aggr(x_mv[:, b, :], x_stats[:, b, :]).then_inc(x_mv_done, 1)
                dve.wait_ge(x_mv_done, after_norm(it, s, G, G))
                dve.tensor_scalar(x_var[:], x_mv[:, :, 1], PRE_EPS, None, ALU.add).then_inc(x_var_ready, 1)
                dve.wait_ge(x_rstd_ready, after_norm(it, s, 1, 1))
                for b in range(G):
                    last = dve.tensor_scalar(ctx_o[t][:, b, :], x_in[t][:, b, :], x_mv[:, b, 0:1],
                                             x_rstd[:, b:b + 1], ALU.subtract, ALU.mult)
                last.then_inc(o_ready, 1)

            def score_max(it, k):
                dve.wait_ge(u_psum, after(it, k, 1, 1))
                dve.tensor_reduce(neg_max[:], ps_ua[:, 0, :].rearrange("p (b n) -> p b n", b=G), AX_X,
                                  ALU.max, negate=True).then_inc(max_done, 1)
                dve.wait_ge(max_done, after(it, k, 1, 1))
                dve.tensor_scalar(exp_bias[:], neg_max[:], SCALE, None, ALU.mult).then_inc(exp_bias_ready, 1)

            def attention(it, k):
                s = k % STREAMS
                dve.wait_ge(adj_loaded[s], 16 * it + 16)
                for b in range(G):
                    dve.wait_ge(exp_done, after(it, k, G, b + 1))
                    dve.tensor_tensor_reduce(delta[:, b, :], prob[:, b, :], adj_in[s][:, b, :], 1.0, 0.0,
                                             ALU.mult, ALU.add, d_sum[:, b:b + 1]).then_inc(delta_done, 1)
                dve.wait_ge(delta_done, after(it, k, G, G))
                dve.scalar_tensor_tensor(out=den[:], in0=z_sum[:], scalar=SUM_EPS, in1=d_sum[:],
                                         op0=ALU.mult, op1=ALU.add).then_inc(den_done, 1)
                dve.wait_ge(den_done, after(it, k, 1, 1))
                dve.reciprocal(inv_den[:], den[:]).then_inc(inv_den_done, 1)
                dve.wait_ge(inv_den_done, after(it, k, 1, 1))
                for b in range(G):
                    dve.tensor_scalar(attn[:, b, :], delta[:, b, :], inv_den[:, b:b + 1], None,
                                      ALU.mult).then_inc(attn_ready, 1)
                for b in range(G):
                    dve.wait_ge(attn_ready, after(it, k, G, b + 1))
                    dve.tensor_tensor_reduce(attn_diag[:, b, :], attn[:, b, :], ident, 1.0, 0.0,
                                             ALU.mult, ALU.add, diag[:, b:b + 1]).then_inc(diag_done, 1)

            def proj_bias(it, k, b, m):
                dve.wait_ge(proj_psum, after(it, k, 6, b * 3 + m + 1))
                out = proj[:, b, m, :] if m < 2 else own[:, b, :]
                dve.tensor_tensor(out, ps_w[:, m, 0:D], row[:, ROW_BIAS + (k // STREAMS) * 3 + m, :],
                                  ALU.add).then_inc(proj_out, 1)

            def mask_attn(it, k):
                dve.wait_ge(aT_psum, after(it, k, 1, 1))
                a = ps_ua[:, 1, :].rearrange("p (b n) -> p b n", b=G).unsqueeze(2).to_broadcast([P, G, 2, S])
                mask = const[:, C_UPPER:C_UPPER + 2, :].unsqueeze(1).to_broadcast([P, G, 2, S])
                dve.tensor_tensor(aT[:], a, mask, ALU.mult).then_inc(aT_ready, 1)

            def attn_low(it, k):
                dve.wait_ge(aT_ready, after(it, k, 1, 1))
                dve.wait_ge(aT_hi_ready, after(it, k, 1, 1))
                dve.tensor_tensor(aT_lo[:], aT[:], aT_hi[:].bitcast(F32), ALU.subtract).then_inc(aT_lo_ready, 1)

            def context_stats(it, k):
                s = k % STREAMS
                for b in range(G):
                    dve.wait_ge(ctx_psum, after(it, k, G, b + 1))
                    dve.wait_ge(diag_done, after(it, k, G, b + 1))
                    dve.wait_ge(proj_out, after(it, k, 6, 3 + 3 * b + 3))
                    dve.scalar_tensor_tensor(out=ctx_o[s][:, b, :], in0=own[:, b, :], scalar=diag[:, b:b + 1],
                                             in1=ps_ctx[:, b, 0:D], op0=ALU.mult, op1=ALU.add
                                             ).then_inc(ctx_done, 1)
                    dve.wait_ge(ctx_done, after(it, k, G, b + 1))
                    dve.bn_stats(c_stats[:, b, :], ctx_o[s][:, b, :]).then_inc(c_stats_done, 1)
                stats_wait(c_stats_done, after(it, k, G, G))
                for b in range(G):
                    dve.bn_aggr(c_mv[:, b, :], c_stats[:, b, :]).then_inc(c_mv_done, 1)
                dve.wait_ge(c_mv_done, after(it, k, G, G))
                dve.tensor_scalar(c_var[:], c_mv[:, :, 1], CTX_EPS, None, ALU.add).then_inc(c_var_ready, 1)

            def normalise(it, k):
                s = k % STREAMS
                dve.wait_ge(c_rstd_ready, after(it, k, 1, 1))
                for b in range(G):
                    last = dve.tensor_scalar(ctx_o[s][:, b, :], ctx_o[s][:, b, :], c_mv[:, b, 0:1],
                                             c_rstd[:, b:b + 1], ALU.subtract, ALU.mult)
                last.then_inc(o_ready, 1)

            def residual(it, k):
                s = k % STREAMS
                dve.wait_ge(c_rstd_ready, after(it, k, 1, 1))
                dve.wait_ge(x1_stored[s], 16 * it + 16)
                dve.wait_ge(x_res_ready, after_norm(it, s, 1, 1))
                for b in range(G):
                    dve.scalar_tensor_tensor(out=x_out[s][:, b, :], in0=ctx_o[s][:, b, :], scalar=c_mv[:, b, 0:1],
                                             in1=row[:, ROW_LN, :], op0=ALU.subtract, op1=ALU.mult
                                             ).then_inc(scaled_done, 1)
                for b in range(G):
                    dve.wait_ge(scaled_done, after_norm(it, s, G, b + 1))
                    dve.scalar_tensor_tensor(out=x_out[s][:, b, :], in0=x_out[s][:, b, :],
                                             scalar=c_rstd[:, b:b + 1], in1=row[:, ROW_LN + 1, :],
                                             op0=ALU.mult, op1=ALU.add).then_inc(shifted_done, 1)
                for b in range(G):
                    dve.wait_ge(shifted_done, after_norm(it, s, G, b + 1))
                    dve.scalar_tensor_tensor(out=x_out[s][:, b, :], in0=x_out[s][:, b, :], scalar=0.0,
                                             in1=x_res[s][:, b, :], op0=ALU.max, op1=ALU.add
                                             ).then_inc(x1_ready, 1)

            pre_norm(0, 0)
            for i in range(LAYERS * 3):
                dve.wait_ge(w_hi_ready, i + 1)
                dve.tensor_tensor(w_lo[:, i].rearrange("p t n -> p (t n)"), w_raw[:, i % 3, :],
                                  w_hi[:, i].rearrange("p t n -> p (t n)").bitcast(F32), ALU.subtract
                                  ).then_inc(w_lo_ready, 1)
            dve.wait_ge(const_loaded, 16 * (2 + ROW_LIN))
            dve.sem_inc(proj_out, 3)
            with dve.Fori(0, iters) as it:
                for k in range(STEPS):
                    score_max(it, k)
                    if k == 0:
                        pre_norm(it, 1)
                    elif k == 3:
                        residual(it, 2)
                        pre_norm(it, 2)
                    else:
                        normalise(it, k - 1)
                    attention(it, k)
                    for m in range(3):
                        proj_bias(it, k, 0, m)
                    proj_bias(it, k, 1, 0)
                    mask_attn(it, k)
                    attn_low(it, k)
                    proj_bias(it, k, 1, 1)
                    proj_bias(it, k, 1, 2)
                    context_stats(it, k)
                    if k == 3:
                        residual(it, 3)


def network_two(nc, x1, adj, weights, rows, columns, consts, out):
    graphs = x1.shape[0]
    iters = graphs // (G * STREAMS)
    x_g = x1.rearrange("(i b) p d -> i p b d", b=G)
    out_g = out.rearrange("(i b) p d -> i p b d", b=G)
    adj_g = adj.rearrange("(i b) p d -> i p b d", b=G)
    LEAD = 2
    ONE = D

    with ExitStack() as ctx:
        def sb(name, shape, dt=F32):
            return ctx.enter_context(nc.sbuf_tensor("n2_" + name, shape, dt))

        def ps(name, shape):
            return ctx.enter_context(nc.psum_tensor("n2_ps_" + name, shape, F32))

        def sem(name):
            return ctx.enter_context(nc.semaphore("n2_" + name))

        w_raw = sb("w_raw", [P, 3, KT * D])
        w_hi = sb("w_hi", [P, LAYERS * 3, KT, D], F32R)
        w_lo = sb("w_lo", [P, LAYERS * 3, KT, D], F32R)
        row = sb("row", [P, 4, D])
        col = sb("col", [P, 4 * KT])
        const = sb("const", [P, 5, S])
        ident = const[:, C_IDENT, :]
        minus_half = sb("minus_half", [P, G])
        half = sb("half", [P, G])

        x_in = [sb(f"x_in{s}", [P, G, D]) for s in range(STREAMS)]
        x_res = [sb(f"x_res{s}", [P, G, D]) for s in range(STREAMS)]
        x_out = [sb(f"x_out{s}", [P, G, D]) for s in range(STREAMS)]
        adj_in = [sb(f"adj_in{s}", [P, G, S]) for s in range(STREAMS)]
        adjT = [sb(f"adjT{s}", [P, G, S]) for s in range(STREAMS)]
        sides = [sb(f"sides{s}", [P, G, 2, S]) for s in range(STREAMS)]
        ctx_o = [sb(f"ctx_o{s}", [P, G, D]) for s in range(STREAMS)]
        hT_hi = [sb(f"hT_hi{s}", [P, KT, GS], F32R) for s in range(STREAMS)]
        hT_lo = [sb(f"hT_lo{s}", [P, KT, GS], F32R) for s in range(STREAMS)]

        hT = sb("hT", [P, KT, GS])
        wh_hi = sb("wh_hi", [P, KT, 2, GS], F32R)
        wh_lo = sb("wh_lo", [P, KT, 2, GS], F32R)
        lin = sb("lin", [P, G, D])
        lin_hi = sb("lin_hi", [P, G, D + 2], F32R)
        lin_lo = sb("lin_lo", [P, G, D + 2], F32R)
        uT2 = sb("uT2", [P, G, 2, S])
        uT = sb("uT", [P, G, S])
        prob = sb("prob", [P, G, S])
        dT = sb("dT", [P, G, S])
        dT_hi = sb("dT_hi", [P, G, S], F32R)
        dT_lo = sb("dT_lo", [P, G, S], F32R)
        den = sb("den", [P, G])
        inv_den = sb("inv_den", [P, G])
        c_stats = sb("c_stats", [P, G, 6])
        c_mv = sb("c_mv", [P, G, 2])
        c_var = sb("c_var", [P, G])
        c_sigma = sb("c_sigma", [P, G])
        c_sigma_eps = sb("c_sigma_eps", [P, G])
        c_rstd = sb("c_rstd", [P, G])
        x_stats = sb("x_stats", [P, G, 6])
        x_mv = sb("x_mv", [P, G, 2])
        x_var = sb("x_var", [P, G])
        x_rstd = sb("x_rstd", [P, G])

        ps_oT = ps("oT", [P, 1024])
        ps_wh = ps("wh", [P, 2, 2, GS])
        ps_lin = ps("lin", [P, 512])
        ps_u = ps("u", [P, G, 2, S])
        ps_ctx = ps("ctx", [P, G, 512])
        ADJ = KT * GS

        const_loaded, w_loaded = sem("const_loaded"), [sem(f"w_loaded{i}") for i in range(6)]
        x_loaded = [sem(f"x_loaded{s}") for s in range(STREAMS)]
        adj_loaded = [sem(f"adj_loaded{s}") for s in range(STREAMS)]
        out_stored = [sem(f"out_stored{s}") for s in range(STREAMS)]
        w_hi_ready, w_lo_ready = sem("w_hi_ready"), sem("w_lo_ready")
        half_ready, ones_ready = sem("half_ready"), sem("ones_ready")
        o_ready, oT_psum, hT_ready = sem("o_ready"), sem("oT_psum"), sem("hT_ready")
        hT_hi_ready, hT_lo_ready = sem("hT_hi_ready"), sem("hT_lo_ready")
        adjT_ready, sides_done = sem("adjT_ready"), sem("sides_done")
        wh_psum, wh_hi_ready, wh_lo_ready = sem("wh_psum"), sem("wh_hi_ready"), sem("wh_lo_ready")
        lin_psum, lin_out = sem("lin_psum"), sem("lin_out")
        lin_hi_ready, lin_lo_ready = sem("lin_hi_ready"), sem("lin_lo_ready")
        u_psum, uT2_done, uT_ready = sem("u_psum"), sem("uT2_done"), sem("uT_ready")
        exp_done, dT_ready = sem("exp_done"), sem("dT_ready")
        dT_hi_ready, dT_lo_ready = sem("dT_hi_ready"), sem("dT_lo_ready")
        ctx_psum, den_done, inv_den_ready = sem("ctx_psum"), sem("den_done"), sem("inv_den_ready")
        ctx_done, c_stats_done, c_mv_done = sem("ctx_done"), sem("c_stats_done"), sem("c_mv_done")
        c_var_ready, c_sigma_ready = sem("c_var_ready"), sem("c_sigma_ready")
        c_sigma_eps_done, c_rstd_done = sem("c_sigma_eps_done"), sem("c_rstd_done")
        x_stats_done, x_mv_done = sem("x_stats_done"), sem("x_mv_done")
        x_var_ready, x_rstd_ready = sem("x_var_ready"), sem("x_rstd_ready")
        x_res_ready, scaled_done, shifted_done = sem("x_res_ready"), sem("scaled_done"), sem("shifted_done")
        sum_ready = sem("sum_ready")

        stats_seen = sem("stats_seen")

        block = ctx.enter_context(nc.Block())

        @block.sync
        def _(sp):
            def group(it, s):
                return (it % iters) * STREAMS + s

            def load_x(it, s):
                sp.dma_start(x_in[s][:], x_g[bass.ds(group(it, s), 1)].rearrange("a p b d -> (a p) b d")
                             ).then_inc(x_loaded[s], 16)

            def load_adj(it, s):
                sp.dma_start(adj_in[s][:], adj_g[bass.ds(group(it, s), 1)].rearrange("a p b d -> (a p) b d")
                             ).then_inc(adj_loaded[s], 16)

            load_x(0, 0)
            load_adj(0, 0)
            sp.dma_start(const[:], consts).then_inc(const_loaded, 16)
            sp.dma_start(col[:], columns).then_inc(const_loaded, 16)
            for i in range(3):
                sp.dma_start(w_raw[:, i, :], weights[6 + i]).then_inc(w_loaded[i], 16)
            load_x(0, 1)
            load_adj(0, 1)
            for r in range(4):
                sp.dma_start(row[:, r, :], rows[ROW_LIN + r:ROW_LIN + r + 1, :].partition_broadcast(P)
                             ).then_inc(const_loaded, 16)
            for i in range(3, 6):
                sp.wait_ge(w_hi_ready, i - 2)
                sp.wait_ge(w_lo_ready, i - 2)
                sp.dma_start(w_raw[:, i - 3, :], weights[6 + i]).then_inc(w_loaded[i], 16)
            sp.wait_ge(o_ready, 1)
            sp.wait_ge(x_res_ready, 1)
            load_x(1, 0)
            sp.wait_ge(sides_done, 2)
            load_adj(1, 0)
            for s in range(STREAMS):
                sp.sem_inc(out_stored[s], 16)

            with sp.Fori(0, iters) as it:
                due = [sp.to_reg(v) for v in (
                    after(it, 1, 1, 1),
                    after_norm(it, 1, 1, 1),
                    after_norm(it, 1, 2, 2),
                    after_norm(it, 0, G, G),
                    after(it, 4, 1, 1),
                    after_norm(it, 2, 1, 1),
                    after_norm(it, 2, 2, 2),
                    after_norm(it, 1, G, G),
                )]
                sp.wait_ge(o_ready, due[0])
                sp.wait_ge(x_res_ready, due[1])
                load_x(it + 1, 1)
                sp.wait_ge(sides_done, due[2])
                load_adj(it + 1, 1)
                sp.wait_ge(sum_ready, due[3])
                sp.dma_start(out_g[bass.ds(group(it, 0), 1)].rearrange("a p b d -> (a p) b d"),
                             x_out[0][:]).then_inc(out_stored[0], 16)
                sp.wait_ge(o_ready, due[4])
                sp.wait_ge(x_res_ready, due[5])
                load_x(it + 2, 0)
                sp.wait_ge(sides_done, due[6])
                load_adj(it + 2, 0)
                sp.wait_ge(sum_ready, due[7])
                sp.dma_start(out_g[bass.ds(group(it, 1), 1)].rearrange("a p b d -> (a p) b d"),
                             x_out[1][:]).then_inc(out_stored[1], 16)
            for s in range(STREAMS):
                sp.wait_ge(x_loaded[s], 16 * (iters + 2 - s))
                sp.wait_ge(adj_loaded[s], 16 * (iters + 2 - s))
                sp.wait_ge(out_stored[s], 16 * (iters + 1))

        @block.tensor
        def _(pe):
            def transpose_o(it, k):
                s = k % STREAMS
                pe.wait_ge(o_ready, after(it, k, 1, 1))
                if k or not isinstance(it, int):
                    pe.wait_ge(hT_ready, after(it, k, 1, 0))
                if (k % STEPS) < STREAMS:
                    pe.wait_ge(adj_loaded[s], 16 * it + 16 * (2 if k == STEPS else 1))
                    for b in range(G):
                        pe.transpose(ps_oT[:, ADJ + b * S:ADJ + (b + 1) * S], adj_in[s][:, b, :], ident)
                for kt in range(KT):
                    for b in range(G):
                        last = pe.transpose(ps_oT[:, kt * GS + b * S:kt * GS + (b + 1) * S],
                                            ctx_o[s][:, b, kt * P:(kt + 1) * P], ident)
                last.then_inc(oT_psum, 1)

            def factor(it, k, ht):
                s, n = k % STREAMS, (k * KT + ht)
                if ht == 0:
                    pe.wait_ge(hT_hi_ready, after(it, k, 1, 1))
                    pe.wait_ge(hT_lo_ready, after(it, k, 1, 1))
                pe.wait_ge(wh_hi_ready, after(it, k, KT, ht + 1))
                pe.wait_ge(wh_lo_ready, after(it, k, KT, ht + 1))
                for m in range(2):
                    w = ((k % STEPS) // STREAMS) * 3 + m
                    last = three_passes(pe, ps_wh[:, n % 2, m, :], [
                        (w_hi[:, w, ot, ht * P:(ht + 1) * P], w_lo[:, w, ot, ht * P:(ht + 1) * P],
                         hT_hi[s][:, ot, :], hT_lo[s][:, ot, :]) for ot in range(KT)])
                last.then_inc(wh_psum, 1)

            def linear(it, k, b):
                s, w = k % STREAMS, (k // STREAMS) * 3 + 2
                pe.wait_ge(lin_out, after(it, k, G, b + 1))
                three_passes(pe, ps_lin[:, 0:D], [
                    (hT_hi[s][:, kt, b * S:(b + 1) * S], hT_lo[s][:, kt, b * S:(b + 1) * S],
                     w_hi[:, w, kt, :], w_lo[:, w, kt, :]) for kt in range(KT)]).then_inc(lin_psum, 1)

            def scores(it, k):
                s = k % STREAMS
                pe.wait_ge(wh_hi_ready, after(it, k, KT, 2 + KT))
                pe.wait_ge(wh_lo_ready, after(it, k, KT, 2 + KT))
                for b in range(G):
                    last = three_passes(pe, ps_u[:, b], [
                        (hT_hi[s][:, kt, b * S:(b + 1) * S], hT_lo[s][:, kt, b * S:(b + 1) * S],
                         wh_hi[:, kt, :, b * S:(b + 1) * S], wh_lo[:, kt, :, b * S:(b + 1) * S])
                        for kt in range(KT)])
                last.then_inc(u_psum, 1)

            def context(it, k, b):
                if b == 0:
                    pe.wait_ge(dT_hi_ready, after(it, k, 1, 1))
                    pe.wait_ge(dT_lo_ready, after(it, k, 1, 1))
                pe.wait_ge(lin_hi_ready, after(it, k, G, b + 1))
                pe.wait_ge(lin_lo_ready, after(it, k, G, b + 1))
                three_passes(pe, ps_ctx[:, b, 0:D + 2], [
                    (dT_hi[:, b, :], dT_lo[:, b, :], lin_hi[:, b, :], lin_lo[:, b, :])]).then_inc(ctx_psum, 1)

            pe.wait_ge(const_loaded, 16 * 6)
            transpose_o(0, 0)
            pe.wait_ge(w_hi_ready, LAYERS * 3)
            pe.wait_ge(w_lo_ready, LAYERS * 3)
            pe.wait_ge(ones_ready, 4)
            for ht in range(LEAD):
                factor(0, 0, ht)
            with pe.Fori(0, iters) as it:
                for k in range(STEPS):
                    linear(it, k, 0)
                    for ht in range(LEAD, KT):
                        factor(it, k, ht)
                    transpose_o(it, k + 1)
                    linear(it, k, 1)
                    scores(it, k)
                    for ht in range(LEAD):
                        factor(it, k + 1, ht)
                    for b in range(G):
                        context(it, k, b)

        @block.scalar
        def _(act):
            def relu_hT(it, k):
                layer = (k % STEPS) // STREAMS
                act.wait_ge(oT_psum, after(it, k, 1, 1))
                if k or not isinstance(it, int):
                    act.wait_ge(hT_lo_ready, after(it, k, 1, 0))
                if layer == 0:
                    act.activation(adjT[k % STREAMS][:].rearrange("p b n -> p (b n)"),
                                   ps_oT[:, ADJ:ADJ + GS], ACT.Copy).then_inc(adjT_ready, 1)
                    last = act.activation(hT[:].rearrange("p t n -> p (t n)"), ps_oT[:, 0:KT * GS], ACT.Relu)
                else:
                    for kt in range(KT):
                        last = act.activation(hT[:, kt, :], ps_oT[:, kt * GS:(kt + 1) * GS], ACT.Relu,
                                              bias=col[:, 3 * KT + kt:3 * KT + kt + 1],
                                              scale=col[:, 2 * KT + kt:2 * KT + kt + 1])
                last.then_inc(hT_ready, 1)
                act.wait_ge(hT_ready, after(it, k, 1, 1))
                act.activation(hT_hi[k % STREAMS][:], hT[:], ACT.Copy).then_inc(hT_hi_ready, 1)

            def keep_x(it, s, first=False):
                if first:
                    act.wait_ge(x_loaded[s], 16)
                else:
                    act.wait_ge(x_loaded[s], 16 * it + 16 * (2 - s))
                act.activation(x_res[s][:], x_in[s][:], ACT.Copy).then_inc(x_res_ready, 1)

            def factor_high(it, k, ht):
                n = k * KT + ht
                act.wait_ge(wh_psum, after(it, k, KT, ht + 1))
                act.activation(wh_hi[:, ht], ps_wh[:, n % 2], ACT.Copy).then_inc(wh_hi_ready, 1)

            def linear_high(it, k, b):
                act.wait_ge(lin_out, after(it, k, G, 1 + b + 1))
                act.activation(lin_hi[:, b, 0:D], lin[:, b, :], ACT.Copy).then_inc(lin_hi_ready, 1)

            def divide(it, k):
                for b in range(G):
                    act.wait_ge(ctx_psum, after(it, k, G, b + 1))
                    act.wait_ge(inv_den_ready, after(it, k, G, b + 1))
                    act.activation(ctx_o[k % STREAMS][:, b, :], ps_ctx[:, b, 0:D], ACT.Copy,
                                   scale=inv_den[:, b:b + 1]).then_inc(ctx_done, 1)

            keep_x(0, 0, first=True)
            for i in range(LAYERS * 3):
                act.wait_ge(w_loaded[i], 16)
                act.activation(w_hi[:, i].rearrange("p t n -> p (t n)"), w_raw[:, i % 3, :], ACT.Copy
                               ).then_inc(w_hi_ready, 1)
                if i == 2:
                    act.wait_ge(const_loaded, 16 * 6)
                    relu_hT(0, 0)
            act.sem_inc(wh_hi_ready, 2)
            for ht in range(LEAD):
                factor_high(0, 0, ht)
            with act.Fori(0, iters) as it:
                for k in range(STEPS):
                    if k > 0:
                        divide(it, k - 1)
                    linear_high(it, k, 0)
                    for ht in range(LEAD, KT):
                        factor_high(it, k, ht)
                    relu_hT(it, k + 1)
                    linear_high(it, k, 1)
                    if k == 0:
                        act.wait_ge(uT_ready, after(it, k, 1, 1))
                        keep_x(it, 1)
                    if k == 3:
                        act.wait_ge(sum_ready, after_norm(it, 0, G, G))
                        keep_x(it, 0)
                    act.wait_ge(uT_ready, after(it, k, 1, 1))
                    act.activation(prob[:], uT[:], ACT.Exp, scale=SCALE).then_inc(exp_done, 1)
                    act.wait_ge(dT_ready, after(it, k, 1, 1))
                    act.activation(dT_hi[:], dT[:], ACT.Copy).then_inc(dT_hi_ready, 1)
                    for ht in range(LEAD):
                        factor_high(it, k + 1, ht)
                divide(it, 3)

        @block.gpsimd
        def _(pool):
            def hT_low(it, k):
                pool.wait_ge(hT_ready, after(it, k, 1, 1))
                pool.wait_ge(hT_hi_ready, after(it, k, 1, 1))
                pool.tensor_tensor(hT_lo[k % STREAMS][:], hT[:], hT_hi[k % STREAMS][:].bitcast(F32),
                                   ALU.subtract).then_inc(hT_lo_ready, 1)

            def linear_low(it, k, b):
                pool.wait_ge(lin_hi_ready, after(it, k, G, b + 1))
                pool.tensor_tensor(lin_lo[:, b, 0:D], lin[:, b, :], lin_hi[:, b, 0:D].bitcast(F32),
                                   ALU.subtract).then_inc(lin_lo_ready, 1)

            def x_power(it, s):
                pool.wait_ge(x_var_ready, after_norm(it, s, 1, 1))
                pool.tensor_tensor(x_rstd[:], x_var[:], minus_half[:], ALU.pow).then_inc(x_rstd_ready, 1)

            def sigma(it, k):
                pool.wait_ge(c_var_ready, after(it, k, 1, 1))
                pool.tensor_tensor(c_sigma[:], c_var[:], half[:], ALU.pow).then_inc(c_sigma_ready, 1)

            pool.memset(minus_half[:], -0.5).then_inc(half_ready, 1)
            pool.memset(half[:], 0.5).then_inc(half_ready, 1)
            pool.memset(lin_hi[:, :, ONE:ONE + 1].bitcast(F32), 1.0).then_inc(ones_ready, 1)
            pool.memset(lin_hi[:, :, ONE + 1:ONE + 2].bitcast(F32), 0.0).then_inc(ones_ready, 1)
            pool.memset(lin_lo[:, :, ONE:ONE + 1].bitcast(F32), 0.0).then_inc(ones_ready, 1)
            pool.memset(lin_lo[:, :, ONE + 1:ONE + 2].bitcast(F32), 0.0).then_inc(ones_ready, 1)
            pool.wait_ge(half_ready, 2)
            x_power(0, 0)
            hT_low(0, 0)
            with pool.Fori(0, iters) as it:
                for k in range(STEPS):
                    if k > 0:
                        sigma(it, k - 1)
                    if k == 0:
                        x_power(it, 1)
                    if k == 3:
                        x_power(it, 2)
                    linear_low(it, k, 0)
                    hT_low(it, k + 1)
                    linear_low(it, k, 1)
                sigma(it, 3)

        @block.vector
        def _(dve):
            def stats_wait(sem_of_stats, value):
                dve.wait_ge(sem_of_stats, value)
                dve.sem_inc(stats_seen, 1)

            def pre_norm(it, s):
                if isinstance(it, int):
                    dve.wait_ge(x_loaded[s], 16)
                else:
                    dve.wait_ge(x_loaded[s % 2], 16 * it + 16 * (2 if s == 2 else 1))
                t = s % STREAMS
                for b in range(G):
                    dve.bn_stats(x_stats[:, b, :], x_in[t][:, b, :]).then_inc(x_stats_done, 1)
                stats_wait(x_stats_done, after_norm(it, s, G, G))
                for b in range(G):
                    dve.bn_aggr(x_mv[:, b, :], x_stats[:, b, :]).then_inc(x_mv_done, 1)
                dve.wait_ge(x_mv_done, after_norm(it, s, G, G))
                dve.tensor_scalar(x_var[:], x_mv[:, :, 1], PRE_EPS, None, ALU.add).then_inc(x_var_ready, 1)
                dve.wait_ge(x_rstd_ready, after_norm(it, s, 1, 1))
                for b in range(G):
                    last = dve.tensor_scalar(ctx_o[t][:, b, :], x_in[t][:, b, :], x_mv[:, b, 0:1],
                                             x_rstd[:, b:b + 1], ALU.subtract, ALU.mult)
                last.then_inc(o_ready, 1)

            def make_sides(it, s):
                t = s % STREAMS
                dve.wait_ge(adjT_ready, after_norm(it, s, 1, 1))
                for m, a in ((0, adjT[t]), (1, adj_in[t])):
                    mask = const[:, C_LEFT + m, :].unsqueeze(1).to_broadcast([P, G, S])
                    dve.tensor_tensor(sides[t][:, :, m, :], a[:], mask, ALU.mult).then_inc(sides_done, 1)

            def inverse_sum(it, k):
                for b in range(G):
                    dve.wait_ge(ctx_psum, after(it, k, G, b + 1))
                    dve.tensor_scalar(den[:, b:b + 1], ps_ctx[:, b, ONE:ONE + 1], SUM_EPS, None,
                                      ALU.add).then_inc(den_done, 1)
                    dve.wait_ge(den_done, after(it, k, G, b + 1))
                    dve.reciprocal(inv_den[:, b:b + 1], den[:, b:b + 1]).then_inc(inv_den_ready, 1)

            def context_stats(it, k):
                s = k % STREAMS
                for b in range(G):
                    dve.wait_ge(ctx_done, after(it, k, G, b + 1))
                    dve.bn_stats(c_stats[:, b, :], ctx_o[s][:, b, :]).then_inc(c_stats_done, 1)
                stats_wait(c_stats_done, after(it, k, G, G))
                for b in range(G):
                    dve.bn_aggr(c_mv[:, b, :], c_stats[:, b, :]).then_inc(c_mv_done, 1)
                dve.wait_ge(c_mv_done, after(it, k, G, G))
                dve.tensor_scalar(c_var[:], c_mv[:, :, 1], D / (D - 1.0), None, ALU.mult).then_inc(c_var_ready, 1)

            def inverse_sigma(it, k):
                dve.wait_ge(c_sigma_ready, after(it, k, 1, 1))
                dve.tensor_scalar(c_sigma_eps[:], c_sigma[:], SIGMA_EPS, None, ALU.add).then_inc(c_sigma_eps_done, 1)
                dve.wait_ge(c_sigma_eps_done, after(it, k, 1, 1))
                dve.reciprocal(c_rstd[:], c_sigma_eps[:]).then_inc(c_rstd_done, 1)
                dve.wait_ge(c_rstd_done, after(it, k, 1, 1))

            def normalise(it, k):
                s = k % STREAMS
                inverse_sigma(it, k)
                for b in range(G):
                    last = dve.tensor_scalar(ctx_o[s][:, b, :], ctx_o[s][:, b, :], c_mv[:, b, 0:1],
                                             c_rstd[:, b:b + 1], ALU.subtract, ALU.mult)
                last.then_inc(o_ready, 1)

            def residual(it, k):
                s = k % STREAMS
                inverse_sigma(it, k)
                dve.wait_ge(out_stored[s], 16 * it + 16)
                dve.wait_ge(x_res_ready, after_norm(it, s, 1, 1))
                for b in range(G):
                    dve.scalar_tensor_tensor(out=x_out[s][:, b, :], in0=ctx_o[s][:, b, :], scalar=c_mv[:, b, 0:1],
                                             in1=row[:, 2, :], op0=ALU.subtract, op1=ALU.mult
                                             ).then_inc(scaled_done, 1)
                for b in range(G):
                    dve.wait_ge(scaled_done, after_norm(it, s, G, b + 1))
                    dve.scalar_tensor_tensor(out=x_out[s][:, b, :], in0=x_out[s][:, b, :],
                                             scalar=c_rstd[:, b:b + 1], in1=row[:, 3, :],
                                             op0=ALU.mult, op1=ALU.add).then_inc(shifted_done, 1)
                for b in range(G):
                    dve.wait_ge(shifted_done, after_norm(it, s, G, b + 1))
                    dve.scalar_tensor_tensor(out=x_out[s][:, b, :], in0=x_out[s][:, b, :], scalar=0.0,
                                             in1=x_res[s][:, b, :], op0=ALU.max, op1=ALU.add
                                             ).then_inc(sum_ready, 1)

            def linear_bias(it, k, b):
                dve.wait_ge(lin_psum, after(it, k, G, b + 1))
                dve.tensor_tensor(lin[:, b, :], ps_lin[:, 0:D], row[:, k // STREAMS, :], ALU.add
                                  ).then_inc(lin_out, 1)

            def factor_low(it, k, ht):
                n = k * KT + ht
                dve.wait_ge(wh_hi_ready, after(it, k, KT, 2 + ht + 1))
                dve.tensor_tensor(wh_lo[:, ht], ps_wh[:, n % 2], wh_hi[:, ht].bitcast(F32), ALU.subtract
                                  ).then_inc(wh_lo_ready, 1)

            def masked_exp(it, k):
                s = k % STREAMS
                dve.wait_ge(u_psum, after(it, k, 1, 1))
                dve.tensor_tensor(uT2[:], ps_u[:], sides[s][:], ALU.mult).then_inc(uT2_done, 1)
                dve.wait_ge(uT2_done, after(it, k, 1, 1))
                dve.tensor_tensor(uT[:], uT2[:, :, 0, :], uT2[:, :, 1, :], ALU.add).then_inc(uT_ready, 1)
                dve.wait_ge(exp_done, after(it, k, 1, 1))
                dve.tensor_tensor(dT[:], prob[:], adjT[s][:], ALU.mult).then_inc(dT_ready, 1)
                dve.wait_ge(dT_ready, after(it, k, 1, 1))
                dve.wait_ge(dT_hi_ready, after(it, k, 1, 1))
                dve.tensor_tensor(dT_lo[:], dT[:], dT_hi[:].bitcast(F32), ALU.subtract).then_inc(dT_lo_ready, 1)

            pre_norm(0, 0)
            for i in range(LAYERS * 3):
                dve.wait_ge(w_hi_ready, i + 1)
                dve.tensor_tensor(w_lo[:, i].rearrange("p t n -> p (t n)"), w_raw[:, i % 3, :],
                                  w_hi[:, i].rearrange("p t n -> p (t n)").bitcast(F32), ALU.subtract
                                  ).then_inc(w_lo_ready, 1)
            dve.wait_ge(const_loaded, 16 * 6)
            make_sides(0, 0)
            dve.sem_inc(wh_lo_ready, 2)
            dve.sem_inc(lin_out, 1)
            for ht in range(LEAD):
                factor_low(0, 0, ht)
            with dve.Fori(0, iters) as it:
                for k in range(STEPS):
                    if k > 0:
                        inverse_sum(it, k - 1)
                        context_stats(it, k - 1)
                    if k == 0:
                        pre_norm(it, 1)
                    linear_bias(it, k, 0)
                    if k == 3:
                        residual(it, 2)
                        pre_norm(it, 2)
                    elif k > 0:
                        normalise(it, k - 1)
                    for ht in range(LEAD, KT):
                        factor_low(it, k, ht)
                    linear_bias(it, k, 1)
                    masked_exp(it, k)
                    if k == 0:
                        make_sides(it, 1)
                    if k == 3:
                        make_sides(it, 2)
                    for ht in range(LEAD):
                        factor_low(it, k + 1, ht)
                inverse_sum(it, 3)
                context_stats(it, 3)
                residual(it, 3)


def build(nc, x, adj, weights, rows, columns, consts, out):
    x1 = nc.dram_tensor("x1", x.shape, F32, kind="Internal").ap()
    network_one(nc, x, adj, weights, rows, columns, consts, x1)
    network_two(nc, x1, adj, weights, rows, columns, consts, out)


def arrange(inputs):
    import numpy as np

    a = {k: np.asarray(v) for k, v in inputs.items()}

    def tiles(w):
        return w.reshape(KT, P, w.shape[1]).transpose(1, 0, 2).reshape(P, KT * w.shape[1])

    weights = [tiles(a[n][l].T) for l in range(LAYERS) for n in ("L0_gnn_Wl", "L0_gnn_Wr", "L0_gnn_Ws")]
    for l in range(LAYERS):
        weights += [tiles(a["L1_gnn_W_left"][l]), tiles(a["L1_gnn_W_right"][l]), tiles(a["L1_gnn_W_lin"][l].T)]
    rows = [a[n][l] for l in range(LAYERS) for n in ("L0_gnn_bl", "L0_gnn_br", "L0_gnn_bs")]
    rows += [a["L0_gnn_ln_w"][1], a["L0_gnn_ln_b"][1], a["L1_gnn_b_lin"][0], a["L1_gnn_b_lin"][1],
             a["L1_gnn_ln_a"][1], a["L1_gnn_ln_b"][1]]
    columns = [a[n][0].reshape(KT, P).T for n in ("L0_gnn_ln_w", "L0_gnn_ln_b", "L1_gnn_ln_a", "L1_gnn_ln_b")]
    part, free = np.indices((P, S))
    masks = [part == free, part > free, part < free, free <= part, free > part]
    return {
        "x": np.ascontiguousarray(a["x"]),
        "adj": np.ascontiguousarray(a["adj"]),
        "weights": np.ascontiguousarray(np.stack(weights)),
        "rows": np.ascontiguousarray(np.stack(rows)),
        "columns": np.ascontiguousarray(np.concatenate(columns, axis=1)),
        "consts": np.ascontiguousarray(np.stack([m.astype(np.float32) for m in masks], axis=1)),
    }


def kernel(**inputs):
    import concourse.bacc as bacc
    from concourse.bass_utils import run_bass_kernel_spmd

    arrays = arrange(inputs)
    nc = bacc.Bacc("TRN2", target_bir_lowering=False, num_devices=1)
    args = [nc.dram_tensor(n, a.shape, mybir.dt.from_np(a.dtype), kind="ExternalInput").ap()
            for n, a in arrays.items()]
    out = nc.dram_tensor("out", arrays["x"].shape, F32, kind="ExternalOutput").ap()
    build(nc, *args, out)
    return run_bass_kernel_spmd(nc, [arrays], core_ids=[0]).results[0]["out"]
```

```python
from contextlib import ExitStack

import concourse.bass as bass
from concourse import mybir

P = 128
S = 128
D = 384
KT = D // P
G = 2
STREAMS = 2
LAYERS = 2
STEPS = STREAMS * LAYERS
GS = G * S
GD = G * D
SCALE = float(D) ** -0.5
PRE_EPS = 1e-5
CTX_EPS = 1e-12
SIGMA_EPS = 1e-3
LOWEST = -3.0e38
SUM_EPS = 1e-10

ALU = mybir.AluOpType
ACT = mybir.ActivationFunctionType
F32 = mybir.dt.float32
F32R = mybir.dt.float32r
AX_X = mybir.AxisListType.X

ROW_BIAS = 0
ROW_LN = 6
ROW_LIN = 8
ROW_LN2 = 10
ROWS = 12
LEFT, RIGHT, SELF = range(3)
C_IDENT, C_UPPER, C_LOWER, C_LEFT, C_RIGHT = range(5)


def after(it, k, per_step, n):
    return it * (STEPS * per_step) + (k * per_step + n)


def after_group(it, s, per_group, n):
    return it * (STREAMS * per_group) + (s * per_group + n)


def loads_until(it, s):
    return 16 * it + 16 * (s // STREAMS + 1)


def group_of(k):
    return k // STEPS * STREAMS + k % STREAMS


def high_pass(pe, out, pairs):
    for i, (a_hi, _, b_hi, _) in enumerate(pairs):
        pe.matmul(out, a_hi, b_hi, start=(i == 0), stop=False)


def low_high_pass(pe, out, pairs):
    for _, a_lo, b_hi, _ in pairs:
        pe.matmul(out, a_lo, b_hi, start=False, stop=False)


def high_low_pass(pe, out, pairs):
    for i, (a_hi, _, _, b_lo) in enumerate(pairs):
        last = pe.matmul(out, a_hi, b_lo, start=False, stop=(i == len(pairs) - 1))
    return last


def low_passes(pe, out, pairs):
    low_high_pass(pe, out, pairs)
    return high_low_pass(pe, out, pairs)


PROJECTIONS = [(0, LEFT), (0, RIGHT), (1, LEFT), (1, RIGHT), (0, SELF), (1, SELF)]


def network_one(nc, x, adj, weights, rows, columns, consts, x1, next_hi, next_lo):
    iters = x.shape[0] // (G * STREAMS)
    x_g = x.rearrange("(i b) p d -> i p b d", b=G)
    x1_g = x1.rearrange("(i b) p d -> i p b d", b=G)
    adj_g = adj.rearrange("(i b) p d -> i p b d", b=G)

    with ExitStack() as ctx:
        def sb(name, shape, dt=F32):
            return ctx.enter_context(nc.sbuf_tensor("n1_" + name, shape, dt))

        def ps(name, shape):
            return ctx.enter_context(nc.psum_tensor("n1_ps_" + name, shape, F32))

        def sem(name):
            return ctx.enter_context(nc.semaphore("n1_" + name))

        w_raw = sb("w_raw", [P, 3, KT * D])
        w_hi = sb("w_hi", [P, LAYERS * 3, KT, D], F32R)
        w_lo = sb("w_lo", [P, LAYERS * 3, KT, D], F32R)
        row = sb("row", [P, ROW_LIN, D])
        col = sb("col", [P, 4 * KT])
        const = sb("const", [P, 5, S])
        ident = const[:, C_IDENT, :]
        minus_half = sb("minus_half", [P, G])

        x_in = [sb(f"x_in{s}", [P, G, D]) for s in range(STREAMS)]
        x_res = [sb(f"x_res{s}", [P, G, D]) for s in range(STREAMS)]
        x_out = [sb(f"x_out{s}", [P, G, D]) for s in range(STREAMS)]
        adj_in = [sb(f"adj_in{s}", [P, G, S]) for s in range(STREAMS)]
        ctx_o = [sb(f"ctx_o{s}", [P, G, D]) for s in range(STREAMS)]
        x_mv = [sb(f"x_mv{s}", [P, G, 2]) for s in range(STREAMS)]
        x_rstd = [sb(f"x_rstd{s}", [P, G]) for s in range(STREAMS)]
        x_shift = [sb(f"x_shift{s}", [P, G]) for s in range(STREAMS)]
        hT_halves = [sb(f"hT_halves{s}", [P, KT, G, 2, S], F32R) for s in range(STREAMS)]

        x_o = sb("x_o", [P, G, D])
        hT = sb("hT", [P, KT, G, S])
        proj = sb("proj", [P, G, 2, D])
        proj_hi = sb("proj_hi", [P, G, 2, D], F32R)
        proj_lo = sb("proj_lo", [P, G, 2, D], F32R)
        own = sb("own", [P, G, D])
        u_cross = sb("u_cross", [P, G, S], F32R)
        u_low = sb("u_low", [P, G, S])
        ident_r = sb("ident_r", [P, S], F32R)
        u = sb("u", [P, G, S])
        prob = sb("prob", [P, G, S])
        delta = sb("delta", [P, G, S])
        delta_diag = sb("delta_diag", [P, G, S])
        aT = sb("aT", [P, G, 2, S])
        aT_hi = sb("aT_hi", [P, G, 2, S], F32R)
        aT_lo = sb("aT_lo", [P, G, 2, S], F32R)
        row_max = sb("row_max", [P, G])
        exp_bias = sb("exp_bias", [P, G])
        z_sum = sb("z_sum", [P, G])
        d_sum = sb("d_sum", [P, G])
        den = sb("den", [P, G])
        eps_den = sb("eps_den", [P, G])
        diag = sb("diag", [P, G])
        c_stats = sb("c_stats", [P, G, 6])
        c_mv = sb("c_mv", [P, G, 2])
        c_var = sb("c_var", [P, G])
        c_rstd = sb("c_rstd", [P, G])
        c_shift = sb("c_shift", [P, G])
        x_stats = sb("x_stats", [P, G, 6])
        x_var = sb("x_var", [P, G])

        ps_oT = ps("oT", [P, 1024])
        ps_u = ps("u", [P, G, 2, S])
        ps_w = ps("w", [P, 3, 512])
        ps_ctx = ps("ctx", [P, G, 512])
        ps_oT_tiles = ps_oT[:, 0:KT * GS].rearrange("p (t b n) -> p t b n", t=KT, b=G)
        ps_aT = ps_ctx[:, :, D:D + S]

        ident_loaded, rows_loaded = sem("ident_loaded"), sem("rows_loaded")
        w_loaded = [sem(f"w_loaded{i}") for i in range(9)]
        x_loaded = [sem(f"x_loaded{s}") for s in range(STREAMS)]
        adj_loaded = [sem(f"adj_loaded{s}") for s in range(STREAMS)]
        x1_stored = [sem(f"x1_stored{s}") for s in range(STREAMS)]
        w_hi_ready, w_lo_ready = sem("w_hi_ready"), sem("w_lo_ready")
        half_ready = sem("half_ready")
        o_ready, oT_psum, hT_ready = sem("o_ready"), sem("oT_psum"), sem("hT_ready")
        hT_hi_ready, hT_lo_ready = sem("hT_hi_ready"), sem("hT_lo_ready")
        u_cross_ready, mirror_psum, ident_r_ready = sem("u_cross_ready"), sem("mirror_psum"), sem("ident_r_ready")
        u_low_done = sem("u_low_done")
        u_psum, max_done, exp_bias_ready = sem("u_psum"), sem("max_done"), sem("exp_bias_ready")
        exp_done, delta_done, den_done = sem("exp_done"), sem("delta_done"), sem("den_done")
        eps_den_done, diag_done = sem("eps_den_done"), sem("diag_done")
        aT_psum, aT_ready = sem("aT_psum"), sem("aT_ready")
        aT_hi_ready, aT_lo_ready = sem("aT_hi_ready"), sem("aT_lo_ready")
        proj_psum, proj_out = sem("proj_psum"), sem("proj_out")
        proj_hi_ready, proj_lo_ready = sem("proj_hi_ready"), sem("proj_lo_ready")
        ctx_psum, ctx_done, c_stats_done = sem("ctx_psum"), sem("ctx_done"), sem("c_stats_done")
        c_mv_done, c_var_ready, c_rstd_ready = sem("c_mv_done"), sem("c_var_ready"), sem("c_rstd_ready")
        c_shift_ready, res_o_ready = sem("c_shift_ready"), sem("res_o_ready")
        x_stats_done, x_mv_done, x_var_ready = sem("x_stats_done"), sem("x_mv_done"), sem("x_var_ready")
        x_rstd_ready, x_shift_ready, x_res_ready = sem("x_rstd_ready"), sem("x_shift_ready"), sem("x_res_ready")
        scaled_ready, shifted_done, x1_ready = sem("scaled_ready"), sem("shifted_done"), sem("x1_ready")
        wait_carried = sem("wait_carried")


        block = ctx.enter_context(nc.Block())

        @block.sync
        def _(sp):
            def load_x(i, s):
                sp.dma_start(x_in[s][:], x_g[bass.ds(i * STREAMS + s, 1)].rearrange("a p b d -> (a p) b d")
                             ).then_inc(x_loaded[s], 16)

            def load_adj(i, s):
                sp.dma_start(adj_in[s][:], adj_g[bass.ds(i * STREAMS + s, 1)].rearrange("a p b d -> (a p) b d")
                             ).then_inc(adj_loaded[s], 16)

            def store_x1(i, s):
                sp.dma_start(x1_g[bass.ds(i * STREAMS + s, 1)].rearrange("a p b d -> (a p) b d"),
                             x_out[s][:]).then_inc(x1_stored[s], 16)

            load_x(0, 0)
            sp.dma_start(const[:], consts).then_inc(ident_loaded, 16)
            for i in range(3):
                sp.dma_start(w_raw[:, i, :], weights[i]).then_inc(w_loaded[i], 16)
            load_adj(0, 0)
            load_x(0, 1)
            sp.dma_start(col[:], columns).then_inc(rows_loaded, 16)
            for r in range(ROW_LIN):
                sp.dma_start(row[:, r, :], rows[r:r + 1, :].partition_broadcast(P)).then_inc(rows_loaded, 16)
            load_adj(0, 1)
            for i in range(3, 9):
                sp.wait_ge(w_hi_ready, i - 2)
                sp.wait_ge(w_lo_ready, i - 2)
                sp.dma_start(w_raw[:, i % 3, :], weights[i]).then_inc(w_loaded[i], 16)
            for s in range(STREAMS):
                sp.sem_inc(x1_stored[s], 16)

            with sp.Fori(0, iters - 1) as it:
                a_normed, a_kept, b_normed, b_kept, a_adj_used, a_summed, b_adj_used, b_summed = (
                    sp.to_reg(v) for v in (
                        after(it, 0, 1, 1), after_group(it, 0, 1, 1),
                        after(it, 1, 1, 1), after_group(it, 1, 1, 1),
                        after(it, 2, G, G), after_group(it, 0, G, G),
                        after(it, 3, G, G), after_group(it, 1, G, G)))
                sp.wait_ge(o_ready, a_normed)
                sp.wait_ge(x_res_ready, a_kept)
                load_x(it + 1, 0)
                sp.wait_ge(o_ready, b_normed)
                sp.wait_ge(x_res_ready, b_kept)
                load_x(it + 1, 1)
                sp.wait_ge(delta_done, a_adj_used)
                load_adj(it + 1, 0)
                sp.wait_ge(x1_ready, a_summed)
                store_x1(it, 0)
                sp.wait_ge(delta_done, b_adj_used)
                load_adj(it + 1, 1)
                sp.wait_ge(x1_ready, b_summed)
                store_x1(it, 1)
            for s in range(STREAMS):
                sp.wait_ge(x1_ready, after_group(iters - 1, s, G, G))
                store_x1(iters - 1, s)
            for s in range(STREAMS):
                sp.wait_ge(x1_stored[s], 16 * (iters + 1))

        @block.tensor
        def _(pe):
            def halves(s, b):
                return [(hT_halves[s][:, kt, b, 0, :], hT_halves[s][:, kt, b, 1, :]) for kt in range(KT)]

            def transpose_o(it, k, first=False):
                o = x_o if k % STEPS < STREAMS else ctx_o[k % STREAMS]
                pe.wait_ge(o_ready, after(it, k, 1, 1))
                if not first:
                    pe.wait_ge(hT_lo_ready, after(it, k, 1, 0))
                for kt in range(KT):
                    for b in range(G):
                        last = pe.transpose(ps_oT[:, kt * GS + b * S:kt * GS + (b + 1) * S],
                                            o[:, b, kt * P:(kt + 1) * P], ident)
                last.then_inc(oT_psum, 1)

            def scores(it, k):
                s = k % STREAMS
                pe.wait_ge(hT_hi_ready, after(it, k, 1, 1))
                pe.wait_ge(hT_lo_ready, after(it, k, 1, 1))
                for b in range(G):
                    for kt, (hi, _) in enumerate(halves(s, b)):
                        last = pe.matmul(ps_u[:, b], hi, hT_halves[s][:, kt, b], start=(kt == 0), stop=(kt == KT - 1))
                last.then_inc(u_psum, 1)

            def mirror_cross(it, k, first=False):
                pe.wait_ge(u_cross_ready, after(it, k, 1, 1))
                if not first:
                    pe.wait_ge(ctx_done, after(it, k, G, 0))
                for b in range(G):
                    last = pe.matmul(ps_ctx[:, b, D:D + S], u_cross[:, b, :], ident_r[:], start=True, stop=True)
                last.then_inc(mirror_psum, 1)

            def project(it, k, n):
                b, m = PROJECTIONS[n]
                pe.wait_ge(proj_out, after(it, k, 6, n + 1))
                w = (k % STEPS // STREAMS) * 3 + m
                pairs = [(*h, w_hi[:, w, kt, :], w_lo[:, w, kt, :]) for kt, h in enumerate(halves(k % STREAMS, b))]
                high_pass(pe, ps_w[:, n % 3, 0:D], pairs)
                low_passes(pe, ps_w[:, n % 3, 0:D], pairs).then_inc(proj_psum, 1)

            def transpose_attn(it, k):
                pe.wait_ge(delta_done, after(it, k, G, G))
                for b in range(G):
                    last = pe.transpose(ps_ctx[:, b, D:D + S], delta[:, b, :], ident)
                last.then_inc(aT_psum, 1)

            def context(it, k, b):
                pairs = [(aT_hi[:, b, m, :], aT_lo[:, b, m, :], proj_hi[:, b, m, :], proj_lo[:, b, m, :])
                         for m in range(2)]
                pe.wait_ge(aT_hi_ready, after(it, k, 1, 1))
                pe.wait_ge(proj_hi_ready, after(it, k, 2 * G, 2 * b + 2))
                high_pass(pe, ps_ctx[:, b, 0:D], pairs)
                pe.wait_ge(aT_lo_ready, after(it, k, 1, 1))
                pe.wait_ge(proj_lo_ready, after(it, k, 2 * G, 2 * b + 2))
                low_passes(pe, ps_ctx[:, b, 0:D], pairs).then_inc(ctx_psum, 1)

            def step(it, k, first=False, final=False):
                last = final and k == 3
                project(it, k, 0)
                mirror_cross(it, k, first)
                for n in range(1, 4):
                    project(it, k, n)
                if not last:
                    transpose_o(it, k + 1)
                transpose_attn(it, k)
                project(it, k, 4)
                project(it, k, 5)
                context(it, k, 0)
                context(it, k, 1)
                if not last:
                    scores(it, k + 1)

            pe.wait_ge(ident_loaded, 16)
            transpose_o(0, 0, first=True)
            scores(0, 0)
            pe.wait_ge(w_hi_ready, 3)
            pe.wait_ge(w_lo_ready, 3)
            pe.wait_ge(ident_r_ready, 1)
            step(0, 0, first=True)
            pe.wait_ge(w_hi_ready, 6)
            pe.wait_ge(w_lo_ready, 6)
            with pe.Fori(0, iters - 1) as it:
                for k in (1, 2, 3, 4):
                    step(it, k)
            for k in (1, 2, 3):
                step(iters - 1, k, final=True)

        @block.scalar
        def _(act):
            def x_normalise(it, s):
                t = s % STREAMS
                act.wait_ge(x_shift_ready, after_group(it, s, 1, 1))
                for b in range(G):
                    last = act.activation(x_o[:, b, :], x_in[t][:, b, :], ACT.Identity,
                                          bias=x_shift[t][:, b:b + 1], scale=x_rstd[t][:, b:b + 1])
                last.then_inc(o_ready, 1)

            def c_normalise(it, k):
                s, done = k % STREAMS, (o_ready if k % STEPS < STREAMS else res_o_ready)
                act.wait_ge(c_shift_ready, after(it, k, 1, 1))
                for b in range(G):
                    last = act.activation(ctx_o[s][:, b, :], ctx_o[s][:, b, :], ACT.Identity,
                                          bias=c_shift[:, b:b + 1], scale=c_rstd[:, b:b + 1])
                last.then_inc(done, 1)

            def relu_hT(it, k):
                act.wait_ge(oT_psum, after(it, k, 1, 1))
                if k % STEPS < STREAMS:
                    act.activation(hT_halves[k % STREAMS][:, :, :, 0, :], ps_oT_tiles, ACT.Relu).then_inc(hT_hi_ready, 1)
                else:
                    for kt in range(KT):
                        last = act.activation(hT[:, kt], ps_oT_tiles[:, kt], ACT.Relu,
                                              bias=col[:, KT + kt:KT + kt + 1], scale=col[:, kt:kt + 1])
                    last.then_inc(hT_ready, 1)

            def high_hT(it, k):
                act.wait_ge(hT_ready, after_group(it, k - STREAMS, 1, 1))
                act.activation(hT_halves[k % STREAMS][:, :, :, 0, :], hT[:], ACT.Copy).then_inc(hT_hi_ready, 1)

            def copy_cross(it, k):
                act.wait_ge(u_psum, after(it, k, 1, 1))
                act.activation(u_cross[:], ps_u[:, :, 1, :], ACT.Copy).then_inc(u_cross_ready, 1)

            def keep_x(it, s):
                act.wait_ge(x_loaded[s % STREAMS], loads_until(it, s))
                act.activation(x_res[s % STREAMS][:], x_in[s % STREAMS][:], ACT.Copy).then_inc(x_res_ready, 1)

            def proj_high(it, k, b, m):
                act.wait_ge(proj_out, after(it, k, 6, 3 + PROJECTIONS.index((b, m)) + 1))
                act.activation(proj_hi[:, b, m], proj[:, b, m], ACT.Copy).then_inc(proj_hi_ready, 1)

            def weights_high(i):
                act.wait_ge(w_loaded[i], 16)
                out = w_hi[:, i] if i < 6 else next_hi[:, i - 6]
                act.activation(out.rearrange("p t n -> p (t n)"), w_raw[:, i % 3, :], ACT.Copy
                               ).then_inc(w_hi_ready, 1)

            def exponential(it, k):
                act.wait_ge(exp_bias_ready, after(it, k, 1, 1))
                for b in range(G):
                    act.activation(prob[:, b, :], u[:, b, :], ACT.Exp,
                                   bias=exp_bias[:, b:b + 1], scale=SCALE,
                                   accum_out=z_sum[:, b:b + 1]).then_inc(exp_done, 1)

            def step(it, k, final=False):
                last = final and k == 3
                exponential(it, k)
                proj_high(it, k, 0, LEFT)
                proj_high(it, k, 0, RIGHT)
                proj_high(it, k, 1, LEFT)
                if not last:
                    relu_hT(it, k + 1)
                proj_high(it, k, 1, RIGHT)
                act.wait_ge(aT_ready, after(it, k, 1, 1))
                act.activation(aT_hi[:], aT[:], ACT.Copy).then_inc(aT_hi_ready, 1)
                if not last and (k + 1) % STEPS >= STREAMS:
                    high_hT(it, k + 1)
                if k in (2, 3) and not final:
                    x_normalise(it, k)
                if not last:
                    copy_cross(it, k + 1)
                c_normalise(it, k)
                if k == 3 and not final:
                    act.wait_ge(x1_ready, after_group(it, 0, G, G))
                    keep_x(it, 2)
                if k == 4:
                    act.wait_ge(x1_ready, after_group(it, 1, G, G))
                    keep_x(it, 3)

            for i in range(3):
                weights_high(i)
                if i == 1:
                    x_normalise(0, 0)
            relu_hT(0, 0)
            act.activation(ident_r[:], ident, ACT.Copy).then_inc(ident_r_ready, 1)
            copy_cross(0, 0)
            x_normalise(0, 1)
            keep_x(0, 0)
            keep_x(0, 1)
            for i in range(3, 6):
                weights_high(i)
            act.wait_ge(rows_loaded, 16 * (1 + ROW_LIN))
            step(0, 0)
            with act.Fori(0, iters - 1) as it:
                for k in (1, 2, 3, 4):
                    step(it, k)
            for k in (1, 2, 3):
                step(iters - 1, k, final=True)
                weights_high(5 + k)

        @block.gpsimd
        def _(pool):
            def proj_low(it, k, b, m):
                pool.wait_ge(proj_hi_ready, after(it, k, 2 * G, 2 * b + m + 1))
                pool.tensor_tensor(proj_lo[:, b, m], proj[:, b, m], proj_hi[:, b, m].bitcast(F32),
                                   ALU.subtract).then_inc(proj_lo_ready, 1)

            def x_power(it, s):
                pool.wait_ge(x_var_ready, after_group(it, s, 1, 1))
                pool.tensor_tensor(x_rstd[s % STREAMS][:], x_var[:], minus_half[:], ALU.pow).then_inc(x_rstd_ready, 1)

            def c_power(it, k):
                pool.wait_ge(c_var_ready, after(it, k, 1, 1))
                pool.tensor_tensor(c_rstd[:], c_var[:], minus_half[:], ALU.pow).then_inc(c_rstd_ready, 1)

            def res_scale(it, k):
                s = k % STREAMS
                pool.wait_ge(res_o_ready, after_group(it, s, 1, 1))
                pool.wait_ge(x1_stored[s], 16 * it + 16)
                for b in range(G):
                    pool.tensor_tensor(x_out[s][:, b, :], ctx_o[s][:, b, :], row[:, ROW_LN, :], ALU.mult
                                       ).then_inc(scaled_ready, 1)

            def res_shift(it, k):
                s = k % STREAMS
                for b in range(G):
                    pool.wait_ge(scaled_ready, after_group(it, s, G, b + 1))
                    pool.tensor_tensor(x_out[s][:, b, :], x_out[s][:, b, :], row[:, ROW_LN + 1, :], ALU.add
                                       ).then_inc(shifted_done, 1)

            def weights_low(i):
                pool.wait_ge(w_hi_ready, i + 1)
                pool.tensor_tensor(next_lo[:, i - 6].rearrange("p t n -> p (t n)"), w_raw[:, i % 3, :],
                                   next_hi[:, i - 6].rearrange("p t n -> p (t n)").bitcast(F32), ALU.subtract
                                   ).then_inc(w_lo_ready, 1)

            def step(it, k, final=False):
                proj_low(it, k, 0, LEFT)
                proj_low(it, k, 0, RIGHT)
                proj_low(it, k, 1, LEFT)
                proj_low(it, k, 1, RIGHT)
                if k in (1, 2) and not final:
                    x_power(it, k + 1)
                if k in (3, 4):
                    res_scale(it, k - 1)
                    res_shift(it, k - 1)
                c_power(it, k)

            pool.memset(minus_half[:], -0.5).then_inc(half_ready, 1)
            pool.wait_ge(half_ready, 1)
            x_power(0, 0)
            x_power(0, 1)
            pool.wait_ge(rows_loaded, 16 * (1 + ROW_LIN))
            step(0, 0)
            with pool.Fori(0, iters - 1) as it:
                for k in (1, 2, 3, 4):
                    step(it, k)
            for k in (1, 2, 3):
                step(iters - 1, k, final=True)
                weights_low(5 + k)
            res_scale(iters - 1, 3)
            res_shift(iters - 1, 3)

        @block.vector
        def _(dve):
            def carried_wait(sem_of_producer, value):
                dve.wait_ge(sem_of_producer, value)
                dve.sem_inc(wait_carried, 1)

            def shift_of(out, mv, rstd):
                return dve.scalar_tensor_tensor(out=out[:], in0=mv[:, :, 0], scalar=-1.0, in1=rstd[:],
                                                op0=ALU.mult, op1=ALU.mult)

            def x_stats_of(it, s):
                t = s % STREAMS
                dve.wait_ge(x_loaded[t], loads_until(it, s))
                for b in range(G):
                    dve.bn_stats(x_stats[:, b, :], x_in[t][:, b, :]).then_inc(x_stats_done, 1)
                carried_wait(x_stats_done, after_group(it, s, G, G))
                for b in range(G):
                    dve.bn_aggr(x_mv[t][:, b, :], x_stats[:, b, :]).then_inc(x_mv_done, 1)
                dve.wait_ge(x_mv_done, after_group(it, s, G, G))
                dve.tensor_scalar(x_var[:], x_mv[t][:, :, 1], PRE_EPS, None, ALU.add).then_inc(x_var_ready, 1)

            def x_shift_of(it, s):
                dve.wait_ge(x_rstd_ready, after_group(it, s, 1, 1))
                shift_of(x_shift[s % STREAMS], x_mv[s % STREAMS], x_rstd[s % STREAMS]).then_inc(x_shift_ready, 1)

            def context_sum(it, k, b):
                s = k % STREAMS
                dve.wait_ge(ctx_psum, after(it, k, G, b + 1))
                dve.wait_ge(diag_done, after(it, k, G, b + 1))
                dve.wait_ge(proj_out, after(it, k, 6, 3 + PROJECTIONS.index((b, SELF)) + 1))
                dve.scalar_tensor_tensor(out=ctx_o[s][:, b, :], in0=own[:, b, :], scalar=diag[:, b:b + 1],
                                         in1=ps_ctx[:, b, 0:D], op0=ALU.mult, op1=ALU.add
                                         ).then_inc(ctx_done, 1)
                dve.wait_ge(ctx_done, after(it, k, G, b + 1))
                dve.bn_stats(c_stats[:, b, :], ctx_o[s][:, b, :]).then_inc(c_stats_done, 1)

            def context_var(it, k):
                carried_wait(c_stats_done, after(it, k, G, G))
                for b in range(G):
                    dve.bn_aggr(c_mv[:, b, :], c_stats[:, b, :]).then_inc(c_mv_done, 1)
                dve.wait_ge(c_mv_done, after(it, k, G, G))
                dve.wait_ge(eps_den_done, after(it, k, 1, 1))
                dve.tensor_tensor(c_var[:], c_mv[:, :, 1], eps_den[:], ALU.add).then_inc(c_var_ready, 1)

            def context_shift(it, k):
                dve.wait_ge(c_rstd_ready, after(it, k, 1, 1))
                shift_of(c_shift, c_mv, c_rstd).then_inc(c_shift_ready, 1)

            def residual(it, k, b):
                s = k % STREAMS
                dve.wait_ge(x_res_ready, after_group(it, s, 1, 1))
                dve.wait_ge(shifted_done, after_group(it, s, G, b + 1))
                dve.scalar_tensor_tensor(out=x_out[s][:, b, :], in0=x_out[s][:, b, :], scalar=0.0,
                                         in1=x_res[s][:, b, :], op0=ALU.max, op1=ALU.add
                                         ).then_inc(x1_ready, 1)

            def hT_low(it, k):
                t = k % STREAMS
                hi, lo = hT_halves[t][:, :, :, 0, :].bitcast(F32), hT_halves[t][:, :, :, 1, :]
                dve.wait_ge(hT_hi_ready, after(it, k, 1, 1))
                if k % STEPS < STREAMS:
                    last = dve.scalar_tensor_tensor(out=lo, in0=ps_oT_tiles, scalar=0.0, in1=hi,
                                                    op0=ALU.max, op1=ALU.subtract)
                else:
                    dve.wait_ge(hT_ready, after_group(it, k - STREAMS, 1, 1))
                    last = dve.tensor_tensor(lo, hT[:], hi, ALU.subtract)
                last.then_inc(hT_lo_ready, 1)

            def score_max(it, k):
                dve.wait_ge(mirror_psum, after(it, k, 1, 1))
                dve.tensor_tensor(u_low[:], ps_aT, u_cross[:].bitcast(F32), ALU.add).then_inc(u_low_done, 1)
                carried_wait(u_low_done, after(it, k, 1, 1))
                for b in range(G):
                    dve.tensor_tensor_reduce(u[:, b, :], ps_u[:, b, 0, :], u_low[:, b, :], 1.0, LOWEST,
                                             ALU.add, ALU.max, row_max[:, b:b + 1]).then_inc(max_done, 1)
                dve.wait_ge(max_done, after(it, k, G, G))
                dve.tensor_scalar(exp_bias[:], row_max[:], -SCALE, None, ALU.mult).then_inc(exp_bias_ready, 1)

            def attention(it, k):
                s = k % STREAMS
                dve.wait_ge(adj_loaded[s], loads_until(it, group_of(k)))
                for b in range(G):
                    dve.wait_ge(exp_done, after(it, k, G, b + 1))
                    dve.tensor_tensor_reduce(delta[:, b, :], prob[:, b, :], adj_in[s][:, b, :], 1.0, 0.0,
                                             ALU.mult, ALU.add, d_sum[:, b:b + 1]).then_inc(delta_done, 1)

            def denominator(it, k):
                dve.wait_ge(delta_done, after(it, k, G, G))
                dve.scalar_tensor_tensor(out=den[:], in0=z_sum[:], scalar=SUM_EPS, in1=d_sum[:],
                                         op0=ALU.mult, op1=ALU.add).then_inc(den_done, 1)

            def delta_diagonal(it, k):
                for b in range(G):
                    dve.wait_ge(delta_done, after(it, k, G, b + 1))
                    dve.tensor_tensor_reduce(delta_diag[:, b, :], delta[:, b, :], ident, 1.0, 0.0,
                                             ALU.mult, ALU.add, diag[:, b:b + 1]).then_inc(diag_done, 1)

            def epsilon_of_den(it, k):
                dve.wait_ge(den_done, after(it, k, 1, 1))
                dve.scalar_tensor_tensor(out=eps_den[:], in0=den[:], scalar=CTX_EPS, in1=den[:],
                                         op0=ALU.mult, op1=ALU.mult).then_inc(eps_den_done, 1)

            def proj_bias(it, k, n):
                b, m = PROJECTIONS[n]
                dve.wait_ge(proj_psum, after(it, k, 6, n + 1))
                out = own[:, b, :] if m == SELF else proj[:, b, m, :]
                dve.tensor_tensor(out, ps_w[:, n % 3, 0:D], row[:, ROW_BIAS + (k % STEPS // STREAMS) * 3 + m, :],
                                  ALU.add).then_inc(proj_out, 1)

            def mask_attn(it, k):
                dve.wait_ge(aT_psum, after(it, k, 1, 1))
                a = ps_aT[:].unsqueeze(2).to_broadcast([P, G, 2, S])
                mask = const[:, C_UPPER:C_UPPER + 2, :].unsqueeze(1).to_broadcast([P, G, 2, S])
                dve.tensor_tensor(aT[:], a, mask, ALU.mult).then_inc(aT_ready, 1)

            def attn_low(it, k):
                dve.wait_ge(aT_ready, after(it, k, 1, 1))
                dve.wait_ge(aT_hi_ready, after(it, k, 1, 1))
                dve.tensor_tensor(aT_lo[:], aT[:], aT_hi[:].bitcast(F32), ALU.subtract).then_inc(aT_lo_ready, 1)

            def step(it, k, final=False):
                last = final and k == 3
                proj_bias(it, k, 0)
                score_max(it, k)
                proj_bias(it, k, 1)
                attention(it, k)
                proj_bias(it, k, 2)
                denominator(it, k)
                delta_diagonal(it, k)
                epsilon_of_den(it, k)
                proj_bias(it, k, 3)
                mask_attn(it, k)
                if k in (1, 2) and not final:
                    x_stats_of(it, k + 1)
                attn_low(it, k)
                if not last:
                    hT_low(it, k + 1)
                proj_bias(it, k, 4)
                proj_bias(it, k, 5)
                if k in (1, 2) and not final:
                    x_shift_of(it, k + 1)
                for b in range(G):
                    context_sum(it, k, b)
                context_var(it, k)
                if k in (3, 4):
                    residual(it, k - 1, 0)
                context_shift(it, k)
                if k in (3, 4):
                    residual(it, k - 1, 1)

            def weights_low(i):
                dve.wait_ge(w_hi_ready, i + 1)
                dve.tensor_tensor(w_lo[:, i].rearrange("p t n -> p (t n)"), w_raw[:, i % 3, :],
                                  w_hi[:, i].rearrange("p t n -> p (t n)").bitcast(F32), ALU.subtract
                                  ).then_inc(w_lo_ready, 1)

            dve.sem_inc(proj_out, 3)
            for s in range(STREAMS):
                x_stats_of(0, s)
                x_shift_of(0, s)
            hT_low(0, 0)
            for i in range(6):
                weights_low(i)
            dve.wait_ge(rows_loaded, 16 * (1 + ROW_LIN))
            step(0, 0)
            with dve.Fori(0, iters - 1) as it:
                for k in (1, 2, 3, 4):
                    step(it, k)
            for k in (1, 2, 3):
                step(iters - 1, k, final=True)
            for b in range(G):
                residual(iters - 1, 3, b)


def network_two(nc, x1, adj, weights, rows, columns, consts, out, first_hi, first_lo):
    iters = x1.shape[0] // (G * STREAMS)
    x_g = x1.rearrange("(i b) p d -> i p b d", b=G)
    out_g = out.rearrange("(i b) p d -> i p b d", b=G)
    adj_g = adj.rearrange("(i b) p d -> i p b d", b=G)
    ONE = D

    with ExitStack() as ctx:
        def sb(name, shape, dt=F32):
            return ctx.enter_context(nc.sbuf_tensor("n2_" + name, shape, dt))

        def ps(name, shape):
            return ctx.enter_context(nc.psum_tensor("n2_ps_" + name, shape, F32))

        def sem(name):
            return ctx.enter_context(nc.semaphore("n2_" + name))

        w_raw = sb("w_raw", [P, 3, KT * D])
        second_hi = sb("second_hi", [P, 3, KT, D], F32R)
        second_lo = sb("second_lo", [P, 3, KT, D], F32R)
        w_hi, w_lo = [first_hi, second_hi], [first_lo, second_lo]
        row = sb("row", [P, 4, D])
        col = sb("col", [P, 4 * KT])
        const = sb("const", [P, 5, S])
        ident = const[:, C_IDENT, :]
        minus_half = sb("minus_half", [P, G])
        half = sb("half", [P, G])

        x_in = [sb(f"x_in{s}", [P, G, D]) for s in range(STREAMS)]
        x_res = [sb(f"x_res{s}", [P, G, D]) for s in range(STREAMS)]
        x_out = [sb(f"x_out{s}", [P, G, D]) for s in range(STREAMS)]
        adj_in = [sb(f"adj_in{s}", [P, G, S]) for s in range(STREAMS)]
        adjT = [sb(f"adjT{s}", [P, G, S]) for s in range(STREAMS)]
        sides = [sb(f"sides{s}", [P, G, 2, S]) for s in range(STREAMS)]
        ctx_o = [sb(f"ctx_o{s}", [P, G, D]) for s in range(STREAMS)]
        hT_hi = [sb(f"hT_hi{s}", [P, KT, GS], F32R) for s in range(STREAMS)]
        hT_lo = [sb(f"hT_lo{s}", [P, KT, GS], F32R) for s in range(STREAMS)]

        x_mv = [sb(f"x_mv{s}", [P, G, 2]) for s in range(STREAMS)]
        x_rstd = [sb(f"x_rstd{s}", [P, G]) for s in range(STREAMS)]
        x_shift = [sb(f"x_shift{s}", [P, G]) for s in range(STREAMS)]

        x_o = sb("x_o", [P, G, D])
        hT = sb("hT", [P, KT, GS])
        wh_hi = sb("wh_hi", [P, KT, 2, GS], F32R)
        wh_lo = sb("wh_lo", [P, KT, 2, GS], F32R)
        lin = sb("lin", [P, G, D])
        lin_hi = sb("lin_hi", [P, G, D + 2], F32R)
        lin_lo = sb("lin_lo", [P, G, D + 2], F32R)
        uT2 = sb("uT2", [P, G, 2, S])
        uT = sb("uT", [P, G, S])
        prob = sb("prob", [P, G, S])
        dT = sb("dT", [P, G, S])
        dT_hi = sb("dT_hi", [P, G, S], F32R)
        dT_lo = sb("dT_lo", [P, G, S], F32R)
        den = sb("den", [P, G])
        inv_den = sb("inv_den", [P, G])
        c_stats = sb("c_stats", [P, G, 6])
        c_mv = sb("c_mv", [P, G, 2])
        c_var = sb("c_var", [P, G])
        c_sigma = sb("c_sigma", [P, G])
        c_sigma_eps = sb("c_sigma_eps", [P, G])
        c_rstd = sb("c_rstd", [P, G])
        c_shift = sb("c_shift", [P, G])
        x_stats = sb("x_stats", [P, G, 6])
        x_var = sb("x_var", [P, G])

        ps_oT = ps("oT", [P, 1024])
        ADJ = KT * GS
        ps_wh = ps("wh", [P, 2, 2, GS])
        ps_lin = ps("lin", [P, 512])
        ps_u = ps("u", [P, G, 2, S])
        ps_ctx = ps("ctx", [P, G, 512])

        ident_loaded, rows_loaded = sem("ident_loaded"), sem("rows_loaded")
        w_loaded = [sem(f"w_loaded{i}") for i in range(3)]
        x_loaded = [sem(f"x_loaded{s}") for s in range(STREAMS)]
        adj_loaded = [sem(f"adj_loaded{s}") for s in range(STREAMS)]
        out_stored = [sem(f"out_stored{s}") for s in range(STREAMS)]
        w_hi_ready, w_lo_ready = sem("w_hi_ready"), sem("w_lo_ready")
        half_ready, ones_ready = sem("half_ready"), sem("ones_ready")
        o_ready, oT_psum, hT_ready = sem("o_ready"), sem("oT_psum"), sem("hT_ready")
        hT_hi_ready, hT_lo_ready = sem("hT_hi_ready"), sem("hT_lo_ready")
        adjT_ready, sides_done = sem("adjT_ready"), sem("sides_done")
        wh_psum, wh_hi_ready, wh_lo_ready = sem("wh_psum"), sem("wh_hi_ready"), sem("wh_lo_ready")
        lin_psum, lin_out = sem("lin_psum"), sem("lin_out")
        lin_hi_ready = sem("lin_hi_ready")
        lin_lo_ready = [sem(f"lin_lo_ready{b}") for b in range(G)]
        u_psum, uT2_done, uT_ready = sem("u_psum"), sem("uT2_done"), sem("uT_ready")
        exp_done, dT_ready = sem("exp_done"), sem("dT_ready")
        dT_hi_ready, dT_lo_ready = sem("dT_hi_ready"), sem("dT_lo_ready")
        ctx_psum, den_done, inv_den_ready = sem("ctx_psum"), sem("den_done"), sem("inv_den_ready")
        ctx_done, c_stats_done, c_mv_done = sem("ctx_done"), sem("c_stats_done"), sem("c_mv_done")
        c_var_ready, c_sigma_ready = sem("c_var_ready"), sem("c_sigma_ready")
        c_sigma_eps_done, c_rstd_done = sem("c_sigma_eps_done"), sem("c_rstd_done")
        c_shift_ready, res_o_ready = sem("c_shift_ready"), sem("res_o_ready")
        x_stats_done, x_mv_done, x_var_ready = sem("x_stats_done"), sem("x_mv_done"), sem("x_var_ready")
        x_rstd_ready, x_shift_ready, x_res_ready = sem("x_rstd_ready"), sem("x_shift_ready"), sem("x_res_ready")
        scaled_ready, shifted_done, sum_ready = sem("scaled_ready"), sem("shifted_done"), sem("sum_ready")
        wait_carried = sem("wait_carried")


        block = ctx.enter_context(nc.Block())

        @block.sync
        def _(sp):
            def load_x(i, s):
                sp.dma_start(x_in[s][:], x_g[bass.ds(i * STREAMS + s, 1)].rearrange("a p b d -> (a p) b d")
                             ).then_inc(x_loaded[s], 16)

            def load_adj(i, s):
                sp.dma_start(adj_in[s][:], adj_g[bass.ds(i * STREAMS + s, 1)].rearrange("a p b d -> (a p) b d")
                             ).then_inc(adj_loaded[s], 16)

            def store_out(i, s):
                sp.dma_start(out_g[bass.ds(i * STREAMS + s, 1)].rearrange("a p b d -> (a p) b d"),
                             x_out[s][:]).then_inc(out_stored[s], 16)

            load_x(0, 0)
            load_adj(0, 0)
            sp.dma_start(const[:], consts).then_inc(ident_loaded, 16)
            load_x(0, 1)
            sp.dma_start(col[:], columns).then_inc(rows_loaded, 16)
            for r in range(4):
                sp.dma_start(row[:, r, :], rows[ROW_LIN + r:ROW_LIN + r + 1, :].partition_broadcast(P)
                             ).then_inc(rows_loaded, 16)
            load_adj(0, 1)
            for i in range(3):
                sp.dma_start(w_raw[:, i, :], weights[9 + i]).then_inc(w_loaded[i], 16)
            for s in range(STREAMS):
                sp.sem_inc(out_stored[s], 16)

            with sp.Fori(0, iters - 1) as it:
                a_normed, a_kept, a_adj_used, b_normed, b_kept, b_adj_used, a_summed, b_summed = (
                    sp.to_reg(v) for v in (
                        after(it, 0, 1, 1), after_group(it, 0, 1, 1), after_group(it, 0, 2, 2),
                        after(it, 1, 1, 1), after_group(it, 1, 1, 1), after_group(it, 1, 2, 2),
                        after_group(it, 0, G, G), after_group(it, 1, G, G)))
                sp.wait_ge(o_ready, a_normed)
                sp.wait_ge(x_res_ready, a_kept)
                load_x(it + 1, 0)
                sp.wait_ge(sides_done, a_adj_used)
                load_adj(it + 1, 0)
                sp.wait_ge(o_ready, b_normed)
                sp.wait_ge(x_res_ready, b_kept)
                load_x(it + 1, 1)
                sp.wait_ge(sides_done, b_adj_used)
                load_adj(it + 1, 1)
                sp.wait_ge(sum_ready, a_summed)
                store_out(it, 0)
                sp.wait_ge(sum_ready, b_summed)
                store_out(it, 1)
            for s in range(STREAMS):
                sp.wait_ge(sum_ready, after_group(iters - 1, s, G, G))
                store_out(iters - 1, s)
            for s in range(STREAMS):
                sp.wait_ge(out_stored[s], 16 * (iters + 1))

        @block.tensor
        def _(pe):
            def transpose_o(it, k, first=False):
                s = k % STREAMS
                o = x_o if k % STEPS < STREAMS else ctx_o[s]
                if not first:
                    pe.wait_ge(hT_lo_ready, after(it, k, 1, 0))
                if k % STEPS < STREAMS:
                    pe.wait_ge(adj_loaded[s], loads_until(it, group_of(k)))
                    for b in range(G):
                        pe.transpose(ps_oT[:, ADJ + b * S:ADJ + (b + 1) * S], adj_in[s][:, b, :], ident)
                pe.wait_ge(o_ready, after(it, k, 1, 1))
                for kt in range(KT):
                    for b in range(G):
                        last = pe.transpose(ps_oT[:, kt * GS + b * S:kt * GS + (b + 1) * S],
                                            o[:, b, kt * P:(kt + 1) * P], ident)
                last.then_inc(oT_psum, 1)

            def factor(it, k, ht):
                s, n, layer = k % STREAMS, k * KT + ht, k % STEPS // STREAMS
                pe.wait_ge(hT_hi_ready, after(it, k, 1, 1))
                pe.wait_ge(wh_hi_ready, after(it, k, KT, ht + 1))
                pe.wait_ge(wh_lo_ready, after(it, k, KT, ht + 1))
                for m in range(2):
                    pairs = [(w_hi[layer][:, m, ot, ht * P:(ht + 1) * P], w_lo[layer][:, m, ot, ht * P:(ht + 1) * P],
                              hT_hi[s][:, ot, :], hT_lo[s][:, ot, :]) for ot in range(KT)]
                    high_pass(pe, ps_wh[:, n % 2, m, :], pairs)
                    low_high_pass(pe, ps_wh[:, n % 2, m, :], pairs)
                    if m == 0:
                        pe.wait_ge(hT_lo_ready, after(it, k, 1, 1))
                    last = high_low_pass(pe, ps_wh[:, n % 2, m, :], pairs)
                last.then_inc(wh_psum, 1)

            def linear(it, k, b):
                s, layer = k % STREAMS, k % STEPS // STREAMS
                pe.wait_ge(lin_out, after(it, k, G, b + 1))
                pairs = [(hT_hi[s][:, kt, b * S:(b + 1) * S], hT_lo[s][:, kt, b * S:(b + 1) * S],
                          w_hi[layer][:, 2, kt, :], w_lo[layer][:, 2, kt, :]) for kt in range(KT)]
                high_pass(pe, ps_lin[:, 0:D], pairs)
                low_passes(pe, ps_lin[:, 0:D], pairs).then_inc(lin_psum, 1)

            def scores(it, k):
                s = k % STREAMS
                for b in range(G):
                    for kt in range(KT):
                        if b == 0:
                            pe.wait_ge(wh_hi_ready, after(it, k, KT, 2 + kt + 1))
                            pe.wait_ge(wh_lo_ready, after(it, k, KT, 2 + kt + 1))
                        h_hi, h_lo = hT_hi[s][:, kt, b * S:(b + 1) * S], hT_lo[s][:, kt, b * S:(b + 1) * S]
                        f_hi, f_lo = wh_hi[:, kt, :, b * S:(b + 1) * S], wh_lo[:, kt, :, b * S:(b + 1) * S]
                        pe.matmul(ps_u[:, b], h_hi, f_hi, start=(kt == 0), stop=False)
                        pe.matmul(ps_u[:, b], h_lo, f_hi, start=False, stop=False)
                        last = pe.matmul(ps_u[:, b], h_hi, f_lo, start=False, stop=(kt == KT - 1))
                last.then_inc(u_psum, 1)

            def context(it, k, b):
                pairs = [(dT_hi[:, b, :], dT_lo[:, b, :], lin_hi[:, b, :], lin_lo[:, b, :])]
                pe.wait_ge(dT_hi_ready, after(it, k, 1, 1))
                pe.wait_ge(lin_hi_ready, after(it, k, G, b + 1))
                high_pass(pe, ps_ctx[:, b, 0:D + 2], pairs)
                pe.wait_ge(dT_lo_ready, after(it, k, 1, 1))
                pe.wait_ge(lin_lo_ready[b], after(it, k, 1, 1))
                low_passes(pe, ps_ctx[:, b, 0:D + 2], pairs).then_inc(ctx_psum, 1)

            def step(it, k, final=False):
                last, last_two = final and k == 3, final and k >= 2
                linear(it, k, 1)
                if not last:
                    factor(it, k + 1, 0)
                for b in range(G):
                    context(it, k, b)
                if not last:
                    for ht in range(1, KT):
                        factor(it, k + 1, ht)
                    linear(it, k + 1, 0)
                    if not last_two:
                        transpose_o(it, k + 2)
                    scores(it, k + 1)

            pe.wait_ge(ident_loaded, 16)
            transpose_o(0, 0, first=True)
            pe.wait_ge(ones_ready, 4)
            for ht in range(KT):
                factor(0, 0, ht)
            linear(0, 0, 0)
            transpose_o(0, 1)
            scores(0, 0)
            step(0, 0)
            pe.wait_ge(w_hi_ready, 3)
            pe.wait_ge(w_lo_ready, 3)
            with pe.Fori(0, iters - 1) as it:
                for k in (1, 2, 3, 4):
                    step(it, k)
            for k in (1, 2, 3):
                step(iters - 1, k, final=True)

        @block.scalar
        def _(act):
            def x_normalise(it, s):
                t = s % STREAMS
                act.wait_ge(x_shift_ready, after_group(it, s, 1, 1))
                for b in range(G):
                    last = act.activation(x_o[:, b, :], x_in[t][:, b, :], ACT.Identity,
                                          bias=x_shift[t][:, b:b + 1], scale=x_rstd[t][:, b:b + 1])
                last.then_inc(o_ready, 1)

            def c_normalise(it, k):
                s, done = k % STREAMS, (o_ready if k % STEPS < STREAMS else res_o_ready)
                act.wait_ge(c_shift_ready, after(it, k, 1, 1))
                for b in range(G):
                    last = act.activation(ctx_o[s][:, b, :], ctx_o[s][:, b, :], ACT.Identity,
                                          bias=c_shift[:, b:b + 1], scale=c_rstd[:, b:b + 1])
                last.then_inc(done, 1)

            def relu_hT(it, k):
                act.wait_ge(oT_psum, after(it, k, 1, 1))
                if k % STEPS < STREAMS:
                    act.activation(hT_hi[k % STREAMS][:].rearrange("p t n -> p (t n)"), ps_oT[:, 0:KT * GS],
                                   ACT.Relu).then_inc(hT_hi_ready, 1)
                    return
                for kt in range(KT):
                    last = act.activation(hT[:, kt, :], ps_oT[:, kt * GS:(kt + 1) * GS], ACT.Relu,
                                          bias=col[:, 3 * KT + kt:3 * KT + kt + 1],
                                          scale=col[:, 2 * KT + kt:2 * KT + kt + 1])
                last.then_inc(hT_ready, 1)
                act.wait_ge(hT_ready, after_group(it, k - STREAMS - k // STEPS * STREAMS, 1, 1))
                act.activation(hT_hi[k % STREAMS][:], hT[:], ACT.Copy).then_inc(hT_hi_ready, 1)

            def copy_adjT(it, k):
                act.wait_ge(oT_psum, after(it, k, 1, 1))
                act.activation(adjT[k % STREAMS][:].rearrange("p b n -> p (b n)"), ps_oT[:, ADJ:ADJ + GS],
                               ACT.Copy).then_inc(adjT_ready, 1)

            def keep_x(it, s):
                act.wait_ge(x_loaded[s % STREAMS], loads_until(it, s))
                act.activation(x_res[s % STREAMS][:], x_in[s % STREAMS][:], ACT.Copy).then_inc(x_res_ready, 1)

            def factor_high(it, k, ht):
                n = k * KT + ht
                act.wait_ge(wh_psum, after(it, k, KT, ht + 1))
                act.activation(wh_hi[:, ht], ps_wh[:, n % 2], ACT.Copy).then_inc(wh_hi_ready, 1)

            def linear_high(it, k, b):
                act.wait_ge(lin_out, after(it, k, G, 1 + b + 1))
                act.activation(lin_hi[:, b, 0:D], lin[:, b, :], ACT.Copy).then_inc(lin_hi_ready, 1)

            def divide(it, k, b):
                act.wait_ge(inv_den_ready, after(it, k, G, b + 1))
                act.activation(ctx_o[k % STREAMS][:, b, :], ps_ctx[:, b, 0:D], ACT.Copy,
                               scale=inv_den[:, b:b + 1]).then_inc(ctx_done, 1)

            def step(it, k, final=False):
                last, last_two = final and k == 3, final and k >= 2
                act.wait_ge(uT_ready, after(it, k, 1, 1))
                act.activation(prob[:], uT[:], ACT.Exp, scale=SCALE).then_inc(exp_done, 1)
                act.wait_ge(dT_ready, after(it, k, 1, 1))
                act.activation(dT_hi[:], dT[:], ACT.Copy).then_inc(dT_hi_ready, 1)
                linear_high(it, k, 1)
                if not last:
                    factor_high(it, k + 1, 0)
                for b in range(G):
                    divide(it, k, b)
                if not last:
                    factor_high(it, k + 1, 1)
                if k in (2, 3) and not final:
                    x_normalise(it, k)
                c_normalise(it, k)
                if not last:
                    factor_high(it, k + 1, 2)
                if not last_two:
                    if (k + 2) % STEPS < STREAMS:
                        copy_adjT(it, k + 2)
                    relu_hT(it, k + 2)
                if not last:
                    linear_high(it, k + 1, 0)
                if k == 3 and not final:
                    act.wait_ge(sum_ready, after_group(it, 0, G, G))
                    keep_x(it, 2)
                if k == 4:
                    act.wait_ge(sum_ready, after_group(it, 1, G, G))
                    keep_x(it, 3)

            x_normalise(0, 0)
            copy_adjT(0, 0)
            relu_hT(0, 0)
            x_normalise(0, 1)
            for ht in range(KT):
                if ht == 0:
                    act.sem_inc(wh_hi_ready, 2)
                factor_high(0, 0, ht)
            copy_adjT(0, 1)
            relu_hT(0, 1)
            linear_high(0, 0, 0)
            keep_x(0, 0)
            keep_x(0, 1)
            for i in range(3):
                act.wait_ge(w_loaded[i], 16)
                act.activation(second_hi[:, i].rearrange("p t n -> p (t n)"), w_raw[:, i, :], ACT.Copy
                               ).then_inc(w_hi_ready, 1)
            step(0, 0)
            with act.Fori(0, iters - 1) as it:
                for k in (1, 2, 3, 4):
                    step(it, k)
            for k in (1, 2, 3):
                step(iters - 1, k, final=True)

        @block.gpsimd
        def _(pool):
            def linear_low(it, k):
                pool.wait_ge(lin_hi_ready, after(it, k, G, 1))
                pool.tensor_tensor(lin_lo[:, 0, 0:D], lin[:, 0, :], lin_hi[:, 0, 0:D].bitcast(F32),
                                   ALU.subtract).then_inc(lin_lo_ready[0], 1)

            def x_power(it, s):
                pool.wait_ge(x_var_ready, after_group(it, s, 1, 1))
                pool.tensor_tensor(x_rstd[s % STREAMS][:], x_var[:], minus_half[:], ALU.pow).then_inc(x_rstd_ready, 1)

            def sigma(it, k):
                pool.wait_ge(c_var_ready, after(it, k, 1, 1))
                pool.tensor_tensor(c_sigma[:], c_var[:], half[:], ALU.pow).then_inc(c_sigma_ready, 1)

            def res_scale(it, k):
                s = k % STREAMS
                pool.wait_ge(res_o_ready, after_group(it, s, 1, 1))
                pool.wait_ge(out_stored[s], 16 * it + 16)
                for b in range(G):
                    pool.tensor_tensor(x_out[s][:, b, :], ctx_o[s][:, b, :], row[:, 2, :], ALU.mult
                                       ).then_inc(scaled_ready, 1)

            def res_shift(it, k):
                s = k % STREAMS
                for b in range(G):
                    pool.wait_ge(scaled_ready, after_group(it, s, G, b + 1))
                    pool.tensor_tensor(x_out[s][:, b, :], x_out[s][:, b, :], row[:, 3, :], ALU.add
                                       ).then_inc(shifted_done, 1)

            def step(it, k, final=False):
                sigma(it, k)
                if k in (1, 2) and not final:
                    x_power(it, k + 1)
                if k in (2, 3):
                    res_scale(it, k)
                    res_shift(it, k)
                if not (final and k == 3):
                    linear_low(it, k + 1)

            pool.memset(minus_half[:], -0.5).then_inc(half_ready, 1)
            pool.memset(half[:], 0.5).then_inc(half_ready, 1)
            pool.memset(lin_hi[:, :, ONE:ONE + 1].bitcast(F32), 1.0).then_inc(ones_ready, 1)
            pool.memset(lin_hi[:, :, ONE + 1:ONE + 2].bitcast(F32), 0.0).then_inc(ones_ready, 1)
            pool.memset(lin_lo[:, :, ONE:ONE + 1].bitcast(F32), 0.0).then_inc(ones_ready, 1)
            pool.memset(lin_lo[:, :, ONE + 1:ONE + 2].bitcast(F32), 0.0).then_inc(ones_ready, 1)
            pool.wait_ge(half_ready, 2)
            x_power(0, 0)
            x_power(0, 1)
            linear_low(0, 0)
            for i in range(3):
                pool.wait_ge(w_hi_ready, i + 1)
                pool.tensor_tensor(second_lo[:, i].rearrange("p t n -> p (t n)"), w_raw[:, i, :],
                                   second_hi[:, i].rearrange("p t n -> p (t n)").bitcast(F32), ALU.subtract
                                   ).then_inc(w_lo_ready, 1)
            pool.wait_ge(rows_loaded, 16 * 5)
            step(0, 0)
            with pool.Fori(0, iters - 1) as it:
                for k in (1, 2, 3, 4):
                    step(it, k)
            for k in (1, 2, 3):
                step(iters - 1, k, final=True)

        @block.vector
        def _(dve):
            def carried_wait(sem_of_producer, value):
                dve.wait_ge(sem_of_producer, value)
                dve.sem_inc(wait_carried, 1)

            def shift_of(out, mv, rstd):
                return dve.scalar_tensor_tensor(out=out[:], in0=mv[:, :, 0], scalar=-1.0, in1=rstd[:],
                                                op0=ALU.mult, op1=ALU.mult)

            def x_stats_of(it, s):
                t = s % STREAMS
                dve.wait_ge(x_loaded[t], loads_until(it, s))
                for b in range(G):
                    dve.bn_stats(x_stats[:, b, :], x_in[t][:, b, :]).then_inc(x_stats_done, 1)
                carried_wait(x_stats_done, after_group(it, s, G, G))
                for b in range(G):
                    dve.bn_aggr(x_mv[t][:, b, :], x_stats[:, b, :]).then_inc(x_mv_done, 1)
                dve.wait_ge(x_mv_done, after_group(it, s, G, G))
                dve.tensor_scalar(x_var[:], x_mv[t][:, :, 1], PRE_EPS, None, ALU.add).then_inc(x_var_ready, 1)

            def x_shift_of(it, s):
                dve.wait_ge(x_rstd_ready, after_group(it, s, 1, 1))
                shift_of(x_shift[s % STREAMS], x_mv[s % STREAMS], x_rstd[s % STREAMS]).then_inc(x_shift_ready, 1)

            def make_sides(it, s):
                t = s % STREAMS
                dve.wait_ge(adjT_ready, after_group(it, s, 1, 1))
                for m, a in ((0, adjT[t]), (1, adj_in[t])):
                    mask = const[:, C_LEFT + m, :].unsqueeze(1).to_broadcast([P, G, S])
                    dve.tensor_tensor(sides[t][:, :, m, :], a[:], mask, ALU.mult).then_inc(sides_done, 1)

            def inverse_sum(it, k, b):
                dve.wait_ge(ctx_psum, after(it, k, G, b + 1))
                dve.tensor_scalar(den[:, b:b + 1], ps_ctx[:, b, ONE:ONE + 1], SUM_EPS, None,
                                  ALU.add).then_inc(den_done, 1)
                dve.wait_ge(den_done, after(it, k, G, b + 1))
                dve.reciprocal(inv_den[:, b:b + 1], den[:, b:b + 1]).then_inc(inv_den_ready, 1)

            def context_stats(it, k):
                s = k % STREAMS
                for b in range(G):
                    dve.wait_ge(ctx_done, after(it, k, G, b + 1))
                    dve.bn_stats(c_stats[:, b, :], ctx_o[s][:, b, :]).then_inc(c_stats_done, 1)
                carried_wait(c_stats_done, after(it, k, G, G))
                for b in range(G):
                    dve.bn_aggr(c_mv[:, b, :], c_stats[:, b, :]).then_inc(c_mv_done, 1)
                dve.wait_ge(c_mv_done, after(it, k, G, G))
                dve.tensor_scalar(c_var[:], c_mv[:, :, 1], D / (D - 1.0), None, ALU.mult).then_inc(c_var_ready, 1)

            def context_shift(it, k):
                dve.wait_ge(c_sigma_ready, after(it, k, 1, 1))
                dve.tensor_scalar(c_sigma_eps[:], c_sigma[:], SIGMA_EPS, None, ALU.add).then_inc(c_sigma_eps_done, 1)
                dve.wait_ge(c_sigma_eps_done, after(it, k, 1, 1))
                dve.reciprocal(c_rstd[:], c_sigma_eps[:]).then_inc(c_rstd_done, 1)
                dve.wait_ge(c_rstd_done, after(it, k, 1, 1))
                shift_of(c_shift, c_mv, c_rstd).then_inc(c_shift_ready, 1)

            def residual(it, k):
                s = k % STREAMS
                dve.wait_ge(x_res_ready, after_group(it, s, 1, 1))
                for b in range(G):
                    dve.wait_ge(shifted_done, after_group(it, s, G, b + 1))
                    dve.scalar_tensor_tensor(out=x_out[s][:, b, :], in0=x_out[s][:, b, :], scalar=0.0,
                                             in1=x_res[s][:, b, :], op0=ALU.max, op1=ALU.add
                                             ).then_inc(sum_ready, 1)

            def hT_low(it, k):
                hi, lo = hT_hi[k % STREAMS][:].bitcast(F32), hT_lo[k % STREAMS][:]
                dve.wait_ge(hT_hi_ready, after(it, k, 1, 1))
                if k % STEPS < STREAMS:
                    last = dve.scalar_tensor_tensor(out=lo.rearrange("p t n -> p (t n)"), in0=ps_oT[:, 0:KT * GS],
                                                    scalar=0.0, in1=hi.rearrange("p t n -> p (t n)"),
                                                    op0=ALU.max, op1=ALU.subtract)
                else:
                    dve.wait_ge(hT_ready, after_group(it, k - STREAMS - k // STEPS * STREAMS, 1, 1))
                    last = dve.tensor_tensor(lo, hT[:], hi, ALU.subtract)
                last.then_inc(hT_lo_ready, 1)

            def linear_bias(it, k, b):
                dve.wait_ge(lin_psum, after(it, k, G, b + 1))
                dve.tensor_tensor(lin[:, b, :], ps_lin[:, 0:D], row[:, k % STEPS // STREAMS, :], ALU.add
                                  ).then_inc(lin_out, 1)

            def linear_low(it, k):
                dve.wait_ge(lin_out, after(it, k, G, 1 + G))
                dve.wait_ge(lin_hi_ready, after(it, k, G, G))
                dve.tensor_tensor(lin_lo[:, 1, 0:D], lin[:, 1, :], lin_hi[:, 1, 0:D].bitcast(F32),
                                  ALU.subtract).then_inc(lin_lo_ready[1], 1)

            def factor_low(it, k, ht):
                n = k * KT + ht
                dve.wait_ge(wh_hi_ready, after(it, k, KT, 2 + ht + 1))
                dve.tensor_tensor(wh_lo[:, ht], ps_wh[:, n % 2], wh_hi[:, ht].bitcast(F32), ALU.subtract
                                  ).then_inc(wh_lo_ready, 1)

            def mask_scores(it, k):
                dve.wait_ge(u_psum, after(it, k, 1, 1))
                dve.tensor_tensor(uT2[:], ps_u[:], sides[k % STREAMS][:], ALU.mult).then_inc(uT2_done, 1)
                dve.wait_ge(uT2_done, after(it, k, 1, 1))
                dve.tensor_tensor(uT[:], uT2[:, :, 0, :], uT2[:, :, 1, :], ALU.add).then_inc(uT_ready, 1)

            def mask_exp(it, k):
                dve.wait_ge(exp_done, after(it, k, 1, 1))
                dve.tensor_tensor(dT[:], prob[:], adjT[k % STREAMS][:], ALU.mult).then_inc(dT_ready, 1)

            def exp_low(it, k):
                dve.wait_ge(dT_ready, after(it, k, 1, 1))
                dve.wait_ge(dT_hi_ready, after(it, k, 1, 1))
                dve.tensor_tensor(dT_lo[:], dT[:], dT_hi[:].bitcast(F32), ALU.subtract).then_inc(dT_lo_ready, 1)

            def step(it, k, final=False):
                last = final and k == 3
                mask_scores(it, k)
                if not last:
                    hT_low(it, k + 1)
                mask_exp(it, k)
                linear_bias(it, k, 1)
                exp_low(it, k)
                linear_low(it, k)
                for b in range(G):
                    inverse_sum(it, k, b)
                if not last:
                    factor_low(it, k + 1, 0)
                context_stats(it, k)
                if not last:
                    factor_low(it, k + 1, 1)
                context_shift(it, k)
                if k in (1, 2) and not final:
                    x_stats_of(it, k + 1)
                if k in (3, 4):
                    residual(it, k - 1)
                if k in (0, 3, 4) and not last:
                    make_sides(it, group_of(k + 1))
                if not last:
                    factor_low(it, k + 1, 2)
                    linear_bias(it, k + 1, 0)
                if k in (1, 2) and not final:
                    x_shift_of(it, k + 1)

            for s in range(STREAMS):
                x_stats_of(0, s)
                x_shift_of(0, s)
            dve.sem_inc(wh_lo_ready, 2)
            dve.sem_inc(lin_out, 1)
            dve.wait_ge(ident_loaded, 16)
            hT_low(0, 0)
            make_sides(0, 0)
            for ht in range(KT):
                factor_low(0, 0, ht)
            dve.wait_ge(rows_loaded, 16 * 5)
            linear_bias(0, 0, 0)
            step(0, 0)
            with dve.Fori(0, iters - 1) as it:
                for k in (1, 2, 3, 4):
                    step(it, k)
            for k in (1, 2, 3):
                step(iters - 1, k, final=True)
            residual(iters - 1, 3)


def build(nc, x, adj, weights, rows, columns, consts, out):
    x1 = nc.dram_tensor("x1", x.shape, F32, kind="Internal").ap()
    with nc.sbuf_tensor("first_hi", [P, 3, KT, D], F32R) as first_hi, \
            nc.sbuf_tensor("first_lo", [P, 3, KT, D], F32R) as first_lo:
        network_one(nc, x, adj, weights, rows, columns, consts, x1, first_hi, first_lo)
        network_two(nc, x1, adj, weights, rows, columns, consts, out, first_hi, first_lo)


def arrange(inputs):
    import numpy as np

    a = {k: np.asarray(v) for k, v in inputs.items()}

    def tiles(w):
        return w.reshape(KT, P, w.shape[1]).transpose(1, 0, 2).reshape(P, KT * w.shape[1])

    weights = [tiles(a[n][l].T) for l in range(LAYERS) for n in ("L0_gnn_Wl", "L0_gnn_Wr", "L0_gnn_Ws")]
    for l in range(LAYERS):
        weights += [tiles(a["L1_gnn_W_left"][l]), tiles(a["L1_gnn_W_right"][l]), tiles(a["L1_gnn_W_lin"][l].T)]
    rows = [a[n][l] for l in range(LAYERS) for n in ("L0_gnn_bl", "L0_gnn_br", "L0_gnn_bs")]
    rows += [a["L0_gnn_ln_w"][1], a["L0_gnn_ln_b"][1], a["L1_gnn_b_lin"][0], a["L1_gnn_b_lin"][1],
             a["L1_gnn_ln_a"][1], a["L1_gnn_ln_b"][1]]
    columns = [a[n][0].reshape(KT, P).T for n in ("L0_gnn_ln_w", "L0_gnn_ln_b", "L1_gnn_ln_a", "L1_gnn_ln_b")]
    part, free = np.indices((P, S))
    masks = [part == free, part > free, part < free, free <= part, free > part]
    return {
        "x": np.ascontiguousarray(a["x"]),
        "adj": np.ascontiguousarray(a["adj"]),
        "weights": np.ascontiguousarray(np.stack(weights)),
        "rows": np.ascontiguousarray(np.stack(rows)),
        "columns": np.ascontiguousarray(np.concatenate(columns, axis=1)),
        "consts": np.ascontiguousarray(np.stack([m.astype(np.float32) for m in masks], axis=1)),
    }


def kernel(**inputs):
    import concourse.bacc as bacc
    from concourse.bass_utils import run_bass_kernel_spmd

    arrays = arrange(inputs)
    nc = bacc.Bacc("TRN2", target_bir_lowering=False, num_devices=1)
    args = [nc.dram_tensor(n, a.shape, mybir.dt.from_np(a.dtype), kind="ExternalInput").ap()
            for n, a in arrays.items()]
    out = nc.dram_tensor("out", arrays["x"].shape, F32, kind="ExternalOutput").ap()
    build(nc, *args, out)
    return run_bass_kernel_spmd(nc, [arrays], core_ids=[0]).results[0]["out"]
```

```python
from contextlib import ExitStack

import concourse.bass as bass
from concourse import mybir

P = 128
S = 128
D = 384
KT = D // P
G = 2
STREAMS = 2
LAYERS = 2
STEPS = STREAMS * LAYERS
GS = G * S
SCALE = float(D) ** -0.5
PRE_EPS = 1e-5
CTX_EPS = 1e-12
SIGMA_EPS = 1e-3
LOWEST = -3.0e38
SUM_EPS = 1e-10

ALU = mybir.AluOpType
ACT = mybir.ActivationFunctionType
F32 = mybir.dt.float32
F32R = mybir.dt.float32r
AX_X = mybir.AxisListType.X

ROW_BIAS = 0
ROW_LN = 6
ROW_LIN = 8
ROW_LN2 = 10
ROWS = 12
C_IDENT, C_UPPER, C_LOWER, C_LEFT, C_RIGHT = range(5)
LEFT, RIGHT, SELF = range(3)
PROJECTIONS = [(0, LEFT), (0, RIGHT), (1, LEFT), (1, RIGHT), (0, SELF), (1, SELF)]
SPLIT_WITH = {1: (6,), 2: (7, 8), 3: ()}


def after(it, k, per_step, n):
    return it * (STEPS * per_step) + (k * per_step + n)


def after_group(it, s, per_group, n):
    return it * (STREAMS * per_group) + (s * per_group + n)


def loads_until(it, s):
    return 16 * it + 16 * (s // STREAMS + 1)


def group_of(k):
    return k // STEPS * STREAMS + k % STREAMS


def high_pass(pe, out, pairs):
    for i, (a_hi, _, b_hi, _) in enumerate(pairs):
        pe.matmul(out, a_hi, b_hi, start=(i == 0), stop=False)


def low_high_pass(pe, out, pairs):
    for _, a_lo, b_hi, _ in pairs:
        pe.matmul(out, a_lo, b_hi, start=False, stop=False)


def high_low_pass(pe, out, pairs):
    for i, (a_hi, _, _, b_lo) in enumerate(pairs):
        last = pe.matmul(out, a_hi, b_lo, start=False, stop=(i == len(pairs) - 1))
    return last


def low_passes(pe, out, pairs):
    low_high_pass(pe, out, pairs)
    return high_low_pass(pe, out, pairs)


class Shared:

    def __init__(self, nc, ctx):
        def sb(name, shape, dt=F32):
            return ctx.enter_context(nc.sbuf_tensor(name, shape, dt))

        self.row = sb("row", [P, ROWS, D])
        self.col = sb("col", [P, 4 * KT])
        self.const = sb("const", [P, 5, S])
        self.minus_half = sb("minus_half", [P, G])
        self.next_hi = sb("next_hi", [P, 3, KT, D], F32R)
        self.next_lo = sb("next_lo", [P, 3, KT, D], F32R)
        self.x_in = [sb(f"x_in{s}", [P, G, D]) for s in range(STREAMS)]
        self.x_res = [sb(f"x_res{s}", [P, G, D]) for s in range(STREAMS)]
        self.x_out = [sb(f"x_out{s}", [P, G, D]) for s in range(STREAMS)]
        self.adj_in = [sb(f"adj_in{s}", [P, G, S]) for s in range(STREAMS)]
        self.ctx_o = [sb(f"ctx_o{s}", [P, G, D]) for s in range(STREAMS)]
        self.hT_halves = [sb(f"hT_halves{s}", [P, KT, G, 2, S], F32R) for s in range(STREAMS)]
        self.x_o = sb("x_o", [P, G, D])
        self.x1_stored = [ctx.enter_context(nc.semaphore(f"x1_stored{s}")) for s in range(STREAMS)]


def network_one(nc, shared, x, adj, weights, rows, columns, consts, x1):
    iters = x.shape[0] // (G * STREAMS)
    row, col, const, minus_half = shared.row, shared.col, shared.const, shared.minus_half
    x_in, x_res, x_out, adj_in = shared.x_in, shared.x_res, shared.x_out, shared.adj_in
    ctx_o, hT_halves, x_o = shared.ctx_o, shared.hT_halves, shared.x_o
    ident = const[:, C_IDENT, :]
    x_g = x.rearrange("(i b) p d -> i p b d", b=G)
    x1_g = x1.rearrange("(i b) p d -> i p b d", b=G)
    adj_g = adj.rearrange("(i b) p d -> i p b d", b=G)

    with ExitStack() as ctx:
        def sb(name, shape, dt=F32):
            return ctx.enter_context(nc.sbuf_tensor("n1_" + name, shape, dt))

        def ps(name, shape):
            return ctx.enter_context(nc.psum_tensor("n1_ps_" + name, shape, F32))

        def sem(name):
            return ctx.enter_context(nc.semaphore("n1_" + name))

        w_raw = sb("w_raw", [P, 3, KT * D])
        w_hi = sb("w_hi", [P, LAYERS * 3, KT, D], F32R)
        w_lo = sb("w_lo", [P, LAYERS * 3, KT, D], F32R)

        x_mv = [sb(f"x_mv{s}", [P, G, 2]) for s in range(STREAMS)]
        x_rstd = [sb(f"x_rstd{s}", [P, G]) for s in range(STREAMS)]
        x_shift = [sb(f"x_shift{s}", [P, G]) for s in range(STREAMS)]

        hT = sb("hT", [P, KT, G, S])
        proj = sb("proj", [P, G, 2, D])
        proj_hi = sb("proj_hi", [P, G, 2, D], F32R)
        proj_lo = sb("proj_lo", [P, G, 2, D], F32R)
        own = sb("own", [P, G, D])
        u_cross = sb("u_cross", [P, G, S], F32R)
        u_low = sb("u_low", [P, G, S])
        ident_r = sb("ident_r", [P, S], F32R)
        u = sb("u", [P, G, S])
        prob = sb("prob", [P, G, S])
        delta = sb("delta", [P, G, S])
        delta_diag = sb("delta_diag", [P, G, S])
        aT = sb("aT", [P, G, 2, S])
        aT_hi = sb("aT_hi", [P, G, 2, S], F32R)
        aT_lo = sb("aT_lo", [P, G, 2, S], F32R)
        row_max = sb("row_max", [P, G])
        exp_bias = sb("exp_bias", [P, G])
        z_sum = sb("z_sum", [P, G])
        d_sum = sb("d_sum", [P, G])
        den = sb("den", [P, G])
        eps_den = sb("eps_den", [P, G])
        diag = sb("diag", [P, G])
        c_stats = sb("c_stats", [P, G, 6])
        c_mv = sb("c_mv", [P, G, 2])
        c_var = sb("c_var", [P, G])
        c_rstd = sb("c_rstd", [P, G])
        c_shift = sb("c_shift", [P, G])
        x_stats = sb("x_stats", [P, G, 6])
        x_var = sb("x_var", [P, G])

        ps_oT = ps("oT", [P, 1024])
        ps_u = ps("u", [P, G, 2, S])
        ps_w = ps("w", [P, 3, 512])
        ps_ctx = ps("ctx", [P, G, 512])
        ps_oT_tiles = ps_oT[:, 0:KT * GS].rearrange("p (t b n) -> p t b n", t=KT, b=G)
        ps_aT = ps_ctx[:, :, D:D + S]

        ident_loaded, rows_loaded = sem("ident_loaded"), sem("rows_loaded")
        first_rows_loaded = sem("first_rows_loaded")
        w_loaded = [sem(f"w_loaded{i}") for i in range(9)]
        x_loaded = [sem(f"x_loaded{s}") for s in range(STREAMS)]
        adj_loaded = [sem(f"adj_loaded{s}") for s in range(STREAMS)]
        x1_stored = shared.x1_stored
        w_hi_ready, w_lo_ready = sem("w_hi_ready"), sem("w_lo_ready")
        half_ready = sem("half_ready")
        o_ready, oT_psum, hT_ready = sem("o_ready"), sem("oT_psum"), sem("hT_ready")
        hT_hi_ready, hT_lo_ready = sem("hT_hi_ready"), sem("hT_lo_ready")
        u_cross_ready, mirror_psum, ident_r_ready = sem("u_cross_ready"), sem("mirror_psum"), sem("ident_r_ready")
        u_low_done = sem("u_low_done")
        u_psum, max_done, exp_bias_ready = sem("u_psum"), sem("max_done"), sem("exp_bias_ready")
        exp_done, delta_done, den_done = sem("exp_done"), sem("delta_done"), sem("den_done")
        eps_den_done, diag_done = sem("eps_den_done"), sem("diag_done")
        aT_psum, aT_ready = sem("aT_psum"), sem("aT_ready")
        aT_hi_ready, aT_lo_ready = sem("aT_hi_ready"), sem("aT_lo_ready")
        proj_psum, proj_out = sem("proj_psum"), sem("proj_out")
        proj_hi_ready, proj_lo_ready = sem("proj_hi_ready"), sem("proj_lo_ready")
        ctx_psum, ctx_done, c_stats_done = sem("ctx_psum"), sem("ctx_done"), sem("c_stats_done")
        c_mv_done, c_var_ready, c_rstd_ready = sem("c_mv_done"), sem("c_var_ready"), sem("c_rstd_ready")
        c_shift_ready, res_o_ready = sem("c_shift_ready"), sem("res_o_ready")
        x_stats_done, x_mv_done, x_var_ready = sem("x_stats_done"), sem("x_mv_done"), sem("x_var_ready")
        x_rstd_ready, x_shift_ready, x_res_ready = sem("x_rstd_ready"), sem("x_shift_ready"), sem("x_res_ready")
        scaled_ready, shifted_done, x1_ready = sem("scaled_ready"), sem("shifted_done"), sem("x1_ready")
        wait_carried = sem("wait_carried")


        block = ctx.enter_context(nc.Block())

        @block.sync
        def _(sp):
            def load_x(i, s, source=x_g):
                sp.dma_start(x_in[s][:], source[bass.ds(i * STREAMS + s, 1)].rearrange("a p b d -> (a p) b d")
                             ).then_inc(x_loaded[s], 16)

            def load_adj(i, s):
                sp.dma_start(adj_in[s][:], adj_g[bass.ds(i * STREAMS + s, 1)].rearrange("a p b d -> (a p) b d")
                             ).then_inc(adj_loaded[s], 16)

            def store_x1(i, s):
                sp.dma_start(x1_g[bass.ds(i * STREAMS + s, 1)].rearrange("a p b d -> (a p) b d"),
                             x_out[s][:]).then_inc(x1_stored[s], 16)

            def load_weights(i):
                if i >= 3:
                    sp.wait_ge(w_hi_ready, i - 2)
                    sp.wait_ge(w_lo_ready, i - 2)
                sp.dma_start(w_raw[:, i % 3, :], weights[i]).then_inc(w_loaded[i], 16)

            def load_row(r):
                return sp.dma_start(row[:, r, :], rows[r:r + 1, :].partition_broadcast(P))

            load_x(0, 0)
            sp.dma_start(const[:], consts).then_inc(ident_loaded, 16)
            for i in range(3):
                load_weights(i)
                load_row(i).then_inc(first_rows_loaded, 16)
            load_adj(0, 0)
            load_x(0, 1)
            sp.dma_start(col[:], columns).then_inc(rows_loaded, 16)
            load_adj(0, 1)
            for i in range(3, 6):
                load_weights(i)
            for r in range(3, ROWS):
                load_row(r).then_inc(rows_loaded, 16)
            for s in range(STREAMS):
                sp.sem_inc(x1_stored[s], 16)

            with sp.Fori(0, iters - 1) as it:
                a_normed, a_kept, b_normed, b_kept, a_adj_used, a_summed, b_adj_used, b_summed = (
                    sp.to_reg(v) for v in (
                        after(it, 0, 1, 1), after_group(it, 0, 1, 1),
                        after(it, 1, 1, 1), after_group(it, 1, 1, 1),
                        after(it, 2, G, G), after_group(it, 0, G, G),
                        after(it, 3, G, G), after_group(it, 1, G, G)))
                sp.wait_ge(o_ready, a_normed)
                sp.wait_ge(x_res_ready, a_kept)
                load_x(it + 1, 0)
                sp.wait_ge(o_ready, b_normed)
                sp.wait_ge(x_res_ready, b_kept)
                load_x(it + 1, 1)
                sp.wait_ge(delta_done, a_adj_used)
                load_adj(it + 1, 0)
                sp.wait_ge(x1_ready, a_summed)
                store_x1(it, 0)
                sp.wait_ge(delta_done, b_adj_used)
                load_adj(it + 1, 1)
                sp.wait_ge(x1_ready, b_summed)
                store_x1(it, 1)
            last = iters - 1
            for s in range(STREAMS):
                sp.wait_ge(x1_stored[s], 32)
                sp.wait_ge(o_ready, after(last, s, 1, 1))
                sp.wait_ge(x_res_ready, after_group(last, s, 1, 1))
                load_x(0, s, x1_g)
            for i in range(6, 9):
                load_weights(i)
            sp.wait_ge(delta_done, after(last, 2, G, G))
            load_adj(0, 0)
            sp.wait_ge(x1_ready, after_group(last, 0, G, G))
            store_x1(last, 0)
            sp.wait_ge(delta_done, after(last, 3, G, G))
            load_adj(0, 1)
            for s in range(STREAMS):
                sp.wait_ge(x_loaded[s], 16 * (iters + 1))
                sp.wait_ge(adj_loaded[s], 16 * (iters + 1))

        @block.tensor
        def _(pe):
            def halves(s, b):
                return [(hT_halves[s][:, kt, b, 0, :], hT_halves[s][:, kt, b, 1, :]) for kt in range(KT)]

            def transpose_o(it, k, first=False):
                o = x_o if k % STEPS < STREAMS else ctx_o[k % STREAMS]
                pe.wait_ge(o_ready, after(it, k, 1, 1))
                if not first:
                    pe.wait_ge(hT_lo_ready, after(it, k, 1, 0))
                for kt in range(KT):
                    for b in range(G):
                        last = pe.transpose(ps_oT[:, kt * GS + b * S:kt * GS + (b + 1) * S],
                                            o[:, b, kt * P:(kt + 1) * P], ident)
                last.then_inc(oT_psum, 1)

            def scores(it, k):
                s = k % STREAMS
                pe.wait_ge(hT_hi_ready, after(it, k, 1, 1))
                pe.wait_ge(hT_lo_ready, after(it, k, 1, 1))
                for b in range(G):
                    for kt, (hi, _) in enumerate(halves(s, b)):
                        last = pe.matmul(ps_u[:, b], hi, hT_halves[s][:, kt, b], start=(kt == 0), stop=(kt == KT - 1))
                last.then_inc(u_psum, 1)

            def mirror_cross(it, k, first=False):
                pe.wait_ge(u_cross_ready, after(it, k, 1, 1))
                if not first:
                    pe.wait_ge(ctx_done, after(it, k, G, 0))
                for b in range(G):
                    last = pe.matmul(ps_ctx[:, b, D:D + S], u_cross[:, b, :], ident_r[:], start=True, stop=True)
                last.then_inc(mirror_psum, 1)

            def project(it, k, n, first=False):
                b, m = PROJECTIONS[n]
                pe.wait_ge(proj_out, after(it, k, 6, n + 1))
                w = (k % STEPS // STREAMS) * 3 + m
                if first:
                    pe.wait_ge(w_hi_ready, w + 1)
                    pe.wait_ge(w_lo_ready, w + 1)
                pairs = [(*h, w_hi[:, w, kt, :], w_lo[:, w, kt, :]) for kt, h in enumerate(halves(k % STREAMS, b))]
                high_pass(pe, ps_w[:, n % 3, 0:D], pairs)
                low_passes(pe, ps_w[:, n % 3, 0:D], pairs).then_inc(proj_psum, 1)

            def transpose_attn(it, k):
                pe.wait_ge(delta_done, after(it, k, G, G))
                for b in range(G):
                    last = pe.transpose(ps_ctx[:, b, D:D + S], delta[:, b, :], ident)
                last.then_inc(aT_psum, 1)

            def context(it, k, b):
                pairs = [(aT_hi[:, b, m, :], aT_lo[:, b, m, :], proj_hi[:, b, m, :], proj_lo[:, b, m, :])
                         for m in range(2)]
                pe.wait_ge(aT_hi_ready, after(it, k, 1, 1))
                pe.wait_ge(proj_hi_ready, after(it, k, 2 * G, 2 * b + 2))
                high_pass(pe, ps_ctx[:, b, 0:D], pairs)
                pe.wait_ge(aT_lo_ready, after(it, k, 1, 1))
                pe.wait_ge(proj_lo_ready, after(it, k, 2 * G, 2 * b + 2))
                low_passes(pe, ps_ctx[:, b, 0:D], pairs).then_inc(ctx_psum, 1)

            def step(it, k, first=False, final=False):
                last = final and k == 3
                if k == 2:
                    pe.wait_ge(w_hi_ready, 6)
                    pe.wait_ge(w_lo_ready, 6)
                project(it, k, 0, first)
                mirror_cross(it, k, first)
                for n in range(1, 4):
                    project(it, k, n, first)
                transpose_o(it, k + 1)
                transpose_attn(it, k)
                project(it, k, 4, first)
                project(it, k, 5, first)
                context(it, k, 0)
                context(it, k, 1)
                if not last:
                    scores(it, k + 1)

            pe.wait_ge(ident_loaded, 16)
            transpose_o(0, 0, first=True)
            scores(0, 0)
            pe.wait_ge(ident_r_ready, 1)
            step(0, 0, first=True)
            with pe.Fori(0, iters - 1) as it:
                for k in (1, 2, 3, 4):
                    step(it, k)
            for k in (1, 2, 3):
                step(iters - 1, k, final=True)

        @block.scalar
        def _(act):
            def x_normalise(it, s):
                t = s % STREAMS
                act.wait_ge(x_shift_ready, after_group(it, s, 1, 1))
                for b in range(G):
                    last = act.activation(x_o[:, b, :], x_in[t][:, b, :], ACT.Identity,
                                          bias=x_shift[t][:, b:b + 1], scale=x_rstd[t][:, b:b + 1])
                last.then_inc(o_ready, 1)

            def c_normalise(it, k):
                s, done = k % STREAMS, (o_ready if k % STEPS < STREAMS else res_o_ready)
                act.wait_ge(c_shift_ready, after(it, k, 1, 1))
                for b in range(G):
                    last = act.activation(ctx_o[s][:, b, :], ctx_o[s][:, b, :], ACT.Identity,
                                          bias=c_shift[:, b:b + 1], scale=c_rstd[:, b:b + 1])
                last.then_inc(done, 1)

            def relu_hT(it, k):
                act.wait_ge(oT_psum, after(it, k, 1, 1))
                if k % STEPS < STREAMS:
                    act.activation(hT_halves[k % STREAMS][:, :, :, 0, :], ps_oT_tiles, ACT.Relu
                                   ).then_inc(hT_hi_ready, 1)
                else:
                    for kt in range(KT):
                        last = act.activation(hT[:, kt], ps_oT_tiles[:, kt], ACT.Relu,
                                              bias=col[:, KT + kt:KT + kt + 1], scale=col[:, kt:kt + 1])
                    last.then_inc(hT_ready, 1)

            def high_hT(it, k):
                act.wait_ge(hT_ready, after_group(it, group_of(k), 1, 1))
                act.activation(hT_halves[k % STREAMS][:, :, :, 0, :], hT[:], ACT.Copy).then_inc(hT_hi_ready, 1)

            def copy_cross(it, k):
                act.wait_ge(u_psum, after(it, k, 1, 1))
                act.activation(u_cross[:], ps_u[:, :, 1, :], ACT.Copy).then_inc(u_cross_ready, 1)

            def keep_x(it, s):
                act.wait_ge(x_loaded[s % STREAMS], loads_until(it, s))
                act.activation(x_res[s % STREAMS][:], x_in[s % STREAMS][:], ACT.Copy).then_inc(x_res_ready, 1)

            def proj_high(it, k, b, m):
                act.wait_ge(proj_out, after(it, k, 6, 3 + PROJECTIONS.index((b, m)) + 1))
                act.activation(proj_hi[:, b, m], proj[:, b, m], ACT.Copy).then_inc(proj_hi_ready, 1)

            def weights_high(i):
                act.wait_ge(w_loaded[i], 16)
                out = w_hi[:, i] if i < 6 else shared.next_hi[:, i - 6]
                act.activation(out.rearrange("p t n -> p (t n)"), w_raw[:, i % 3, :], ACT.Copy
                               ).then_inc(w_hi_ready, 1)

            def exponential(it, k):
                act.wait_ge(exp_bias_ready, after(it, k, 1, 1))
                for b in range(G):
                    act.activation(prob[:, b, :], u[:, b, :], ACT.Exp,
                                   bias=exp_bias[:, b:b + 1], scale=SCALE,
                                   accum_out=z_sum[:, b:b + 1]).then_inc(exp_done, 1)

            def step(it, k, first=False, final=False, split=()):
                last = final and k == 3
                exponential(it, k)
                if first:
                    x_normalise(0, 1)
                proj_high(it, k, 0, LEFT)
                proj_high(it, k, 0, RIGHT)
                proj_high(it, k, 1, LEFT)
                relu_hT(it, k + 1)
                proj_high(it, k, 1, RIGHT)
                act.wait_ge(aT_ready, after(it, k, 1, 1))
                act.activation(aT_hi[:], aT[:], ACT.Copy).then_inc(aT_hi_ready, 1)
                if (k + 1) % STEPS >= STREAMS:
                    high_hT(it, k + 1)
                for i in split:
                    weights_high(i)
                if k in (2, 3):
                    x_normalise(it, k)
                if not last:
                    copy_cross(it, k + 1)
                c_normalise(it, k)
                if k == 3 and not final:
                    act.wait_ge(x1_ready, after_group(it, 0, G, G))
                    keep_x(it, 2)
                if k == 4:
                    act.wait_ge(x1_ready, after_group(it, 1, G, G))
                    keep_x(it, 3)

            x_normalise(0, 0)
            weights_high(0)
            weights_high(1)
            relu_hT(0, 0)
            weights_high(2)
            act.activation(ident_r[:], ident, ACT.Copy).then_inc(ident_r_ready, 1)
            copy_cross(0, 0)
            keep_x(0, 0)
            step(0, 0, first=True, split=(3, 4, 5))
            keep_x(0, 1)
            act.wait_ge(rows_loaded, 16 * (1 + ROWS - 3))
            with act.Fori(0, iters - 1) as it:
                for k in (1, 2, 3, 4):
                    step(it, k)
            for k in (1, 2, 3):
                step(iters - 1, k, final=True, split=SPLIT_WITH[k])

        @block.gpsimd
        def _(pool):
            def proj_low(it, k, b, m):
                pool.wait_ge(proj_hi_ready, after(it, k, 2 * G, 2 * b + m + 1))
                pool.tensor_tensor(proj_lo[:, b, m], proj[:, b, m], proj_hi[:, b, m].bitcast(F32),
                                   ALU.subtract).then_inc(proj_lo_ready, 1)

            def x_power(it, s):
                pool.wait_ge(x_var_ready, after_group(it, s, 1, 1))
                pool.tensor_tensor(x_rstd[s % STREAMS][:], x_var[:], minus_half[:], ALU.pow).then_inc(x_rstd_ready, 1)

            def c_power(it, k):
                pool.wait_ge(c_var_ready, after(it, k, 1, 1))
                pool.tensor_tensor(c_rstd[:], c_var[:], minus_half[:], ALU.pow).then_inc(c_rstd_ready, 1)

            def res_scale(it, k):
                s = k % STREAMS
                pool.wait_ge(res_o_ready, after_group(it, s, 1, 1))
                pool.wait_ge(x1_stored[s], 16 * it + 16)
                for b in range(G):
                    pool.tensor_tensor(x_out[s][:, b, :], ctx_o[s][:, b, :], row[:, ROW_LN, :], ALU.mult
                                       ).then_inc(scaled_ready, 1)

            def res_shift(it, k):
                s = k % STREAMS
                for b in range(G):
                    pool.wait_ge(scaled_ready, after_group(it, s, G, b + 1))
                    pool.tensor_tensor(x_out[s][:, b, :], x_out[s][:, b, :], row[:, ROW_LN + 1, :], ALU.add
                                       ).then_inc(shifted_done, 1)

            def weights_low(i):
                pool.wait_ge(w_hi_ready, i + 1)
                lo, hi = (w_lo[:, i], w_hi[:, i]) if i < 6 else (shared.next_lo[:, i - 6], shared.next_hi[:, i - 6])
                pool.tensor_tensor(lo.rearrange("p t n -> p (t n)"), w_raw[:, i % 3, :],
                                   hi.rearrange("p t n -> p (t n)").bitcast(F32), ALU.subtract
                                   ).then_inc(w_lo_ready, 1)

            def step(it, k, split=()):
                proj_low(it, k, 0, LEFT)
                proj_low(it, k, 0, RIGHT)
                proj_low(it, k, 1, LEFT)
                proj_low(it, k, 1, RIGHT)
                if k in (1, 2):
                    x_power(it, k + 1)
                if k in (3, 4):
                    res_scale(it, k - 1)
                    res_shift(it, k - 1)
                for i in split:
                    weights_low(i)
                c_power(it, k)

            pool.memset(minus_half[:], -0.5).then_inc(half_ready, 1)
            pool.wait_ge(half_ready, 1)
            x_power(0, 0)
            x_power(0, 1)
            step(0, 0, split=(3,))
            weights_low(4)
            weights_low(5)
            pool.wait_ge(rows_loaded, 16 * (1 + ROWS - 3))
            with pool.Fori(0, iters - 1) as it:
                for k in (1, 2, 3, 4):
                    step(it, k)
            for k in (1, 2, 3):
                step(iters - 1, k, split=SPLIT_WITH[k])

        @block.vector
        def _(dve):
            def carried_wait(sem_of_producer, value):
                dve.wait_ge(sem_of_producer, value)
                dve.sem_inc(wait_carried, 1)

            def shift_of(out, mv, rstd):
                return dve.scalar_tensor_tensor(out=out[:], in0=mv[:, :, 0], scalar=-1.0, in1=rstd[:],
                                                op0=ALU.mult, op1=ALU.mult)

            def x_stats_of(it, s):
                t = s % STREAMS
                dve.wait_ge(x_loaded[t], loads_until(it, s))
                for b in range(G):
                    dve.bn_stats(x_stats[:, b, :], x_in[t][:, b, :]).then_inc(x_stats_done, 1)
                carried_wait(x_stats_done, after_group(it, s, G, G))
                for b in range(G):
                    dve.bn_aggr(x_mv[t][:, b, :], x_stats[:, b, :]).then_inc(x_mv_done, 1)
                dve.wait_ge(x_mv_done, after_group(it, s, G, G))
                dve.tensor_scalar(x_var[:], x_mv[t][:, :, 1], PRE_EPS, None, ALU.add).then_inc(x_var_ready, 1)

            def x_shift_of(it, s):
                dve.wait_ge(x_rstd_ready, after_group(it, s, 1, 1))
                shift_of(x_shift[s % STREAMS], x_mv[s % STREAMS], x_rstd[s % STREAMS]).then_inc(x_shift_ready, 1)

            def context_sum(it, k, b):
                s = k % STREAMS
                dve.wait_ge(ctx_psum, after(it, k, G, b + 1))
                dve.wait_ge(diag_done, after(it, k, G, b + 1))
                dve.wait_ge(proj_out, after(it, k, 6, 3 + PROJECTIONS.index((b, SELF)) + 1))
                dve.scalar_tensor_tensor(out=ctx_o[s][:, b, :], in0=own[:, b, :], scalar=diag[:, b:b + 1],
                                         in1=ps_ctx[:, b, 0:D], op0=ALU.mult, op1=ALU.add
                                         ).then_inc(ctx_done, 1)
                dve.wait_ge(ctx_done, after(it, k, G, b + 1))
                dve.bn_stats(c_stats[:, b, :], ctx_o[s][:, b, :]).then_inc(c_stats_done, 1)

            def context_var(it, k):
                carried_wait(c_stats_done, after(it, k, G, G))
                for b in range(G):
                    dve.bn_aggr(c_mv[:, b, :], c_stats[:, b, :]).then_inc(c_mv_done, 1)
                dve.wait_ge(c_mv_done, after(it, k, G, G))
                dve.wait_ge(eps_den_done, after(it, k, 1, 1))
                dve.tensor_tensor(c_var[:], c_mv[:, :, 1], eps_den[:], ALU.add).then_inc(c_var_ready, 1)

            def context_shift(it, k):
                dve.wait_ge(c_rstd_ready, after(it, k, 1, 1))
                shift_of(c_shift, c_mv, c_rstd).then_inc(c_shift_ready, 1)

            def residual(it, k, b):
                s = k % STREAMS
                dve.wait_ge(x_res_ready, after_group(it, s, 1, 1))
                dve.wait_ge(shifted_done, after_group(it, s, G, b + 1))
                dve.scalar_tensor_tensor(out=x_out[s][:, b, :], in0=x_out[s][:, b, :], scalar=0.0,
                                         in1=x_res[s][:, b, :], op0=ALU.max, op1=ALU.add
                                         ).then_inc(x1_ready, 1)

            def hT_low(it, k):
                t = k % STREAMS
                hi, lo = hT_halves[t][:, :, :, 0, :].bitcast(F32), hT_halves[t][:, :, :, 1, :]
                dve.wait_ge(hT_hi_ready, after(it, k, 1, 1))
                if k % STEPS < STREAMS:
                    last = dve.scalar_tensor_tensor(out=lo, in0=ps_oT_tiles, scalar=0.0, in1=hi,
                                                    op0=ALU.max, op1=ALU.subtract)
                else:
                    dve.wait_ge(hT_ready, after_group(it, group_of(k), 1, 1))
                    last = dve.tensor_tensor(lo, hT[:], hi, ALU.subtract)
                last.then_inc(hT_lo_ready, 1)

            def score_max(it, k):
                dve.wait_ge(mirror_psum, after(it, k, 1, 1))
                dve.tensor_tensor(u_low[:], ps_aT, u_cross[:].bitcast(F32), ALU.add).then_inc(u_low_done, 1)
                carried_wait(u_low_done, after(it, k, 1, 1))
                for b in range(G):
                    dve.tensor_tensor_reduce(u[:, b, :], ps_u[:, b, 0, :], u_low[:, b, :], 1.0, LOWEST,
                                             ALU.add, ALU.max, row_max[:, b:b + 1]).then_inc(max_done, 1)
                dve.wait_ge(max_done, after(it, k, G, G))
                dve.tensor_scalar(exp_bias[:], row_max[:], -SCALE, None, ALU.mult).then_inc(exp_bias_ready, 1)

            def attention(it, k):
                s = k % STREAMS
                dve.wait_ge(adj_loaded[s], loads_until(it, group_of(k)))
                for b in range(G):
                    dve.wait_ge(exp_done, after(it, k, G, b + 1))
                    dve.tensor_tensor_reduce(delta[:, b, :], prob[:, b, :], adj_in[s][:, b, :], 1.0, 0.0,
                                             ALU.mult, ALU.add, d_sum[:, b:b + 1]).then_inc(delta_done, 1)

            def denominator(it, k):
                dve.wait_ge(delta_done, after(it, k, G, G))
                dve.scalar_tensor_tensor(out=den[:], in0=z_sum[:], scalar=SUM_EPS, in1=d_sum[:],
                                         op0=ALU.mult, op1=ALU.add).then_inc(den_done, 1)

            def delta_diagonal(it, k):
                for b in range(G):
                    dve.wait_ge(delta_done, after(it, k, G, b + 1))
                    dve.tensor_tensor_reduce(delta_diag[:, b, :], delta[:, b, :], ident, 1.0, 0.0,
                                             ALU.mult, ALU.add, diag[:, b:b + 1]).then_inc(diag_done, 1)

            def epsilon_of_den(it, k):
                dve.wait_ge(den_done, after(it, k, 1, 1))
                dve.scalar_tensor_tensor(out=eps_den[:], in0=den[:], scalar=CTX_EPS, in1=den[:],
                                         op0=ALU.mult, op1=ALU.mult).then_inc(eps_den_done, 1)

            def proj_bias(it, k, n):
                b, m = PROJECTIONS[n]
                dve.wait_ge(proj_psum, after(it, k, 6, n + 1))
                out = own[:, b, :] if m == SELF else proj[:, b, m, :]
                dve.tensor_tensor(out, ps_w[:, n % 3, 0:D], row[:, ROW_BIAS + (k % STEPS // STREAMS) * 3 + m, :],
                                  ALU.add).then_inc(proj_out, 1)

            def mask_attn(it, k):
                dve.wait_ge(aT_psum, after(it, k, 1, 1))
                a = ps_aT[:].unsqueeze(2).to_broadcast([P, G, 2, S])
                mask = const[:, C_UPPER:C_UPPER + 2, :].unsqueeze(1).to_broadcast([P, G, 2, S])
                dve.tensor_tensor(aT[:], a, mask, ALU.mult).then_inc(aT_ready, 1)

            def attn_low(it, k):
                dve.wait_ge(aT_ready, after(it, k, 1, 1))
                dve.wait_ge(aT_hi_ready, after(it, k, 1, 1))
                dve.tensor_tensor(aT_lo[:], aT[:], aT_hi[:].bitcast(F32), ALU.subtract).then_inc(aT_lo_ready, 1)

            def step(it, k):
                proj_bias(it, k, 0)
                score_max(it, k)
                proj_bias(it, k, 1)
                attention(it, k)
                proj_bias(it, k, 2)
                denominator(it, k)
                delta_diagonal(it, k)
                epsilon_of_den(it, k)
                proj_bias(it, k, 3)
                mask_attn(it, k)
                if k in (1, 2):
                    x_stats_of(it, k + 1)
                attn_low(it, k)
                hT_low(it, k + 1)
                proj_bias(it, k, 4)
                proj_bias(it, k, 5)
                if k in (1, 2):
                    x_shift_of(it, k + 1)
                for b in range(G):
                    context_sum(it, k, b)
                context_var(it, k)
                if k in (3, 4):
                    residual(it, k - 1, 0)
                context_shift(it, k)
                if k in (3, 4):
                    residual(it, k - 1, 1)

            def weights_low(i):
                dve.wait_ge(w_hi_ready, i + 1)
                dve.tensor_tensor(w_lo[:, i].rearrange("p t n -> p (t n)"), w_raw[:, i % 3, :],
                                  w_hi[:, i].rearrange("p t n -> p (t n)").bitcast(F32), ALU.subtract
                                  ).then_inc(w_lo_ready, 1)

            dve.sem_inc(proj_out, 3)
            x_stats_of(0, 0)
            x_shift_of(0, 0)
            weights_low(0)
            hT_low(0, 0)
            weights_low(1)
            weights_low(2)
            x_stats_of(0, 1)
            x_shift_of(0, 1)
            dve.wait_ge(first_rows_loaded, 16 * 3)
            step(0, 0)
            dve.wait_ge(rows_loaded, 16 * (1 + ROWS - 3))
            with dve.Fori(0, iters - 1) as it:
                for k in (1, 2, 3, 4):
                    step(it, k)
            for k in (1, 2, 3):
                step(iters - 1, k)


def network_two(nc, shared, x1, adj, weights, out):
    iters = x1.shape[0] // (G * STREAMS)
    row, col, const, minus_half = shared.row, shared.col, shared.const, shared.minus_half
    x_in, x_res, x_out, adj_in = shared.x_in, shared.x_res, shared.x_out, shared.adj_in
    ctx_o, x_o = shared.ctx_o, shared.x_o
    hT_hi = [t[:, :, :, 0, :] for t in shared.hT_halves]
    hT_lo = [t[:, :, :, 1, :] for t in shared.hT_halves]
    ident = const[:, C_IDENT, :]
    x_g = x1.rearrange("(i b) p d -> i p b d", b=G)
    out_g = out.rearrange("(i b) p d -> i p b d", b=G)
    adj_g = adj.rearrange("(i b) p d -> i p b d", b=G)
    ONE = D

    with ExitStack() as ctx:
        def sb(name, shape, dt=F32):
            return ctx.enter_context(nc.sbuf_tensor("n2_" + name, shape, dt))

        def ps(name, shape):
            return ctx.enter_context(nc.psum_tensor("n2_ps_" + name, shape, F32))

        def sem(name):
            return ctx.enter_context(nc.semaphore("n2_" + name))

        w_raw = sb("w_raw", [P, 3, KT * D])
        second_hi = sb("second_hi", [P, 3, KT, D], F32R)
        second_lo = sb("second_lo", [P, 3, KT, D], F32R)
        w_hi, w_lo = [shared.next_hi, second_hi], [shared.next_lo, second_lo]
        half = sb("half", [P, G])

        adjT = [sb(f"adjT{s}", [P, G, S]) for s in range(STREAMS)]
        sides = [sb(f"sides{s}", [P, G, 2, S]) for s in range(STREAMS)]

        x_mv = [sb(f"x_mv{s}", [P, G, 2]) for s in range(STREAMS)]
        x_rstd = [sb(f"x_rstd{s}", [P, G]) for s in range(STREAMS)]
        x_shift = [sb(f"x_shift{s}", [P, G]) for s in range(STREAMS)]

        hT = sb("hT", [P, KT, G, S])
        wh_hi = sb("wh_hi", [P, KT, 2, GS], F32R)
        wh_lo = sb("wh_lo", [P, KT, 2, GS], F32R)
        lin = sb("lin", [P, G, D])
        lin_hi = sb("lin_hi", [P, G, D + 2], F32R)
        lin_lo = sb("lin_lo", [P, G, D + 2], F32R)
        uT2 = sb("uT2", [P, G, 2, S])
        uT = sb("uT", [P, G, S])
        prob = sb("prob", [P, G, S])
        dT = sb("dT", [P, G, S])
        dT_hi = sb("dT_hi", [P, G, S], F32R)
        dT_lo = sb("dT_lo", [P, G, S], F32R)
        den = sb("den", [P, G])
        inv_den = sb("inv_den", [P, G])
        c_stats = sb("c_stats", [P, G, 6])
        c_mv = sb("c_mv", [P, G, 2])
        c_var = sb("c_var", [P, G])
        c_sigma = sb("c_sigma", [P, G])
        c_sigma_eps = sb("c_sigma_eps", [P, G])
        c_rstd = sb("c_rstd", [P, G])
        c_shift = sb("c_shift", [P, G])
        x_stats = sb("x_stats", [P, G, 6])
        x_var = sb("x_var", [P, G])

        ps_oT = ps("oT", [P, 1024])
        ps_oT_tiles = ps_oT[:, 0:KT * GS].rearrange("p (t b n) -> p t b n", t=KT, b=G)
        ADJ = KT * GS
        ps_wh = ps("wh", [P, 2, 2, GS])
        ps_lin = ps("lin", [P, 512])
        ps_u = ps("u", [P, G, 2, S])
        ps_ctx = ps("ctx", [P, G, 512])

        last_scaled, last_shifted = sem("last_scaled"), sem("last_shifted")
        last_summed = sem("last_summed")
        w_loaded = [sem(f"w_loaded{i}") for i in range(3)]
        x_loaded = [sem(f"x_loaded{s}") for s in range(STREAMS)]
        adj_loaded = [sem(f"adj_loaded{s}") for s in range(STREAMS)]
        out_stored = [sem(f"out_stored{s}") for s in range(STREAMS)]
        w_hi_ready, w_lo_ready = sem("w_hi_ready"), sem("w_lo_ready")
        half_ready, ones_ready = sem("half_ready"), sem("ones_ready")
        o_ready, oT_psum, hT_ready = sem("o_ready"), sem("oT_psum"), sem("hT_ready")
        hT_rest_ready = sem("hT_rest_ready")
        hT_hi_ready, hT_lo_ready = sem("hT_hi_ready"), sem("hT_lo_ready")
        adjT_ready, sides_done = sem("adjT_ready"), sem("sides_done")
        wh_psum, wh_hi_ready, wh_lo_ready = sem("wh_psum"), sem("wh_hi_ready"), sem("wh_lo_ready")
        lin_psum, lin_out = sem("lin_psum"), sem("lin_out")
        lin_hi_ready = sem("lin_hi_ready")
        lin_lo_ready = [sem(f"lin_lo_ready{b}") for b in range(G)]
        u_psum, uT2_done, uT_ready = sem("u_psum"), sem("uT2_done"), sem("uT_ready")
        exp_done, dT_ready = sem("exp_done"), sem("dT_ready")
        dT_hi_ready, dT_lo_ready = sem("dT_hi_ready"), sem("dT_lo_ready")
        ctx_psum, den_done, inv_den_ready = sem("ctx_psum"), sem("den_done"), sem("inv_den_ready")
        ctx_done, c_stats_done, c_mv_done = sem("ctx_done"), sem("c_stats_done"), sem("c_mv_done")
        c_var_ready, c_sigma_ready = sem("c_var_ready"), sem("c_sigma_ready")
        c_sigma_eps_done, c_rstd_done = sem("c_sigma_eps_done"), sem("c_rstd_done")
        c_shift_ready, res_o_ready = sem("c_shift_ready"), sem("res_o_ready")
        x_stats_done, x_mv_done, x_var_ready = sem("x_stats_done"), sem("x_mv_done"), sem("x_var_ready")
        x_rstd_ready, x_shift_ready, x_res_ready = sem("x_rstd_ready"), sem("x_shift_ready"), sem("x_res_ready")
        scaled_ready, shifted_done, sum_ready = sem("scaled_ready"), sem("shifted_done"), sem("sum_ready")
        wait_carried = sem("wait_carried")


        block = ctx.enter_context(nc.Block())

        @block.sync
        def _(sp):
            def load_x(i, s):
                sp.dma_start(x_in[s][:], x_g[bass.ds(i * STREAMS + s, 1)].rearrange("a p b d -> (a p) b d")
                             ).then_inc(x_loaded[s], 16)

            def load_adj(i, s):
                sp.dma_start(adj_in[s][:], adj_g[bass.ds(i * STREAMS + s, 1)].rearrange("a p b d -> (a p) b d")
                             ).then_inc(adj_loaded[s], 16)

            def store_out(i, s):
                sp.dma_start(out_g[bass.ds(i * STREAMS + s, 1)].rearrange("a p b d -> (a p) b d"),
                             x_out[s][:]).then_inc(out_stored[s], 16)

            for i in range(3):
                sp.dma_start(w_raw[:, i, :], weights[9 + i]).then_inc(w_loaded[i], 16)
            for s in range(STREAMS):
                sp.sem_inc(x_loaded[s], 16)
                sp.sem_inc(adj_loaded[s], 16)
            sp.wait_ge(last_summed, G)
            sp.dma_start(x_g[x_g.shape[0] - 1], x_out[1][:]).then_inc(shared.x1_stored[1], 16)
            for s in range(STREAMS):
                sp.wait_ge(shared.x1_stored[s], 16 * (iters + 1))
                sp.sem_inc(out_stored[s], 16)

            with sp.Fori(0, iters - 1) as it:
                a_normed, a_kept, a_adj_used, b_normed, b_kept, b_adj_used, a_summed, b_summed = (
                    sp.to_reg(v) for v in (
                        after(it, 0, 1, 1), after_group(it, 0, 1, 1), after_group(it, 0, 2, 2),
                        after(it, 1, 1, 1), after_group(it, 1, 1, 1), after_group(it, 1, 2, 2),
                        after_group(it, 0, G, G), after_group(it, 1, G, G)))
                sp.wait_ge(o_ready, a_normed)
                sp.wait_ge(x_res_ready, a_kept)
                load_x(it + 1, 0)
                sp.wait_ge(sides_done, a_adj_used)
                load_adj(it + 1, 0)
                sp.wait_ge(o_ready, b_normed)
                sp.wait_ge(x_res_ready, b_kept)
                load_x(it + 1, 1)
                sp.wait_ge(sides_done, b_adj_used)
                load_adj(it + 1, 1)
                sp.wait_ge(sum_ready, a_summed)
                store_out(it, 0)
                sp.wait_ge(sum_ready, b_summed)
                store_out(it, 1)
            for s in range(STREAMS):
                sp.wait_ge(sum_ready, after_group(iters - 1, s, G, G))
                store_out(iters - 1, s)
            for s in range(STREAMS):
                sp.wait_ge(out_stored[s], 16 * (iters + 1))

        @block.tensor
        def _(pe):
            def transpose_adj(s):
                for b in range(G):
                    last = pe.transpose(ps_oT[:, ADJ + b * S:ADJ + (b + 1) * S], adj_in[s][:, b, :], ident)
                return last

            def transpose_o(it, k):
                s = k % STREAMS
                o = x_o if k % STEPS < STREAMS else ctx_o[s]
                pe.wait_ge(hT_lo_ready, after(it, k, 1, 0))
                if k % STEPS < STREAMS:
                    pe.wait_ge(adj_loaded[s], loads_until(it, group_of(k)))
                    transpose_adj(s)
                pe.wait_ge(o_ready, after(it, k, 1, 1))
                for kt in range(KT):
                    for b in range(G):
                        last = pe.transpose(ps_oT[:, kt * GS + b * S:kt * GS + (b + 1) * S],
                                            o[:, b, kt * P:(kt + 1) * P], ident)
                last.then_inc(oT_psum, 1)

            def factor(it, k, ht):
                s, n, layer = k % STREAMS, k * KT + ht, k % STEPS // STREAMS
                pe.wait_ge(hT_hi_ready, after(it, k, 1, 1))
                pe.wait_ge(wh_hi_ready, after(it, k, KT, ht + 1))
                pe.wait_ge(wh_lo_ready, after(it, k, KT, ht + 1))
                for m in range(2):
                    pairs = [(w_hi[layer][:, m, ot, ht * P:(ht + 1) * P], w_lo[layer][:, m, ot, ht * P:(ht + 1) * P],
                              hT_hi[s][:, ot], hT_lo[s][:, ot]) for ot in range(KT)]
                    high_pass(pe, ps_wh[:, n % 2, m, :], pairs)
                    low_high_pass(pe, ps_wh[:, n % 2, m, :], pairs)
                    if m == 0:
                        pe.wait_ge(hT_lo_ready, after(it, k, 1, 1))
                        if layer == 1:
                            pe.wait_ge(hT_rest_ready, after_group(it, group_of(k), 1, 1))
                    last = high_low_pass(pe, ps_wh[:, n % 2, m, :], pairs)
                last.then_inc(wh_psum, 1)

            def linear(it, k, b):
                s, layer = k % STREAMS, k % STEPS // STREAMS
                pe.wait_ge(lin_out, after(it, k, G, b + 1))
                pairs = [(hT_hi[s][:, kt, b], hT_lo[s][:, kt, b],
                          w_hi[layer][:, 2, kt, :], w_lo[layer][:, 2, kt, :]) for kt in range(KT)]
                high_pass(pe, ps_lin[:, 0:D], pairs)
                low_passes(pe, ps_lin[:, 0:D], pairs).then_inc(lin_psum, 1)

            def scores(it, k):
                s = k % STREAMS
                for b in range(G):
                    for kt in range(KT):
                        if b == 0:
                            pe.wait_ge(wh_hi_ready, after(it, k, KT, 2 + kt + 1))
                            pe.wait_ge(wh_lo_ready, after(it, k, KT, 2 + kt + 1))
                        h_hi, h_lo = hT_hi[s][:, kt, b], hT_lo[s][:, kt, b]
                        f_hi, f_lo = wh_hi[:, kt, :, b * S:(b + 1) * S], wh_lo[:, kt, :, b * S:(b + 1) * S]
                        pe.matmul(ps_u[:, b], h_hi, f_hi, start=(kt == 0), stop=False)
                        pe.matmul(ps_u[:, b], h_lo, f_hi, start=False, stop=False)
                        last = pe.matmul(ps_u[:, b], h_hi, f_lo, start=False, stop=(kt == KT - 1))
                last.then_inc(u_psum, 1)

            def context(it, k, b):
                pairs = [(dT_hi[:, b, :], dT_lo[:, b, :], lin_hi[:, b, :], lin_lo[:, b, :])]
                pe.wait_ge(dT_hi_ready, after(it, k, 1, 1))
                pe.wait_ge(lin_hi_ready, after(it, k, G, b + 1))
                high_pass(pe, ps_ctx[:, b, 0:D + 2], pairs)
                pe.wait_ge(dT_lo_ready, after(it, k, 1, 1))
                pe.wait_ge(lin_lo_ready[b], after(it, k, 1, 1))
                low_passes(pe, ps_ctx[:, b, 0:D + 2], pairs).then_inc(ctx_psum, 1)

            def step(it, k, final=False):
                last, last_two = final and k == 3, final and k >= 2
                linear(it, k, 1)
                if not last:
                    factor(it, k + 1, 0)
                for b in range(G):
                    context(it, k, b)
                if not last:
                    for ht in range(1, KT):
                        factor(it, k + 1, ht)
                    linear(it, k + 1, 0)
                    if not last_two:
                        transpose_o(it, k + 2)
                    scores(it, k + 1)

            transpose_adj(0).then_inc(oT_psum, 1)
            for ht in range(KT):
                factor(0, 0, ht)
            linear(0, 0, 0)
            pe.wait_ge(adjT_ready, 1)
            transpose_o(0, 1)
            scores(0, 0)
            pe.wait_ge(ones_ready, 4)
            step(0, 0)
            pe.wait_ge(w_hi_ready, 3)
            pe.wait_ge(w_lo_ready, 3)
            with pe.Fori(0, iters - 1) as it:
                for k in (1, 2, 3, 4):
                    step(it, k)
            for k in (1, 2, 3):
                step(iters - 1, k, final=True)

        @block.scalar
        def _(act):
            def x_normalise(it, s):
                t = s % STREAMS
                act.wait_ge(x_shift_ready, after_group(it, s, 1, 1))
                for b in range(G):
                    last = act.activation(x_o[:, b, :], x_in[t][:, b, :], ACT.Identity,
                                          bias=x_shift[t][:, b:b + 1], scale=x_rstd[t][:, b:b + 1])
                last.then_inc(o_ready, 1)

            def c_normalise(it, k):
                s, done = k % STREAMS, (o_ready if k % STEPS < STREAMS else res_o_ready)
                act.wait_ge(c_shift_ready, after(it, k, 1, 1))
                for b in range(G):
                    last = act.activation(ctx_o[s][:, b, :], ctx_o[s][:, b, :], ACT.Identity,
                                          bias=c_shift[:, b:b + 1], scale=c_rstd[:, b:b + 1])
                last.then_inc(done, 1)

            def relu_hT(it, k):
                act.wait_ge(oT_psum, after(it, k, 1, 1))
                if k % STEPS < STREAMS:
                    act.activation(hT_hi[k % STREAMS], ps_oT_tiles, ACT.Relu).then_inc(hT_hi_ready, 1)
                    return
                for kt in range(KT):
                    last = act.activation(hT[:, kt], ps_oT_tiles[:, kt], ACT.Relu,
                                          bias=col[:, 3 * KT + kt:3 * KT + kt + 1],
                                          scale=col[:, 2 * KT + kt:2 * KT + kt + 1])
                last.then_inc(hT_ready, 1)
                act.wait_ge(hT_ready, after_group(it, group_of(k), 1, 1))
                act.activation(hT_hi[k % STREAMS], hT[:], ACT.Copy).then_inc(hT_hi_ready, 1)

            def copy_adjT(it, k):
                act.wait_ge(oT_psum, after(it, k, 1, 1))
                act.activation(adjT[k % STREAMS][:].rearrange("p b n -> p (b n)"), ps_oT[:, ADJ:ADJ + GS],
                               ACT.Copy).then_inc(adjT_ready, 1)

            def keep_x(it, s):
                act.wait_ge(x_loaded[s % STREAMS], loads_until(it, s))
                act.activation(x_res[s % STREAMS][:], x_in[s % STREAMS][:], ACT.Copy).then_inc(x_res_ready, 1)

            def factor_high(it, k, ht):
                n = k * KT + ht
                act.wait_ge(wh_psum, after(it, k, KT, ht + 1))
                act.activation(wh_hi[:, ht], ps_wh[:, n % 2], ACT.Copy).then_inc(wh_hi_ready, 1)

            def linear_high(it, k, b):
                act.wait_ge(lin_out, after(it, k, G, 1 + b + 1))
                act.activation(lin_hi[:, b, 0:D], lin[:, b, :], ACT.Copy).then_inc(lin_hi_ready, 1)

            def divide(it, k, b):
                act.wait_ge(inv_den_ready, after(it, k, G, b + 1))
                act.activation(ctx_o[k % STREAMS][:, b, :], ps_ctx[:, b, 0:D], ACT.Copy,
                               scale=inv_den[:, b:b + 1]).then_inc(ctx_done, 1)

            def step(it, k, final=False):
                last, last_two = final and k == 3, final and k >= 2
                act.wait_ge(uT_ready, after(it, k, 1, 1))
                act.activation(prob[:], uT[:], ACT.Exp, scale=SCALE).then_inc(exp_done, 1)
                act.wait_ge(dT_ready, after(it, k, 1, 1))
                act.activation(dT_hi[:], dT[:], ACT.Copy).then_inc(dT_hi_ready, 1)
                linear_high(it, k, 1)
                if not last:
                    factor_high(it, k + 1, 0)
                for b in range(G):
                    divide(it, k, b)
                if not last:
                    factor_high(it, k + 1, 1)
                if k in (2, 3) and not final:
                    x_normalise(it, k)
                c_normalise(it, k)
                if not last:
                    factor_high(it, k + 1, 2)
                if not last_two:
                    if (k + 2) % STEPS < STREAMS:
                        copy_adjT(it, k + 2)
                    relu_hT(it, k + 2)
                if not last:
                    linear_high(it, k + 1, 0)
                if k == 3 and not final:
                    act.wait_ge(sum_ready, after_group(it, 0, G, G))
                    keep_x(it, 2)
                if k == 4:
                    act.wait_ge(sum_ready, after_group(it, 1, G, G))
                    keep_x(it, 3)

            act.sem_inc(o_ready, 2)
            act.sem_inc(hT_hi_ready, 1)
            act.sem_inc(wh_hi_ready, 2)
            copy_adjT(0, 0)
            for ht in range(KT):
                act.wait_ge(w_loaded[ht], 16)
                act.activation(second_hi[:, ht].rearrange("p t n -> p (t n)"), w_raw[:, ht, :], ACT.Copy
                               ).then_inc(w_hi_ready, 1)
                factor_high(0, 0, ht)
            copy_adjT(0, 1)
            relu_hT(0, 1)
            linear_high(0, 0, 0)
            keep_x(0, 0)
            act.wait_ge(last_summed, G)
            keep_x(0, 1)
            step(0, 0)
            with act.Fori(0, iters - 1) as it:
                for k in (1, 2, 3, 4):
                    step(it, k)
            for k in (1, 2, 3):
                step(iters - 1, k, final=True)

        @block.gpsimd
        def _(pool):
            def linear_low(it, k):
                pool.wait_ge(lin_hi_ready, after(it, k, G, 1))
                pool.tensor_tensor(lin_lo[:, 0, 0:D], lin[:, 0, :], lin_hi[:, 0, 0:D].bitcast(F32),
                                   ALU.subtract).then_inc(lin_lo_ready[0], 1)

            def hT_low_rest(it, k):
                pool.wait_ge(hT_ready, after_group(it, group_of(k), 1, 1))
                pool.wait_ge(hT_hi_ready, after(it, k, 1, 1))
                pool.tensor_tensor(hT_lo[k % STREAMS][:, KT - 1], hT[:, KT - 1],
                                   hT_hi[k % STREAMS][:, KT - 1].bitcast(F32), ALU.subtract
                                   ).then_inc(hT_rest_ready, 1)

            def x_power(it, s):
                pool.wait_ge(x_var_ready, after_group(it, s, 1, 1))
                pool.tensor_tensor(x_rstd[s % STREAMS][:], x_var[:], minus_half[:], ALU.pow).then_inc(x_rstd_ready, 1)

            def sigma(it, k):
                pool.wait_ge(c_var_ready, after(it, k, 1, 1))
                pool.tensor_tensor(c_sigma[:], c_var[:], half[:], ALU.pow).then_inc(c_sigma_ready, 1)

            def res_scale(it, k):
                s = k % STREAMS
                pool.wait_ge(res_o_ready, after_group(it, s, 1, 1))
                pool.wait_ge(out_stored[s], 16 * it + 16)
                for b in range(G):
                    pool.tensor_tensor(x_out[s][:, b, :], ctx_o[s][:, b, :], row[:, ROW_LN2, :], ALU.mult
                                       ).then_inc(scaled_ready, 1)

            def res_shift(it, k):
                s = k % STREAMS
                for b in range(G):
                    pool.wait_ge(scaled_ready, after_group(it, s, G, b + 1))
                    pool.tensor_tensor(x_out[s][:, b, :], x_out[s][:, b, :], row[:, ROW_LN2 + 1, :], ALU.add
                                       ).then_inc(shifted_done, 1)

            def step(it, k, final=False):
                sigma(it, k)
                if k in (1, 2) and not final:
                    x_power(it, k + 1)
                if k in (2, 3):
                    res_scale(it, k)
                    res_shift(it, k)
                if (k + 2) % STEPS >= STREAMS and not final or k == 1:
                    hT_low_rest(it, k + 2)
                if not (final and k == 3):
                    linear_low(it, k + 1)

            pool.memset(half[:], 0.5).then_inc(half_ready, 1)
            pool.memset(lin_hi[:, :, ONE:ONE + 1].bitcast(F32), 1.0).then_inc(ones_ready, 1)
            pool.memset(lin_hi[:, :, ONE + 1:ONE + 2].bitcast(F32), 0.0).then_inc(ones_ready, 1)
            pool.memset(lin_lo[:, :, ONE:ONE + 1].bitcast(F32), 0.0).then_inc(ones_ready, 1)
            pool.memset(lin_lo[:, :, ONE + 1:ONE + 2].bitcast(F32), 0.0).then_inc(ones_ready, 1)
            pool.sem_inc(x_rstd_ready, 2)
            for b in range(G):
                pool.tensor_tensor(x_out[1][:, b, :], ctx_o[1][:, b, :], row[:, ROW_LN, :], ALU.mult
                                   ).then_inc(last_scaled, 1)
            for b in range(G):
                pool.wait_ge(last_scaled, b + 1)
                pool.tensor_tensor(x_out[1][:, b, :], x_out[1][:, b, :], row[:, ROW_LN + 1, :], ALU.add
                                   ).then_inc(last_shifted, 1)
            for i in range(3):
                if i == 2:
                    linear_low(0, 0)
                pool.wait_ge(w_hi_ready, i + 1)
                pool.tensor_tensor(second_lo[:, i].rearrange("p t n -> p (t n)"), w_raw[:, i, :],
                                   second_hi[:, i].rearrange("p t n -> p (t n)").bitcast(F32), ALU.subtract
                                   ).then_inc(w_lo_ready, 1)
            pool.wait_ge(half_ready, 1)
            step(0, 0)
            with pool.Fori(0, iters - 1) as it:
                for k in (1, 2, 3, 4):
                    step(it, k)
            for k in (1, 2, 3):
                step(iters - 1, k, final=True)

        @block.vector
        def _(dve):
            def carried_wait(sem_of_producer, value):
                dve.wait_ge(sem_of_producer, value)
                dve.sem_inc(wait_carried, 1)

            def shift_of(out, mv, rstd):
                return dve.scalar_tensor_tensor(out=out[:], in0=mv[:, :, 0], scalar=-1.0, in1=rstd[:],
                                                op0=ALU.mult, op1=ALU.mult)

            def x_stats_of(it, s):
                t = s % STREAMS
                dve.wait_ge(x_loaded[t], loads_until(it, s))
                for b in range(G):
                    dve.bn_stats(x_stats[:, b, :], x_in[t][:, b, :]).then_inc(x_stats_done, 1)
                carried_wait(x_stats_done, after_group(it, s, G, G))
                for b in range(G):
                    dve.bn_aggr(x_mv[t][:, b, :], x_stats[:, b, :]).then_inc(x_mv_done, 1)
                dve.wait_ge(x_mv_done, after_group(it, s, G, G))
                dve.tensor_scalar(x_var[:], x_mv[t][:, :, 1], PRE_EPS, None, ALU.add).then_inc(x_var_ready, 1)

            def x_shift_of(it, s):
                dve.wait_ge(x_rstd_ready, after_group(it, s, 1, 1))
                shift_of(x_shift[s % STREAMS], x_mv[s % STREAMS], x_rstd[s % STREAMS]).then_inc(x_shift_ready, 1)

            def make_sides(it, s):
                t = s % STREAMS
                dve.wait_ge(adjT_ready, after_group(it, s, 1, 1))
                for m, a in ((0, adjT[t]), (1, adj_in[t])):
                    mask = const[:, C_LEFT + m, :].unsqueeze(1).to_broadcast([P, G, S])
                    dve.tensor_tensor(sides[t][:, :, m, :], a[:], mask, ALU.mult).then_inc(sides_done, 1)

            def inverse_sum(it, k, b):
                dve.wait_ge(ctx_psum, after(it, k, G, b + 1))
                dve.tensor_scalar(den[:, b:b + 1], ps_ctx[:, b, ONE:ONE + 1], SUM_EPS, None,
                                  ALU.add).then_inc(den_done, 1)
                dve.wait_ge(den_done, after(it, k, G, b + 1))
                dve.reciprocal(inv_den[:, b:b + 1], den[:, b:b + 1]).then_inc(inv_den_ready, 1)

            def context_stats(it, k):
                s = k % STREAMS
                for b in range(G):
                    dve.wait_ge(ctx_done, after(it, k, G, b + 1))
                    dve.bn_stats(c_stats[:, b, :], ctx_o[s][:, b, :]).then_inc(c_stats_done, 1)
                carried_wait(c_stats_done, after(it, k, G, G))
                for b in range(G):
                    dve.bn_aggr(c_mv[:, b, :], c_stats[:, b, :]).then_inc(c_mv_done, 1)
                dve.wait_ge(c_mv_done, after(it, k, G, G))
                dve.tensor_scalar(c_var[:], c_mv[:, :, 1], D / (D - 1.0), None, ALU.mult).then_inc(c_var_ready, 1)

            def context_shift(it, k):
                dve.wait_ge(c_sigma_ready, after(it, k, 1, 1))
                dve.tensor_scalar(c_sigma_eps[:], c_sigma[:], SIGMA_EPS, None, ALU.add).then_inc(c_sigma_eps_done, 1)
                dve.wait_ge(c_sigma_eps_done, after(it, k, 1, 1))
                dve.reciprocal(c_rstd[:], c_sigma_eps[:]).then_inc(c_rstd_done, 1)
                dve.wait_ge(c_rstd_done, after(it, k, 1, 1))
                shift_of(c_shift, c_mv, c_rstd).then_inc(c_shift_ready, 1)

            def residual(it, k):
                s = k % STREAMS
                dve.wait_ge(x_res_ready, after_group(it, s, 1, 1))
                for b in range(G):
                    dve.wait_ge(shifted_done, after_group(it, s, G, b + 1))
                    dve.scalar_tensor_tensor(out=x_out[s][:, b, :], in0=x_out[s][:, b, :], scalar=0.0,
                                             in1=x_res[s][:, b, :], op0=ALU.max, op1=ALU.add
                                             ).then_inc(sum_ready, 1)

            def hT_low(it, k):
                hi, lo = hT_hi[k % STREAMS].bitcast(F32), hT_lo[k % STREAMS]
                dve.wait_ge(hT_hi_ready, after(it, k, 1, 1))
                if k % STEPS < STREAMS:
                    last = dve.scalar_tensor_tensor(out=lo, in0=ps_oT_tiles, scalar=0.0, in1=hi,
                                                    op0=ALU.max, op1=ALU.subtract)
                else:
                    dve.wait_ge(hT_ready, after_group(it, group_of(k), 1, 1))
                    last = dve.tensor_tensor(lo[:, 0:KT - 1], hT[:, 0:KT - 1], hi[:, 0:KT - 1], ALU.subtract)
                last.then_inc(hT_lo_ready, 1)

            def linear_bias(it, k, b):
                dve.wait_ge(lin_psum, after(it, k, G, b + 1))
                dve.tensor_tensor(lin[:, b, :], ps_lin[:, 0:D], row[:, ROW_LIN + k % STEPS // STREAMS, :], ALU.add
                                  ).then_inc(lin_out, 1)

            def linear_low(it, k):
                dve.wait_ge(lin_out, after(it, k, G, 1 + G))
                dve.wait_ge(lin_hi_ready, after(it, k, G, G))
                dve.tensor_tensor(lin_lo[:, 1, 0:D], lin[:, 1, :], lin_hi[:, 1, 0:D].bitcast(F32),
                                  ALU.subtract).then_inc(lin_lo_ready[1], 1)

            def factor_low(it, k, ht):
                n = k * KT + ht
                dve.wait_ge(wh_hi_ready, after(it, k, KT, 2 + ht + 1))
                dve.tensor_tensor(wh_lo[:, ht], ps_wh[:, n % 2], wh_hi[:, ht].bitcast(F32), ALU.subtract
                                  ).then_inc(wh_lo_ready, 1)

            def mask_scores(it, k):
                dve.wait_ge(u_psum, after(it, k, 1, 1))
                dve.tensor_tensor(uT2[:], ps_u[:], sides[k % STREAMS][:], ALU.mult).then_inc(uT2_done, 1)
                dve.wait_ge(uT2_done, after(it, k, 1, 1))
                dve.tensor_tensor(uT[:], uT2[:, :, 0, :], uT2[:, :, 1, :], ALU.add).then_inc(uT_ready, 1)

            def mask_exp(it, k):
                dve.wait_ge(exp_done, after(it, k, 1, 1))
                dve.tensor_tensor(dT[:], prob[:], adjT[k % STREAMS][:], ALU.mult).then_inc(dT_ready, 1)

            def exp_low(it, k):
                dve.wait_ge(dT_ready, after(it, k, 1, 1))
                dve.wait_ge(dT_hi_ready, after(it, k, 1, 1))
                dve.tensor_tensor(dT_lo[:], dT[:], dT_hi[:].bitcast(F32), ALU.subtract).then_inc(dT_lo_ready, 1)

            def step(it, k, final=False):
                last = final and k == 3
                if (k + 1) % STEPS < STREAMS and not last:
                    hT_low(it, k + 1)
                mask_scores(it, k)
                if (k + 1) % STEPS >= STREAMS:
                    hT_low(it, k + 1)
                mask_exp(it, k)
                linear_bias(it, k, 1)
                exp_low(it, k)
                linear_low(it, k)
                for b in range(G):
                    inverse_sum(it, k, b)
                if not last:
                    factor_low(it, k + 1, 0)
                context_stats(it, k)
                if not last:
                    factor_low(it, k + 1, 1)
                context_shift(it, k)
                if k in (1, 2) and not final:
                    x_stats_of(it, k + 1)
                if k in (3, 4):
                    residual(it, k - 1)
                if k in (0, 3, 4) and not last:
                    make_sides(it, group_of(k + 1))
                if not last:
                    factor_low(it, k + 1, 2)
                    linear_bias(it, k + 1, 0)
                if k in (1, 2) and not final:
                    x_shift_of(it, k + 1)

            dve.sem_inc(x_stats_done, 2 * G)
            dve.sem_inc(x_mv_done, 2 * G)
            dve.sem_inc(x_var_ready, 2)
            dve.sem_inc(x_shift_ready, 2)
            dve.sem_inc(hT_lo_ready, 1)
            dve.sem_inc(wh_lo_ready, 2)
            dve.sem_inc(lin_out, 1)
            make_sides(0, 0)
            for ht in range(KT):
                factor_low(0, 0, ht)
            for b in range(G):
                dve.wait_ge(last_shifted, b + 1)
                dve.scalar_tensor_tensor(out=x_out[1][:, b, :], in0=x_out[1][:, b, :], scalar=0.0,
                                         in1=x_res[1][:, b, :], op0=ALU.max, op1=ALU.add
                                         ).then_inc(last_summed, 1)
            linear_bias(0, 0, 0)
            step(0, 0)
            with dve.Fori(0, iters - 1) as it:
                for k in (1, 2, 3, 4):
                    step(it, k)
            for k in (1, 2, 3):
                step(iters - 1, k, final=True)
            residual(iters - 1, 3)


def build(nc, x, adj, weights, rows, columns, consts, out):
    x1 = nc.dram_tensor("x1", x.shape, F32, kind="Internal").ap()
    with ExitStack() as ctx:
        shared = Shared(nc, ctx)
        network_one(nc, shared, x, adj, weights, rows, columns, consts, x1)
        network_two(nc, shared, x1, adj, weights, out)


def arrange(inputs):
    import numpy as np

    a = {k: np.asarray(v) for k, v in inputs.items()}

    def tiles(w):
        return w.reshape(KT, P, w.shape[1]).transpose(1, 0, 2).reshape(P, KT * w.shape[1])

    weights = [tiles(a[n][l].T) for l in range(LAYERS) for n in ("L0_gnn_Wl", "L0_gnn_Wr", "L0_gnn_Ws")]
    for l in range(LAYERS):
        weights += [tiles(a["L1_gnn_W_left"][l]), tiles(a["L1_gnn_W_right"][l]), tiles(a["L1_gnn_W_lin"][l].T)]
    rows = [a[n][l] for l in range(LAYERS) for n in ("L0_gnn_bl", "L0_gnn_br", "L0_gnn_bs")]
    rows += [a["L0_gnn_ln_w"][1], a["L0_gnn_ln_b"][1], a["L1_gnn_b_lin"][0], a["L1_gnn_b_lin"][1],
             a["L1_gnn_ln_a"][1], a["L1_gnn_ln_b"][1]]
    columns = [a[n][0].reshape(KT, P).T for n in ("L0_gnn_ln_w", "L0_gnn_ln_b", "L1_gnn_ln_a", "L1_gnn_ln_b")]
    part, free = np.indices((P, S))
    masks = [part == free, part > free, part < free, free <= part, free > part]
    return {
        "x": np.ascontiguousarray(a["x"]),
        "adj": np.ascontiguousarray(a["adj"]),
        "weights": np.ascontiguousarray(np.stack(weights)),
        "rows": np.ascontiguousarray(np.stack(rows)),
        "columns": np.ascontiguousarray(np.concatenate(columns, axis=1)),
        "consts": np.ascontiguousarray(np.stack([m.astype(np.float32) for m in masks], axis=1)),
    }


def kernel(**inputs):
    import concourse.bacc as bacc
    from concourse.bass_utils import run_bass_kernel_spmd

    arrays = arrange(inputs)
    nc = bacc.Bacc("TRN2", target_bir_lowering=False, num_devices=1)
    args = [nc.dram_tensor(n, a.shape, mybir.dt.from_np(a.dtype), kind="ExternalInput").ap()
            for n, a in arrays.items()]
    out = nc.dram_tensor("out", arrays["x"].shape, F32, kind="ExternalOutput").ap()
    build(nc, *args, out)
    return run_bass_kernel_spmd(nc, [arrays], core_ids=[0]).results[0]["out"]
```
